# Optimizing a Trainium2 kernel written in Bass

```python
import numpy as np
import jax
import jax.numpy as jnp

def _softmax(x, axis=-1):
    return jax.nn.softmax(x, axis=axis)

def _gelu(x):
    return jax.nn.gelu(x, approximate=True)

def _silu(x):
    return jax.nn.silu(x)

def _sigmoid(x):
    return jax.nn.sigmoid(x)

def _layernorm(x, axis=-1, eps=1e-05):
    m = jnp.mean(x, axis=axis, keepdims=True)
    v = jnp.var(x, axis=axis, keepdims=True)
    return (x - m) / jnp.sqrt(v + eps)

def _scatter_add(tgt, idx, src, axis=0):
    return tgt.at[idx].add(src)

def _segment_sum(src, seg, n):
    return jax.ops.segment_sum(src, seg, n)
kernel_name = 'mk_seq_preln_d2_jaxref_r4_fbee51'

def setup_inputs(seed: int=0):
    np.random.seed(seed)
    _w = jnp.asarray

    def _L0_attn_setup():
        import jax, jax.numpy as jnp
        import numpy as np
        HIDDEN = 512
        NUM_HEADS = 6
        HEAD_DIM = 64
        KEY_DIM = NUM_HEADS * HEAD_DIM
        VALUE_DIM = KEY_DIM
        CONV_K = 4
        EPS = 1e-05

        def _causal_depthwise_conv(x, w):
            B, T, C = x.shape
            K = w.shape[1]
            xp = jnp.pad(x, ((0, 0), (K - 1, 0), (0, 0)))
            y = jnp.zeros_like(x)
            for i in range(K):
                y = y + xp[:, i:i + T, :] * w[:, i]
            return jax.nn.silu(y)

        def _l2norm(x, eps=1e-06):
            return x * jax.lax.rsqrt(jnp.sum(x * x, axis=-1, keepdims=True) + eps)
        key = jax.random.key(seed)
        ks = jax.random.split(key, 16)
        s = lambda fan: 1.0 / np.sqrt(fan)
        inp = {'hidden_states': jax.random.normal(ks[0], (2, 512, HIDDEN), jnp.float32), 'Wq': jax.random.normal(ks[1], (KEY_DIM, HIDDEN), jnp.float32) * s(HIDDEN), 'Wk': jax.random.normal(ks[2], (KEY_DIM, HIDDEN), jnp.float32) * s(HIDDEN), 'Wv': jax.random.normal(ks[3], (VALUE_DIM, HIDDEN), jnp.float32) * s(HIDDEN), 'Wo': jax.random.normal(ks[4], (HIDDEN, VALUE_DIM), jnp.float32) * s(VALUE_DIM), 'Wb': jax.random.normal(ks[5], (NUM_HEADS, HIDDEN), jnp.float32) * s(HIDDEN), 'Wa': jax.random.normal(ks[6], (NUM_HEADS, HIDDEN), jnp.float32) * s(HIDDEN), 'Wg': jax.random.normal(ks[7], (VALUE_DIM, HIDDEN), jnp.float32) * s(HIDDEN), 'conv_q': jax.random.normal(ks[8], (KEY_DIM, CONV_K), jnp.float32) * s(CONV_K), 'conv_k': jax.random.normal(ks[9], (KEY_DIM, CONV_K), jnp.float32) * s(CONV_K), 'conv_v': jax.random.normal(ks[10], (VALUE_DIM, CONV_K), jnp.float32) * s(CONV_K), 'o_norm_w': jnp.ones((HEAD_DIM,), jnp.float32)}
        A = jax.random.uniform(ks[11], (NUM_HEADS,), jnp.float32, 0.0001, 16.0)
        inp['A_log'] = jnp.log(A)
        dt = jnp.exp(jax.random.uniform(ks[12], (NUM_HEADS,), jnp.float32) * (np.log(0.1) - np.log(0.001)) + np.log(0.001))
        dt = jnp.clip(dt, 0.0001, None)
        inp['dt_bias'] = dt + jnp.log(-jnp.expm1(-dt))
        return inp
    _L0_attn_in = _L0_attn_setup()

    def _L0_ffn_setup():
        import jax, jax.numpy as jnp
        import numpy as np
        BLOCK_SIZE = 32
        HIDDEN_SIZE = 512
        MLP_DIM = 4096
        NVFP4_LUT = jnp.array([0.0, 0.5, 1.0, 1.5, 2.0, 3.0, 4.0, 6.0, 0.0, -0.5, -1.0, -1.5, -2.0, -3.0, -4.0, -6.0], dtype=jnp.float32)

        def dequant_nvfp4(W_packed, scales, block=BLOCK_SIZE):
            N = W_packed.shape[0]
            low = W_packed & 15
            high = W_packed >> 4 & 15
            idx = jnp.stack([low, high], axis=-1).reshape(N, -1)
            vals = NVFP4_LUT[idx]
            K = vals.shape[1]
            vals = vals.reshape(N, K // block, block) * scales[:, :, None]
            return vals.reshape(N, K)
        key = jax.random.key(seed)
        ks = jax.random.split(key, 7)
        x = jax.random.normal(ks[0], (4, 32, HIDDEN_SIZE), dtype=jnp.float32)
        gate_W_packed = jax.random.randint(ks[1], (MLP_DIM, HIDDEN_SIZE // 2), 0, 64, dtype=jnp.int32)
        gate_scales = jax.random.uniform(ks[2], (MLP_DIM, HIDDEN_SIZE // BLOCK_SIZE), dtype=jnp.float32) * 0.1 + 0.001
        up_W_packed = jax.random.randint(ks[3], (MLP_DIM, HIDDEN_SIZE // 2), 0, 64, dtype=jnp.int32)
        up_scales = jax.random.uniform(ks[4], (MLP_DIM, HIDDEN_SIZE // BLOCK_SIZE), dtype=jnp.float32) * 0.1 + 0.001
        down_W_packed = jax.random.randint(ks[5], (HIDDEN_SIZE, MLP_DIM // 2), 0, 64, dtype=jnp.int32)
        down_scales = jax.random.uniform(ks[6], (HIDDEN_SIZE, MLP_DIM // BLOCK_SIZE), dtype=jnp.float32) * 0.1 + 0.001
        return {'x': x, 'gate_W_packed': gate_W_packed, 'gate_scales': gate_scales, 'up_W_packed': up_W_packed, 'up_scales': up_scales, 'down_W_packed': down_W_packed, 'down_scales': down_scales}
    _L0_ffn_in = _L0_ffn_setup()

    def _L1_attn_setup():
        import jax, jax.numpy as jnp
        import numpy as np
        import math
        DIM, HEADS, COMPRESS = (512, 16, 8)
        HEAD_DIM = DIM // HEADS
        HALF = HEAD_DIM // 2
        LATENT = DIM // COMPRESS
        B, S = (2, 512)

        def _rope_tables(seq_len):
            inv_freq = 1.0 / 10000.0 ** (jnp.arange(0, HALF, 2, dtype=jnp.float32) / HALF)
            t = jnp.arange(seq_len, dtype=jnp.float32)
            freqs = t[:, None] * inv_freq[None, :]
            emb = jnp.concatenate([freqs, freqs], axis=-1)
            cos = jnp.cos(emb)[None, :, None, :]
            sin = jnp.sin(emb)[None, :, None, :]
            return (cos, sin)

        def _rotate_half(x):
            x1, x2 = jnp.split(x, 2, axis=-1)
            return jnp.concatenate([-x2, x1], axis=-1)
        key = jax.random.key(seed)
        ks = jax.random.split(key, 7)
        sc = lambda fan_in: 1.0 / math.sqrt(fan_in)
        return {'x': jax.random.normal(ks[0], (B, S, DIM), jnp.float32), 'wq_d': jax.random.normal(ks[1], (DIM, LATENT), jnp.float32) * sc(DIM), 'wkv_d': jax.random.normal(ks[2], (DIM, LATENT), jnp.float32) * sc(DIM), 'wq_u': jax.random.normal(ks[3], (LATENT, HEADS * HALF), jnp.float32) * sc(LATENT), 'wk_u': jax.random.normal(ks[4], (LATENT, HEADS * HALF), jnp.float32) * sc(LATENT), 'wv_u': jax.random.normal(ks[5], (LATENT, DIM), jnp.float32) * sc(LATENT), 'wo': jax.random.normal(ks[6], (DIM, DIM), jnp.float32) * sc(DIM)}
    _L1_attn_in = _L1_attn_setup()

    def _L1_ffn_setup():
        import jax, jax.numpy as jnp
        import numpy as np

        def _sparsify_2to4(h):
            B, S, I = h.shape
            g = h.reshape(B, S, I // 4, 4)
            a = jnp.abs(g)
            _, idx = jax.lax.top_k(a, 2)
            pos = jnp.arange(4)
            mask = (pos == idx[..., 0:1]) | (pos == idx[..., 1:2])
            return (g * mask.astype(g.dtype)).reshape(B, S, I)
        key = jax.random.key(seed)
        k1, k2, k3, k4 = jax.random.split(key, 4)
        B, S, H, I = (4, 512, 512, 2048)
        x = jax.random.normal(k1, (B, S, H), dtype=jnp.float32)
        w_gate = jax.random.normal(k2, (H, I), dtype=jnp.float32) / np.sqrt(H)
        w_up = jax.random.normal(k3, (H, I), dtype=jnp.float32) / np.sqrt(H)
        w_down = jax.random.normal(k4, (I, H), dtype=jnp.float32) / np.sqrt(I)
        return {'x': x, 'w_gate': w_gate, 'w_up': w_up, 'w_down': w_down}
    _L1_ffn_in = _L1_ffn_setup()
    _d = {'L0_attn_hidden_states': _L0_attn_in['hidden_states'], 'L0_attn_Wq': _L0_attn_in['Wq'], 'L0_attn_Wk': _L0_attn_in['Wk'], 'L0_attn_Wv': _L0_attn_in['Wv'], 'L0_attn_Wo': _L0_attn_in['Wo'], 'L0_attn_Wb': _L0_attn_in['Wb'], 'L0_attn_Wa': _L0_attn_in['Wa'], 'L0_attn_Wg': _L0_attn_in['Wg'], 'L0_attn_conv_q': _L0_attn_in['conv_q'], 'L0_attn_conv_k': _L0_attn_in['conv_k'], 'L0_attn_conv_v': _L0_attn_in['conv_v'], 'L0_attn_o_norm_w': _L0_attn_in['o_norm_w'], 'L0_attn_A_log': _L0_attn_in['A_log'], 'L0_attn_dt_bias': _L0_attn_in['dt_bias'], 'L0_ffn_gate_W_packed': _L0_ffn_in['gate_W_packed'], 'L0_ffn_gate_scales': _L0_ffn_in['gate_scales'], 'L0_ffn_up_W_packed': _L0_ffn_in['up_W_packed'], 'L0_ffn_up_scales': _L0_ffn_in['up_scales'], 'L0_ffn_down_W_packed': _L0_ffn_in['down_W_packed'], 'L0_ffn_down_scales': _L0_ffn_in['down_scales'], 'L1_attn_wq_d': _L1_attn_in['wq_d'], 'L1_attn_wkv_d': _L1_attn_in['wkv_d'], 'L1_attn_wq_u': _L1_attn_in['wq_u'], 'L1_attn_wk_u': _L1_attn_in['wk_u'], 'L1_attn_wv_u': _L1_attn_in['wv_u'], 'L1_attn_wo': _L1_attn_in['wo'], 'L1_ffn_w_gate': _L1_ffn_in['w_gate'], 'L1_ffn_w_up': _L1_ffn_in['w_up'], 'L1_ffn_w_down': _L1_ffn_in['w_down']}
    _x0 = _d['L0_attn_hidden_states']
    _d['L0_attn_hidden_states'] = jax.random.normal(jax.random.fold_in(jax.random.key(seed), 1), (2, 1024, 512), dtype=_x0.dtype)
    del _x0
    return _d

def reference(L0_attn_hidden_states, L0_attn_Wq, L0_attn_Wk, L0_attn_Wv, L0_attn_Wo, L0_attn_Wb, L0_attn_Wa, L0_attn_Wg, L0_attn_conv_q, L0_attn_conv_k, L0_attn_conv_v, L0_attn_o_norm_w, L0_attn_A_log, L0_attn_dt_bias, L0_ffn_gate_W_packed, L0_ffn_gate_scales, L0_ffn_up_W_packed, L0_ffn_up_scales, L0_ffn_down_W_packed, L0_ffn_down_scales, L1_attn_wq_d, L1_attn_wkv_d, L1_attn_wq_u, L1_attn_wk_u, L1_attn_wv_u, L1_attn_wo, L1_ffn_w_gate, L1_ffn_w_up, L1_ffn_w_down):

    def _L0_attn_ref(hidden_states, Wq, Wk, Wv, Wo, Wb, Wa, Wg, conv_q, conv_k, conv_v, o_norm_w, A_log, dt_bias):
        import jax, jax.numpy as jnp
        import numpy as np
        HIDDEN = 512
        NUM_HEADS = 6
        HEAD_DIM = 64
        KEY_DIM = NUM_HEADS * HEAD_DIM
        VALUE_DIM = KEY_DIM
        CONV_K = 4
        EPS = 1e-05

        def _causal_depthwise_conv(x, w):
            B, T, C = x.shape
            K = w.shape[1]
            xp = jnp.pad(x, ((0, 0), (K - 1, 0), (0, 0)))
            y = jnp.zeros_like(x)
            for i in range(K):
                y = y + xp[:, i:i + T, :] * w[:, i]
            return jax.nn.silu(y)

        def _l2norm(x, eps=1e-06):
            return x * jax.lax.rsqrt(jnp.sum(x * x, axis=-1, keepdims=True) + eps)
        x = hidden_states
        B, T, D = x.shape
        H, dk, dv = (NUM_HEADS, HEAD_DIM, HEAD_DIM)
        q = _causal_depthwise_conv(jnp.einsum('btd,kd->btk', x, Wq), conv_q)
        k = _causal_depthwise_conv(jnp.einsum('btd,kd->btk', x, Wk), conv_k)
        v = _causal_depthwise_conv(jnp.einsum('btd,kd->btk', x, Wv), conv_v)
        q = _l2norm(q.reshape(B, T, H, dk))
        k = _l2norm(k.reshape(B, T, H, dk))
        v = v.reshape(B, T, H, dv)
        beta = jax.nn.sigmoid(jnp.einsum('btd,hd->bth', x, Wb))
        g = -jnp.exp(A_log) * jax.nn.softplus(jnp.einsum('btd,hd->bth', x, Wa) + dt_bias)
        scale = dk ** (-0.5)

        def step(S, inputs):
            q_t, k_t, v_t, g_t, b_t = inputs
            S = S * jnp.exp(g_t)[..., None, None]
            kv = jnp.einsum('bhk,bhkv->bhv', k_t, S)
            u = b_t[..., None] * (v_t - kv)
            S = S + jnp.einsum('bhk,bhv->bhkv', k_t, u)
            o_t = jnp.einsum('bhk,bhkv->bhv', q_t * scale, S)
            return (S, o_t)
        tfirst = lambda a: jnp.moveaxis(a, 1, 0)
        S0 = jnp.zeros((B, H, dk, dv), x.dtype)
        _, o = jax.lax.scan(step, S0, (tfirst(q), tfirst(k), tfirst(v), tfirst(g), tfirst(beta)))
        o = jnp.moveaxis(o, 0, 1)
        gate = jnp.einsum('btd,vd->btv', x, Wg).reshape(B, T, H, dv)
        o = o * jax.lax.rsqrt(jnp.mean(o * o, axis=-1, keepdims=True) + EPS)
        o = o * o_norm_w * jax.nn.silu(gate)
        out = jnp.einsum('btv,dv->btd', o.reshape(B, T, H * dv), Wo)
        return out

    def _L0_ffn_ref(x, gate_W_packed, gate_scales, up_W_packed, up_scales, down_W_packed, down_scales):
        import jax, jax.numpy as jnp
        import numpy as np
        BLOCK_SIZE = 32
        HIDDEN_SIZE = 512
        MLP_DIM = 4096
        NVFP4_LUT = jnp.array([0.0, 0.5, 1.0, 1.5, 2.0, 3.0, 4.0, 6.0, 0.0, -0.5, -1.0, -1.5, -2.0, -3.0, -4.0, -6.0], dtype=jnp.float32)

        def dequant_nvfp4(W_packed, scales, block=BLOCK_SIZE):
            N = W_packed.shape[0]
            low = W_packed & 15
            high = W_packed >> 4 & 15
            idx = jnp.stack([low, high], axis=-1).reshape(N, -1)
            vals = NVFP4_LUT[idx]
            K = vals.shape[1]
            vals = vals.reshape(N, K // block, block) * scales[:, :, None]
            return vals.reshape(N, K)
        B, S, H = x.shape
        xt = x.reshape(B * S, H)
        Wg = dequant_nvfp4(gate_W_packed, gate_scales)
        Wu = dequant_nvfp4(up_W_packed, up_scales)
        Wd = dequant_nvfp4(down_W_packed, down_scales)
        gate = jnp.einsum('th,nh->tn', xt, Wg)
        up = jnp.einsum('th,nh->tn', xt, Wu)
        gelu = jnp.tanh(0.7978845608028654 * (gate + 0.044715 * gate ** 3)) * gate * 0.5 + gate * 0.5
        inter = gelu * up
        out = jnp.einsum('tn,hn->th', inter, Wd)
        return out.reshape(B, S, H)

    def _L1_attn_ref(x, wq_d, wkv_d, wq_u, wk_u, wv_u, wo):
        import jax, jax.numpy as jnp
        import numpy as np
        import math
        DIM, HEADS, COMPRESS = (512, 16, 8)
        HEAD_DIM = DIM // HEADS
        HALF = HEAD_DIM // 2
        LATENT = DIM // COMPRESS
        B, S = (2, 512)

        def _rope_tables(seq_len):
            inv_freq = 1.0 / 10000.0 ** (jnp.arange(0, HALF, 2, dtype=jnp.float32) / HALF)
            t = jnp.arange(seq_len, dtype=jnp.float32)
            freqs = t[:, None] * inv_freq[None, :]
            emb = jnp.concatenate([freqs, freqs], axis=-1)
            cos = jnp.cos(emb)[None, :, None, :]
            sin = jnp.sin(emb)[None, :, None, :]
            return (cos, sin)

        def _rotate_half(x):
            x1, x2 = jnp.split(x, 2, axis=-1)
            return jnp.concatenate([-x2, x1], axis=-1)
        b, s, d = x.shape
        q_latent = x @ wq_d
        kv_latent = x @ wkv_d
        q = (q_latent @ wq_u).reshape(b, s, HEADS, HALF)
        k = (kv_latent @ wk_u).reshape(b, s, HEADS, HALF)
        v = (kv_latent @ wv_u).reshape(b, s, HEADS, HEAD_DIM)
        cos, sin = _rope_tables(s)
        q = q * cos + _rotate_half(q) * sin
        k = k * cos + _rotate_half(k) * sin
        scale = 1.0 / math.sqrt(HALF)
        attn = jnp.einsum('bqhd,bkhd->bhqk', q, k) * scale
        attn = jax.nn.softmax(attn, axis=-1)
        out = jnp.einsum('bhqk,bkhd->bqhd', attn, v)
        out = out.reshape(b, s, d)
        return out @ wo

    def _L1_ffn_ref(x, w_gate, w_up, w_down):
        import jax, jax.numpy as jnp
        import numpy as np

        def _sparsify_2to4(h):
            B, S, I = h.shape
            g = h.reshape(B, S, I // 4, 4)
            a = jnp.abs(g)
            _, idx = jax.lax.top_k(a, 2)
            pos = jnp.arange(4)
            mask = (pos == idx[..., 0:1]) | (pos == idx[..., 1:2])
            return (g * mask.astype(g.dtype)).reshape(B, S, I)
        h = jax.nn.silu(jnp.einsum('bsh,hi->bsi', x, w_gate)) * jnp.einsum('bsh,hi->bsi', x, w_up)
        h_sparse = _sparsify_2to4(h)
        return jnp.einsum('bsi,ih->bsh', h_sparse, w_down)
    x = L0_attn_hidden_states
    x = x + _L0_attn_ref(_layernorm(x, axis=-1), L0_attn_Wq, L0_attn_Wk, L0_attn_Wv, L0_attn_Wo, L0_attn_Wb, L0_attn_Wa, L0_attn_Wg, L0_attn_conv_q, L0_attn_conv_k, L0_attn_conv_v, L0_attn_o_norm_w, L0_attn_A_log, L0_attn_dt_bias)
    x = x + _L0_ffn_ref(_layernorm(x, axis=-1), L0_ffn_gate_W_packed, L0_ffn_gate_scales, L0_ffn_up_W_packed, L0_ffn_up_scales, L0_ffn_down_W_packed, L0_ffn_down_scales)
    x = x + _L1_attn_ref(_layernorm(x, axis=-1), L1_attn_wq_d, L1_attn_wkv_d, L1_attn_wq_u, L1_attn_wk_u, L1_attn_wv_u, L1_attn_wo)
    x = x + _L1_ffn_ref(_layernorm(x, axis=-1), L1_ffn_w_gate, L1_ffn_w_up, L1_ffn_w_down)
    return x

_drawn_inputs = setup_inputs


def setup_inputs(seed=0):
    import zlib

    import numpy as np

    out = dict(_drawn_inputs(seed))
    spreads = {'L0_attn_o_norm_w': (1.0, 0.2)}
    factors = {'L1_attn_wq_d': 8.0,
     'L1_attn_wkv_d': 8.0,
     'L1_attn_wq_u': 8.0,
     'L1_attn_wk_u': 8.0,
     'L1_attn_wv_u': 8.0,
     'L1_attn_wo': 8.0,
     'L1_ffn_w_gate': 6.162,
     'L1_ffn_w_up': 5.749,
     'L1_ffn_w_down': 5.752}
    for name, (base, spread) in spreads.items():
        noise = np.random.default_rng([zlib.crc32(name.encode()), seed]).standard_normal(out[name].shape)
        drawn = base * np.exp(spread * noise) if base else spread * noise
        out[name] = jnp.asarray(drawn.astype(out[name].dtype))
    for name, factor in factors.items():
        out[name] = (out[name] * factor).astype(out[name].dtype)
    return out
```

```python
from contextlib import ExitStack

import numpy as np
import concourse.bass as bass
from concourse import mybir

F32 = mybir.dt.float32
F32R = mybir.dt.float32r
F16 = mybir.dt.float16
BF16 = mybir.dt.bfloat16
I32 = mybir.dt.int32
ALU = mybir.AluOpType
ACT = mybir.ActivationFunctionType
AX = mybir.AxisListType

P = 128
BATCH, SEQ, DIM = 2, 1024, 512
TOKENS = BATCH * SEQ
TILES = TOKENS // P
KT = DIM // P
TB = 512
BLOCKS = TOKENS // TB
SUB = TB // P
EPS = 1e-5


class Scope:

    def __init__(self, nc, prefix):
        self.nc, self.prefix, self.stack, self.sems = nc, prefix, ExitStack(), []

    def __enter__(self):
        self.stack.__enter__()
        return self

    def __exit__(self, *a):
        self.stack.__exit__(*a)
        if self.sems:
            self.nc.clear_and_free_semaphores(self.sems)
            self.nc.all_engine_barrier()

    def sb(self, name, shape, dt=F32):
        return self.stack.enter_context(self.nc.sbuf_tensor(f"{self.prefix}_{name}", shape, dt))

    def ps(self, name, shape, dt=F32):
        return self.stack.enter_context(self.nc.psum_tensor(f"{self.prefix}_{name}", shape, dt))

    def sem(self, name):
        self.sems.append(self.nc.alloc_semaphore(name=f"{self.prefix}_{name}"))
        return self.sems[-1]

    def block(self):
        return self.stack.enter_context(self.nc.Block())


def matmul3(pe, out, w_hi, w_lo, x_hi, x_lo, start, stop):
    pe.matmul(out, w_hi, x_hi, start=start, stop=False)
    pe.matmul(out, w_hi, x_lo, start=False, stop=False)
    return pe.matmul(out, w_lo, x_hi, start=False, stop=stop)


def feature_tiles_plain(kt):
    return slice(kt * P, (kt + 1) * P)


def feature_tiles_nibbles(kt):
    return slice(2 * P * (kt // 2) + kt % 2, 2 * P * (kt // 2 + 1), 2)


def normalise(nc, prefix, stream, ident, feat_hi, feat_lo, feature_tiles):
    with Scope(nc, prefix) as s:
        raw = s.sb("raw_stats", [P, TILES, 6])
        mean, gap, var = (s.sb(x, [P, TILES]) for x in ("mean", "gap", "var"))
        power = s.sb("power", [P, TILES])
        rstd = s.sb("rstd", [P, TILES])
        normed = s.sb("normed", [P, 2, DIM])
        turned = [s.ps(f"turned{b}", [P, KT, P]) for b in range(2)]
        stats_done, moments, rstd_done = s.sem("stats_done"), s.sem("moments"), s.sem("rstd_done")
        const_ready = s.sem("const_ready")
        normed_done, turned_done = s.sem("normed_done"), s.sem("turned_done")
        hi_done, lo_done = s.sem("hi_done"), s.sem("lo_done")
        block = s.block()

        @block.gpsimd
        def _(pool):
            pool.memset(power[:], -0.5).then_inc(const_ready, 1)
            pool.wait_ge(const_ready, 1)
            pool.wait_ge(moments, 7)
            pool.tensor_tensor(rstd[:], var[:], power[:], ALU.pow).then_inc(rstd_done, 1)

        @block.vector
        def _(dve):
            with dve.Fori(0, TILES) as i:
                dve.bn_stats(raw[:, bass.ds(i, 1), :], stream[:, bass.ds(i, 1), :]).then_inc(stats_done, 1)
            dve.wait_ge(stats_done, TILES)
            dve.tensor_tensor(mean[:], raw[:, :, 1], raw[:, :, 4], ALU.add).then_inc(moments, 1)
            dve.tensor_tensor(gap[:], raw[:, :, 1], raw[:, :, 4], ALU.subtract).then_inc(moments, 1)
            dve.tensor_tensor(var[:], raw[:, :, 2], raw[:, :, 5], ALU.add).then_inc(moments, 1)
            dve.wait_ge(moments, 3)
            dve.tensor_scalar(mean[:], mean[:], 0.5, None, ALU.mult).then_inc(moments, 1)
            dve.scalar_tensor_tensor(out=gap[:], in0=gap[:], scalar=0.25, in1=gap[:],
                                     op0=ALU.mult, op1=ALU.mult).then_inc(moments, 1)
            dve.tensor_scalar(var[:], var[:], 1.0 / DIM, EPS, ALU.mult, ALU.add).then_inc(moments, 1)
            dve.wait_ge(moments, 6)
            dve.tensor_tensor(var[:], var[:], gap[:], ALU.add).then_inc(moments, 1)
            dve.wait_ge(rstd_done, 1)
            dve.sem_inc(lo_done, 2)

            def scale(i, b):
                dve.wait_ge(turned_done, i + 1)
                dve.tensor_scalar(normed[:, b, :], stream[:, bass.ds(i, 1), :],
                                  mean[:, bass.ds(i, 1)], rstd[:, bass.ds(i, 1)],
                                  ALU.subtract, ALU.mult).then_inc(normed_done, 1)

            def low(i, b):
                dve.wait_ge(hi_done, i + 1)
                cols = bass.ts(i, P)
                dve.tensor_tensor(feat_lo[:, :, cols], turned[b][:], feat_hi[:, :, cols].bitcast(F32),
                                  ALU.subtract).then_inc(lo_done, 1)

            with dve.Fori(0, TILES // 2) as i:
                for b in range(2):
                    scale(2 * i + b, b)
                for b in range(2):
                    low(2 * i + b, b)

        @block.tensor
        def _(pe):
            pe.sem_inc(turned_done, 2)
            with pe.Fori(0, TILES // 2) as i:
                for b in range(2):
                    pe.wait_ge(normed_done, 2 * i + b + 1)
                    pe.wait_ge(lo_done, 2 * i + b + 1)
                    for kt in range(KT):
                        last = pe.transpose(turned[b][:, kt, :], normed[:, b, feature_tiles(kt)], ident[:])
                    last.then_inc(turned_done, 1)

        @block.scalar
        def _(act):
            with act.Fori(0, TILES // 2) as i:
                for b in range(2):
                    act.wait_ge(turned_done, 2 * i + b + 3)
                    act.copy(feat_hi[:, :, bass.ts(2 * i + b, P)], turned[b][:]).then_inc(hi_done, 1)


FP4_GROUP = 2 * P
FP4_HIDDEN = 4096
FP4_GROUPS = FP4_HIDDEN // FP4_GROUP
FP4_BLOCK = 32
FP4_COLS = 2 * 2 * FP4_GROUP + DIM


def nvfp4_feed_forward(nc, stream, feat_hi, feat_lo, codes, scales):
    with Scope(nc, "fp4") as s:
        words = s.sb("words", [P, FP4_COLS], I32)
        scale = s.sb("scale", [P, FP4_COLS])
        bits = s.sb("bits", [P, FP4_COLS], I32)
        weight = s.sb("weight", [P, 2, FP4_COLS])
        w_hi = [s.sb(f"w_hi{b}", [P, 2, FP4_COLS], F32R) for b in range(2)]
        w_lo = [s.sb(f"w_lo{b}", [P, 2, FP4_COLS], F32R) for b in range(2)]
        gelu = s.sb("gelu", [P, 2, TB])
        hidden = s.sb("hidden", [P, 2, TB])
        h_hi = s.sb("h_hi", [P, 2, 2, TB], F32R)
        h_lo = s.sb("h_lo", [P, 2, 2, TB], F32R)
        gate_ps = [s.ps(f"gate{b}", [P, TB]) for b in range(2)]
        up_ps = [s.ps(f"up{b}", [P, TB]) for b in range(2)]
        down_ps = [s.ps(f"down{b}", [P, DIM]) for b in range(SUB)]

        loaded = s.sem("loaded")
        dve_step = s.sem("dve_step")
        w_hi_done, w_lo_done = s.sem("w_hi_done"), s.sem("w_lo_done")
        gate_done, up_done = s.sem("gate_done"), s.sem("up_done")
        gelu_done, product_done = s.sem("gelu_done"), s.sem("product_done")
        h_hi_done, h_lo_done = s.sem("h_hi_done"), s.sem("h_lo_done")
        down_done, added = s.sem("down_done"), s.sem("added")
        block = s.block()
        LOOPS = FP4_GROUPS // 2
        STEPS = 2 * BLOCKS

        @block.sync
        def _(sp):
            def load(group):
                sp.dma_start(words[:], codes[bass.ds(group, 1), :, :].rearrange("g p c -> (g p) c")).then_inc(loaded, 16)
                src = scales[bass.ds(group, 1), :, :]
                rows = bass.AP(tensor=src.tensor, offset=src.offset,
                               ap=[[FP4_COLS, P // 16], [0, 16], [1, FP4_COLS]])
                sp.dma_start(scale[:], rows).then_inc(loaded, 16)

            load(0)
            with sp.Fori(0, FP4_GROUPS - 1) as group:
                sp.wait_ge(dve_step, 6 * group + 7)
                load(group + 1)

        def bits_of(dve, nibble, n):
            dve.wait_ge(dve_step, 3 * n + 1)
            dve.tensor_scalar(bits[:], words[:], 28 - 4 * nibble, 3,
                              ALU.logical_shift_left, ALU.arith_shift_right).then_inc(dve_step, 1)
            dve.wait_ge(dve_step, 3 * n + 2)
            dve.tensor_scalar(bits[:], bits[:], 0x8E000000 - (1 << 32), None,
                              ALU.bitwise_and).then_inc(dve_step, 1)
            dve.wait_ge(dve_step, 3 * n + 3)
            dve.wait_ge(w_lo_done, n + 1)
            dve.scalar_tensor_tensor(out=weight[:, nibble, :], in0=bits[:].bitcast(F16)[:, 1::2],
                                     scalar=16384.0, in1=scale[:], op0=ALU.mult,
                                     op1=ALU.mult).then_inc(dve_step, 1)

        def low_weights(dve, group, b, nibble):
            n = 2 * group + nibble
            dve.wait_ge(w_hi_done, n + 3)
            dve.tensor_tensor(w_lo[b][:, nibble, :], weight[:, nibble, :],
                              w_hi[b][:, nibble, :].bitcast(F32), ALU.subtract).then_inc(w_lo_done, 1)

        @block.vector
        def _(dve):
            dve.sem_inc(dve_step, 1)
            dve.sem_inc(added, SUB)
            dve.sem_inc(product_done, 2)
            dve.sem_inc(h_lo_done, 2)
            dve.sem_inc(w_lo_done, 2)

            def prepare(group, nibble):
                if nibble == 0:
                    dve.wait_ge(loaded, 32 * group + 32)
                bits_of(dve, nibble, 2 * group + nibble)

            def add(n, tb):
                for j in range(SUB):
                    dve.wait_ge(down_done, SUB * (n + 2) + j + 1)
                    tile = stream[:, tb * SUB + j, :]
                    dve.tensor_tensor(tile, tile, down_ps[j][:], ALU.add).then_inc(added, 1)

            def body(it, first, last):
                for t in range(STEPS):
                    n = STEPS * it + t
                    b, tb = t // BLOCKS, t % BLOCKS
                    for c in range(2):
                        chunk = 2 * n + c
                        dve.wait_ge(up_done, chunk + 1)
                        dve.wait_ge(gelu_done, chunk + 1)
                        dve.wait_ge(h_lo_done, chunk + 1)
                        dve.tensor_tensor(hidden[:, c, :], gelu[:, c, :], up_ps[c][:],
                                          ALU.mult).then_inc(product_done, 1)
                    for c in range(2):
                        chunk = 2 * n + c
                        dve.wait_ge(h_hi_done, chunk + 3)
                        dve.tensor_tensor(h_lo[:, t % 2, c, :], hidden[:, c, :],
                                          h_hi[:, t % 2, c, :].bitcast(F32), ALU.subtract).then_inc(h_lo_done, 1)
                    if not (first and t == 0):
                        add(n - 1, (tb - 1) % BLOCKS)
                    if not (last and b == 1):
                        group = 2 * it + b + 1
                        if tb == 1:
                            dve.wait_ge(down_done, SUB * (2 + STEPS * it + BLOCKS * b))
                            prepare(group, 0)
                        if tb == 2:
                            low_weights(dve, group, 1 - b, 0)
                            prepare(group, 1)
                        if tb == 3:
                            low_weights(dve, group, 1 - b, 1)

            for nibble in range(2):
                prepare(0, nibble)
                low_weights(dve, 0, 0, nibble)
            body(0, True, False)
            with dve.Fori(1, LOOPS - 1) as it:
                body(it, False, False)
            body(LOOPS - 1, False, True)
            add(STEPS * LOOPS - 1, BLOCKS - 1)

        @block.scalar
        def _(act):
            act.preload_act_table(ACT.Gelu_apprx_tanh)
            act.sem_inc(w_hi_done, 2)
            act.sem_inc(h_hi_done, 2)

            def high_weights(group, b, nibble):
                n = 2 * group + nibble
                act.wait_ge(dve_step, 3 * n + 4)
                act.copy(w_hi[b][:, nibble, :], weight[:, nibble, :]).then_inc(w_hi_done, 1)

            def body(it, last):
                for t in range(STEPS):
                    n = STEPS * it + t
                    b, tb = t // BLOCKS, t % BLOCKS
                    for c in range(2):
                        chunk = 2 * n + c
                        act.wait_ge(gate_done, chunk + 1)
                        act.wait_ge(product_done, chunk + 1)
                        act.activation(gelu[:, c, :], gate_ps[c][:], ACT.Gelu_apprx_tanh).then_inc(gelu_done, 1)
                    for c in range(2):
                        chunk = 2 * n + c
                        act.wait_ge(product_done, chunk + 3)
                        act.wait_ge(down_done, SUB * (n + 1))
                        act.copy(h_hi[:, t % 2, c, :], hidden[:, c, :]).then_inc(h_hi_done, 1)
                    if not (last and b == 1) and tb in (1, 2):
                        high_weights(2 * it + b + 1, 1 - b, tb - 1)

            high_weights(0, 0, 0)
            high_weights(0, 0, 1)
            with act.Fori(0, LOOPS - 1) as it:
                body(it, False)
            body(LOOPS - 1, True)

        @block.tensor
        def _(pe):
            pe.sem_inc(down_done, 2 * SUB)

            def gate_up(n, group, b, tb):
                pe.wait_ge(w_hi_done, 2 * group + 4)
                pe.wait_ge(w_lo_done, 2 * group + 4)
                cols = slice(tb * TB, (tb + 1) * TB)
                for c in range(2):
                    for part, ps in ((0, gate_ps[c]), (1, up_ps[c])):
                        if part == 0 and not (isinstance(n, int) and n == 0):
                            pe.wait_ge(gelu_done, 2 * n + c - 1)
                        if part == 1:
                            pe.wait_ge(product_done, 2 * n + c + 1)
                        for kt in range(KT):
                            at = part * 2 * FP4_GROUP + (kt // 2) * FP4_GROUP + c * P
                            last = matmul3(pe, ps[:], w_hi[b][:, kt % 2, at:at + P], w_lo[b][:, kt % 2, at:at + P],
                                           feat_hi[:, kt, cols], feat_lo[:, kt, cols], kt == 0, kt == KT - 1)
                        last.then_inc((gate_done, up_done)[part], 1)

            def down(n, b, t):
                pe.wait_ge(h_hi_done, 2 * n + 4)
                pe.wait_ge(h_lo_done, 2 * n + 4)
                for j in range(SUB):
                    pe.wait_ge(added, SUB * n + j + 1)
                    rows = slice(j * P, (j + 1) * P)
                    for c in range(2):
                        last = matmul3(pe, down_ps[j][:], h_hi[:, t % 2, c, rows], h_lo[:, t % 2, c, rows],
                                       w_hi[b][:, c, 4 * FP4_GROUP:], w_lo[b][:, c, 4 * FP4_GROUP:],
                                       c == 0, c == 1)
                    last.then_inc(down_done, 1)

            def body(it, last):
                for t in range(STEPS):
                    n = STEPS * it + t
                    if not (last and t == STEPS - 1):
                        nxt = t + 1
                        gate_up(n + 1, 2 * it + nxt // BLOCKS, (nxt // BLOCKS) % 2, nxt % BLOCKS)
                    down(n, t // BLOCKS, t)

            gate_up(0, 0, 0, 0)
            with pe.Fori(0, LOOPS - 1) as it:
                body(it, False)
            body(LOOPS - 1, True)


HEADS0, HEAD_DIM0, CONV = 6, 64, 4
KEY = HEADS0 * HEAD_DIM0
CT = KEY // P
CHUNK = P
CHUNKS = SEQ // CHUNK
BH = BATCH * HEADS0
LOGITS = 2 * HEADS0
GATE_COLS = KEY + LOGITS
LEVELS = 6


def masks():
    r, c = np.arange(P)[:, None], np.arange(P)[None, :]
    below = [-((r // n % 2 == 1) & (c // n == r // n - 1)).astype(np.float32) for n in (1, 2, 4, 8, 16, 32, 64)]
    out = [r <= c, r > c, np.ones((P, P)), r < c, below[0].T] + below[1:]
    return np.ascontiguousarray(np.stack([np.asarray(m, np.float32) for m in out], 1))


UPTO, AFTER, ONES, BEFORE, PAIR_T, LEVEL0 = range(6)
N_MASKS = LEVEL0 + LEVELS


def project_conv(nc, feat_hi, feat_lo, w_qkv, conv_w, qkv):
    with Scope(nc, "pc") as s:
        taps = s.sb("taps", [P, CT * 3 * CONV])
        w32 = [s.sb(f"w32_{q}", [P, KT * P]) for q in range(3)]
        w_hi = [s.sb(f"w_hi{q}", [P, KT * P], F32R) for q in range(3)]
        w_lo = [s.sb(f"w_lo{q}", [P, KT * P], F32R) for q in range(3)]
        padded = s.sb("padded", [P, BATCH, CONV - 1 + SEQ])
        banks = [s.ps(f"bank{b}", [P, TB]) for b in range(BLOCKS)]
        arrived_w = [s.sem(f"arrived_w{q}") for q in range(3)]
        arrived = s.sem("arrived")
        zeroed = s.sem("zeroed")
        w_hi_done, w_lo_done = s.sem("w_hi_done"), s.sem("w_lo_done")
        product_done, copied = s.sem("product_done"), s.sem("copied")
        taps_done, silu_done = s.sem("taps_done"), s.sem("silu_done")
        block = s.block()

        @block.sync
        def _(sp):
            sp.dma_start(taps[:], conv_w.rearrange("p i t -> p (i t)")).then_inc(arrived, 16)
            for tile in range(CT):
                for q in range(3):
                    if tile:
                        sp.wait_ge(w_lo_done, 3 * (tile - 1) + q + 1)
                    sp.dma_start(w32[q][:], w_qkv[tile, q]).then_inc(arrived_w[q], 16)

        @block.gpsimd
        def _(pool):
            pool.memset(padded[:, :, 0:CONV - 1], 0.0).then_inc(zeroed, 1)

        @block.scalar
        def _(act):
            act.preload_act_table(ACT.Silu)
            act.sem_inc(copied, BLOCKS)

            def high_weights(tile, q):
                act.wait_ge(arrived_w[q], 16 * tile + 16)
                act.wait_ge(product_done, 4 * (3 * tile + q) + 4)
                act.copy(w_hi[q][:], w32[q][:]).then_inc(w_hi_done, 1)

            def body(tile, last):
                for q in range(3):
                    n = 3 * tile + q
                    if not (last and q == 2):
                        high_weights(tile + (q == 2), (q + 1) % 3)
                    act.wait_ge(taps_done, 4 * n + 4)
                    for blk in range(BLOCKS):
                        act.wait_ge(product_done, 4 * n + blk + 13)
                        b, half = divmod(blk, SEQ // TB)
                        at = CONV - 1 + half * TB
                        act.copy(padded[:, b, at:at + TB], banks[blk][:]).then_inc(copied, 1)
                    act.wait_ge(taps_done, 4 * n + 8)
                    row = qkv[:, bass.ds(3 * q + tile, 1), :]
                    act.activation(row, row, ACT.Silu).then_inc(silu_done, 1)

            high_weights(0, 0)
            with act.Fori(0, CT - 1) as tile:
                body(tile, False)
            body(CT - 1, True)

        @block.vector
        def _(dve):
            dve.sem_inc(taps_done, 4)
            dve.wait_ge(arrived, 16)
            dve.wait_ge(zeroed, 1)

            def low_weights(tile, q):
                dve.wait_ge(w_hi_done, 3 * tile + q + 1)
                dve.tensor_tensor(w_lo[q][:], w32[q][:], w_hi[q][:].bitcast(F32),
                                  ALU.subtract).then_inc(w_lo_done, 1)

            def body(tile, last):
                for q in range(3):
                    n = 3 * tile + q
                    if not (last and q == 2):
                        low_weights(tile + (q == 2), (q + 1) % 3)
                    dve.wait_ge(copied, 4 * n + 8)
                    row = qkv[:, bass.ds(3 * q + tile, 1), :].rearrange("p o (b t) -> p (o b) t", b=BATCH)
                    for i in range(CONV):
                        at = 3 * CONV * tile + CONV * q + i
                        tap = taps[:, bass.ds(at, 1)]
                        src = padded[:, :, i:i + SEQ]
                        if i == 0:
                            dve.tensor_scalar(row, src, tap, None, ALU.mult).then_inc(taps_done, 1)
                        else:
                            dve.wait_ge(taps_done, 4 * n + 4 + i)
                            dve.scalar_tensor_tensor(out=row, in0=src, scalar=tap, in1=row,
                                                     op0=ALU.mult, op1=ALU.add).then_inc(taps_done, 1)

            low_weights(0, 0)
            with dve.Fori(0, CT - 1) as tile:
                body(tile, False)
            body(CT - 1, True)

        @block.tensor
        def _(pe):
            pe.sem_inc(product_done, 12)
            with pe.Fori(0, CT) as tile:
                for q in range(3):
                    n = 3 * tile + q
                    pe.wait_ge(w_lo_done, n + 1)
                    for blk in range(BLOCKS):
                        pe.wait_ge(copied, 4 * n + blk + 1)
                        cols = slice(blk * TB, (blk + 1) * TB)
                        for kt in range(KT):
                            at = slice(kt * P, (kt + 1) * P)
                            last = matmul3(pe, banks[blk][:], w_hi[q][:, at], w_lo[q][:, at],
                                           feat_hi[:, kt, cols], feat_lo[:, kt, cols], kt == 0, kt == KT - 1)
                        last.then_inc(product_done, 1)


def gates_and_decays(nc, feat_hi, feat_lo, w_gate, head_rows, gate, beta, decay):
    with Scope(nc, "gd") as s:
        w32 = s.sb("w32", [P, KT, GATE_COLS])
        w_hi, w_lo = s.sb("w_hi", [P, KT, GATE_COLS], F32R), s.sb("w_lo", [P, KT, GATE_COLS], F32R)
        rows = s.sb("rows", [P, KEY + 2 * HEADS0])
        tile_hi, tile_lo = s.sb("tile_hi", [P, 2, KT, P], F32R), s.sb("tile_lo", [P, 2, KT, P], F32R)
        logits = s.sb("logits", [P, TILES, LOGITS])
        soft = s.sb("soft", [P, TILES, HEADS0])
        rate = s.sb("rate", [P, HEADS0])
        banks = [s.ps(f"bank{b}", [P, GATE_COLS]) for b in range(2)]
        arrived = s.sem("arrived")
        w_hi_done, w_lo_done = s.sem("w_hi_done"), s.sem("w_lo_done")
        tiled, product_done, silu_done, logits_done, weighted = (
            s.sem(x) for x in ("tiled", "product_done", "silu_done", "logits_done", "weighted"))
        act_step, dve_step = s.sem("act_step"), s.sem("dve_step")
        block = s.block()

        @block.sync
        def _(sp):
            sp.dma_start(w32[:], w_gate.rearrange("k p n -> p k n")).then_inc(arrived, 16)
            sp.dma_start(rows[:], head_rows.partition_broadcast(P)).then_inc(arrived, 16)

        @block.gpsimd
        def _(pool):
            with pool.Fori(0, TILES // 2) as i:
                for b in range(2):
                    pool.wait_ge(product_done, 2 * i + b + 1)
                    cols = bass.ts(2 * i + b, P)
                    pool.tensor_copy(tile_hi[:, b], feat_hi[:, :, cols]).then_inc(tiled, 1)
                    pool.tensor_copy(tile_lo[:, b], feat_lo[:, :, cols]).then_inc(tiled, 1)

        @block.tensor
        def _(pe):
            pe.sem_inc(product_done, 2)
            pe.wait_ge(w_lo_done, 1)
            with pe.Fori(0, TILES // 2) as i:
                for b in range(2):
                    pe.wait_ge(tiled, 4 * i + 2 * b + 2)
                    pe.wait_ge(logits_done, 2 * i + b + 1)
                    for kt in range(KT):
                        last = matmul3(pe, banks[b][:], tile_hi[:, b, kt, :], tile_lo[:, b, kt, :],
                                       w_hi[:, kt, :], w_lo[:, kt, :], kt == 0, kt == KT - 1)
                    last.then_inc(product_done, 1)

        @block.scalar
        def _(act):
            act.preload_act_table(ACT.Silu)
            act.sem_inc(logits_done, 2)
            act.wait_ge(arrived, 32)
            act.copy(w_hi[:], w32[:]).then_inc(w_hi_done, 1)
            with act.Fori(0, TILES // 2) as i:
                for b in range(2):
                    act.wait_ge(product_done, 2 * i + b + 3)
                    at = bass.ds(2 * i + b, 1)
                    act.activation(gate[:, at, 0:KEY], banks[b][:, 0:KEY], ACT.Silu).then_inc(silu_done, 1)
                    act.copy(logits[:, at, :], banks[b][:, KEY:]).then_inc(logits_done, 1)
            act.preload_act_table_set("natural_log_exp_and_others")
            act.activation(rate[:], rows[:, KEY + HEADS0:], ACT.Exp).then_inc(act_step, 1)
            act.wait_ge(logits_done, TILES + 2)
            act.activation(beta[:], logits[:, :, 0:HEADS0], ACT.Exp, scale=-1.0).then_inc(act_step, 1)
            act.wait_ge(dve_step, 2)
            act.activation(soft[:], soft[:], ACT.Exp, scale=-1.0).then_inc(act_step, 1)
            act.wait_ge(dve_step, 3)
            act.activation(soft[:], soft[:], ACT.Ln).then_inc(act_step, 1)

        @block.vector
        def _(dve):
            dve.wait_ge(w_hi_done, 1)
            dve.tensor_tensor(w_lo[:], w32[:], w_hi[:].bitcast(F32), ALU.subtract).then_inc(w_lo_done, 1)
            norm_weight = rows[:, 0:KEY].rearrange("p (o n) -> p o n", o=1)
            with dve.Fori(0, TILES) as i:
                dve.wait_ge(silu_done, i + 1)
                row = gate[:, bass.ds(i, 1), 0:KEY]
                dve.tensor_tensor(row, row, norm_weight, ALU.mult).then_inc(weighted, 1)
            dve.wait_ge(logits_done, TILES + 2)
            z = logits[:, :, HEADS0:]
            bias = rows[:, KEY:KEY + HEADS0].rearrange("p (o h) -> p o h", o=1).broadcast_to([P, TILES, HEADS0])
            dve.tensor_tensor(z, z, bias, ALU.add).then_inc(dve_step, 1)
            dve.wait_ge(dve_step, 1)
            dve.scalar_tensor_tensor(out=soft[:], in0=z, scalar=-1.0, in1=z, op0=ALU.mult,
                                     op1=ALU.max).then_inc(dve_step, 1)
            dve.wait_ge(act_step, 3)
            dve.tensor_scalar(soft[:], soft[:], 1.0, None, ALU.add).then_inc(dve_step, 1)
            dve.tensor_scalar(beta[:], beta[:], 1.0, None, ALU.add).then_inc(dve_step, 1)
            dve.wait_ge(dve_step, 4)
            dve.reciprocal(beta[:], beta[:]).then_inc(dve_step, 1)
            dve.wait_ge(act_step, 4)
            dve.scalar_tensor_tensor(out=soft[:], in0=z, scalar=0.0, in1=soft[:],
                                     op0=ALU.max, op1=ALU.add).then_inc(dve_step, 1)
            dve.wait_ge(dve_step, 6)
            spread = rate[:].rearrange("p (o h) -> p o h", o=1).broadcast_to([P, TILES, HEADS0])
            dve.tensor_tensor(decay[:], soft[:], spread, ALU.mult).then_inc(dve_step, 1)
            dve.wait_ge(dve_step, 7)
            dve.tensor_scalar(decay[:], decay[:], -1.0, None, ALU.mult).then_inc(dve_step, 1)


def delta_rule(nc, stream, ident, mask, hidden, qkv, beta, decay, w_out):
    with Scope(nc, "dr") as s:
        FOURS = BH // 4
        PAIRS = BH // 2
        w_hi, w_lo = s.sb("w_hi", [P, CT, DIM], F32R), s.sb("w_lo", [P, CT, DIM], F32R)
        raw = s.sb("raw", [P, BATCH, 3 * CT, P])
        norm, power = (s.sb(x, [P, BATCH, 2, HEADS0]) for x in ("norm", "power"))
        q_n, k_n, k_d, v_t = (s.sb(x, [P, BATCH, KEY]) for x in ("q_n", "k_n", "k_d", "v_t"))
        o_n = q_n
        o_hi, o_lo = s.sb("o_hi", [P, BATCH, CT, P], F32R), s.sb("o_lo", [P, BATCH, CT, P], F32R)
        q_g = s.sb("q_g", [P, BATCH, KEY])
        o_square = q_g
        k_w = raw[:].rearrange("p b i t -> p (b i t)")[:, 0:BATCH * KEY].rearrange("p (b n) -> p b n", b=BATCH)
        fm = s.sb("fm", [P, 3, BATCH, CT, P])
        g_now, beta_now = s.sb("g_now", [P, BATCH, HEADS0]), s.sb("beta_now", [P, BATCH, HEADS0])
        g_cols = s.sb("g_cols", [P, BH, P])
        w32 = g_cols[:].rearrange("p h t -> p (h t)").rearrange("p (k n) -> p k n", k=CT)
        e_g = s.sb("e_g", [P, 3, BH])
        minus_e_g = s.sb("minus_e_g", [P, BH])
        e_end = s.sb("e_end", [P, PAIRS])
        att = s.sb("att", [P, BH, P])
        a_t = s.sb("a_t", [P, BH, P])
        t_m, t_t, y_m = (s.sb(x, [P, BH, P]) for x in ("t_m", "t_t", "y_m"))
        square = y_m[:].rearrange("p h t -> p (h t)").rearrange("p (b a n) -> p b a n", b=BATCH, a=2)
        w_t = s.sb("w_t", [P, PAIRS, P])
        u_m = s.sb("u_m", [P, BH, HEAD_DIM0])
        state = s.sb("state", [P, PAIRS, HEAD_DIM0])
        o_norm = s.sb("o_norm", [P, BH])
        banks = [s.ps(f"bank{b}", [P, TB]) for b in range(8)]

        arrived, residual_in = s.sem("arrived"), s.sem("residual_in")
        w_hi_done, w_lo_done, const_done = s.sem("w_hi_done"), s.sem("w_lo_done"), s.sem("const_done")
        raw_done, now_done, g_cols_done, norm_done, masked, beta_in, o_norm_done = (
            s.sem(x) for x in ("raw_done", "now_done", "g_cols_done", "norm_done", "masked", "beta_in", "o_norm_done"))
        turned, sums_done, dlog_done, fm_turned, kk_done, qk_done, t0_turned = (
            s.sem(x) for x in ("turned", "sums_done", "dlog_done", "fm_turned", "kk_done", "qk_done", "t0_turned"))
        y_ps, z_ps, w_ps, u_ps, o_ps, state_ps, o_turned, out_ps = (
            s.sem(x) for x in ("y_ps", "z_ps", "w_ps", "u_ps", "o_ps", "state_ps", "o_turned", "out_ps"))
        e_g_done, squared, v_done, dec_done, fm_done, t0_done, w_done, o_squared, o_hi_done = (
            s.sem(x) for x in ("e_g_done", "squared", "v_done", "dec_done", "fm_done", "t0_done", "w_done",
                               "o_squared", "o_hi_done"))
        summed, normed, scaled, small, a_done, att_done, tt_done, y_done, t_done = (
            s.sem(x) for x in ("summed", "normed", "scaled", "small", "a_done", "att_done", "tt_done", "y_done", "t_done"))
        evens_done = s.sem("evens_done")
        u_done, state_done, o_summed, o_done, gated, o_lo_done, written = (
            s.sem(x) for x in ("u_done", "state_done", "o_summed", "o_done", "gated", "o_lo_done", "written"))
        block = s.block()

        def const(which, heads):
            return mask[:, which:which + 1, :].broadcast_to([P, heads, P])

        def fours(ap, f):
            return ap[:, 4 * f:4 * f + 4, :]

        def product_heads(ap, f):
            return ap[:, (slice(0, 8, 2), slice(1, 8, 2), slice(8, 12))[f], :]

        def bank_of_four(b):
            return banks[b][:].rearrange("p (h t) -> p h t", h=4)

        def bank_of_heads(b):
            return banks[b][:, 0:KEY].rearrange("p (h d) -> p h d", h=HEADS0)

        def heads(ap):
            if len(ap.shape) == 2:
                return ap.rearrange("p (h d) -> p h d", d=HEAD_DIM0)
            return ap.rearrange("p b (h d) -> p (b h) d", d=HEAD_DIM0)

        def along(ap, width):
            return ap.unsqueeze(2).broadcast_to([P, ap.shape[1], width])

        def tile_of(b, c):
            return bass.ds(b * CHUNKS + c, 1)

        def half_rows(h):
            return slice((h % 2) * HEAD_DIM0, (h % 2 + 1) * HEAD_DIM0)

        @block.sync
        def _(sp):
            sp.dma_start(w32, w_out.rearrange("(k p) n -> p k n", p=P)).then_inc(arrived, 16)
            with sp.Fori(0, CHUNKS) as c:
                for b in range(BATCH):
                    sp.wait_ge(gated, 2 * c + b + 1)
                    rows = hidden[bass.ds((b * CHUNKS + c) * P, P), :]
                    sp.dma_start(stream[:, tile_of(b, c), :], rows).then_inc(residual_in, 16)

        @block.gpsimd
        def _(pool):
            pool.memset(power[:], -0.5).then_inc(const_done, 1)
            pool.memset(state[:], 0.0).then_inc(const_done, 1)
            pool.wait_ge(const_done, 2)
            pool.wait_ge(w_lo_done, 1)
            with pool.Fori(0, CHUNKS) as c:
                pool.wait_ge(written, 2 * c + 2)
                pool.wait_ge(state_done, 2 * c + 2)
                for b in range(BATCH):
                    cols = bass.ds(b * SEQ + c * CHUNK, CHUNK)
                    pool.tensor_copy(raw[:, b], qkv[:, :, cols]).then_inc(raw_done, 1)
                for b in range(BATCH):
                    pool.tensor_copy(g_now[:, b, :], decay[:, tile_of(b, c), :]).then_inc(now_done, 1)
                    pool.tensor_copy(beta_now[:, b, :], beta[:, tile_of(b, c), :]).then_inc(now_done, 1)
                pool.wait_ge(now_done, 4 * c + 4)
                g_flat = g_now[:].rearrange("p b h -> p (b h)")
                beta_flat = beta_now[:].rearrange("p b h -> p (b h)")
                pool.tensor_tensor(g_cols[:], const(UPTO, BH), along(g_flat, P), ALU.mult).then_inc(g_cols_done, 1)
                pool.wait_ge(summed, 2 * c + 2)
                pool.tensor_tensor(norm[:], norm[:], power[:], ALU.pow).then_inc(norm_done, 1)
                pool.wait_ge(dec_done, 3 * c + 3)
                pool.tensor_tensor(a_t[:], att[:], const(BEFORE, BH), ALU.mult).then_inc(masked, 1)
                pool.wait_ge(masked, 2 * c + 1)
                pool.tensor_tensor(a_t[:], a_t[:], along(beta_flat, P), ALU.mult).then_inc(beta_in, 1)
                pool.tensor_tensor(att[:], att[:], const(UPTO, BH), ALU.mult).then_inc(masked, 1)
                pool.wait_ge(o_summed, 2 * c + 2)
                pool.tensor_tensor(o_norm[:], o_norm[:], power[:].rearrange("p b a h -> p (b a h)")[:, 0:BH],
                                   ALU.pow).then_inc(o_norm_done, 1)

        @block.scalar
        def _(act):
            act.preload_act_table(ACT.Exp)
            act.wait_ge(arrived, 16)
            act.copy(w_hi[:], w32).then_inc(w_hi_done, 1)
            with act.Fori(0, CHUNKS) as c:
                for b in range(BATCH):
                    for part in range(2):
                        act.wait_ge(turned, 6 * c + 3 * b + part + 1)
                        act.activation(square[:, b, part, :], banks[3 * b + part][:, 0:KEY],
                                       ACT.Square).then_inc(squared, 1)
                    act.wait_ge(turned, 6 * c + 3 * b + 3)
                    act.copy(v_t[:, b, :], banks[3 * b + 2][:, 0:KEY]).then_inc(v_done, 1)
                act.wait_ge(sums_done, c + 1)
                act.activation(e_g[:], banks[6][:, 0:3 * BH], ACT.Exp).then_inc(e_g_done, 1)
                for f in range(FOURS):
                    act.wait_ge(dlog_done, 3 * c + f + 1)
                    act.activation(fours(att, f), bank_of_four(7 - f % 2), ACT.Exp).then_inc(dec_done, 1)
                for x in range(6):
                    act.wait_ge(fm_turned, 6 * c + x + 1)
                    act.copy(fm[:, x // 2, x % 2], banks[x][:, 0:KEY].rearrange("p (k t) -> p k t", k=CT))\
                       .then_inc(fm_done, 1)
                for f in range(FOURS):
                    act.wait_ge(t0_turned, 3 * c + f + 1)
                    act.copy(fours(t_m, f), bank_of_four(f)).then_inc(t0_done, 1)
                for b in range(BATCH):
                    act.wait_ge(w_ps, 2 * c + b + 1)
                    act.copy(w_t[:, CT * b:CT * b + CT, :], banks[6 + b][:, 0:KEY].rearrange("p (k t) -> p k t", k=CT))\
                       .then_inc(w_done, 1)
                for odd in range(2):
                    act.wait_ge(o_ps, 2 * c + odd + 1)
                    act.activation(o_square[:, odd, :], banks[2 + odd][:, 0:KEY], ACT.Square).then_inc(o_squared, 1)
                for b in range(BATCH):
                    act.wait_ge(o_turned, 2 * c + b + 1)
                    act.copy(o_hi[:, b], banks[5 + b][:, 0:KEY].rearrange("p (k t) -> p k t", k=CT))\
                       .then_inc(o_hi_done, 1)

        @block.vector
        def _(dve):
            dve.wait_ge(w_hi_done, 1)
            dve.tensor_tensor(w_lo[:], w32, w_hi[:].bitcast(F32), ALU.subtract).then_inc(w_lo_done, 1)
            dve.sem_inc(written, 2)
            dve.sem_inc(state_done, 2)
            with dve.Fori(0, CHUNKS) as c:
                dve.wait_ge(squared, 4 * c + 4)
                dve.tensor_reduce(norm[:].rearrange("p b a h -> p (b a h)"),
                                  square.rearrange("p b a (h d) -> p (b a h) d", d=HEAD_DIM0),
                                  AX.X, ALU.add).then_inc(summed, 1)
                dve.wait_ge(summed, 2 * c + 1)
                dve.tensor_scalar(norm[:], norm[:], 1e-6, None, ALU.add).then_inc(summed, 1)
                dve.wait_ge(norm_done, c + 1)
                dve.tensor_scalar(norm[:, :, 0, :], norm[:, :, 0, :], HEAD_DIM0 ** -0.5, None,
                                  ALU.mult).then_inc(small, 1)
                dve.wait_ge(e_g_done, c + 1)
                dve.tensor_scalar(minus_e_g[:], e_g[:, 0, :], -1.0, None, ALU.mult).then_inc(small, 1)
                dve.tensor_copy(e_end[0:HEAD_DIM0, :], e_g[0:HEAD_DIM0, 2, 0::2]).then_inc(small, 1)
                dve.tensor_copy(e_end[HEAD_DIM0:, :], e_g[HEAD_DIM0:, 2, 1::2]).then_inc(small, 1)
                dve.wait_ge(small, 4 * c + 4)
                for b in range(BATCH):
                    dve.tensor_tensor(heads(k_n[:, b, :]), bank_of_heads(3 * b + 1),
                                      along(norm[:, b, 1, :], HEAD_DIM0), ALU.mult).then_inc(normed, 1)
                    dve.tensor_tensor(heads(q_n[:, b, :]), bank_of_heads(3 * b),
                                      along(norm[:, b, 0, :], HEAD_DIM0), ALU.mult).then_inc(normed, 1)
                dve.wait_ge(normed, 4 * c + 4)
                dve.tensor_tensor(heads(q_g[:]), heads(q_n[:]), along(e_g[:, 0, :], HEAD_DIM0), ALU.mult).then_inc(scaled, 1)
                dve.tensor_tensor(heads(k_w), heads(k_n[:]), along(minus_e_g[:], HEAD_DIM0), ALU.mult).then_inc(scaled, 1)
                dve.tensor_tensor(heads(k_d[:]), heads(k_n[:]), along(e_g[:, 1, :], HEAD_DIM0), ALU.mult).then_inc(scaled, 1)
                dve.wait_ge(beta_in, c + 1)
                for f in range(FOURS):
                    dve.wait_ge(kk_done, 3 * c + f + 1)
                    dve.tensor_tensor(product_heads(a_t, f), bank_of_four(f), product_heads(a_t, f), ALU.mult).then_inc(a_done, 1)
                dve.wait_ge(a_done, 3 * c + 3)
                dve.tensor_tensor(t_t[:], a_t[:], const(PAIR_T, BH), ALU.mult).then_inc(tt_done, 1)
                dve.wait_ge(tt_done, 2 * c + 1)
                dve.tensor_tensor(t_t[:], t_t[:], ident[:].unsqueeze(1).broadcast_to([P, BH, P]), ALU.add).then_inc(tt_done, 1)
                dve.wait_ge(masked, 2 * c + 2)
                for f in range(FOURS):
                    dve.wait_ge(qk_done, 3 * c + f + 1)
                    dve.tensor_tensor(product_heads(att, f), bank_of_four(3 + f), product_heads(att, f), ALU.mult).then_inc(att_done, 1)
                dve.wait_ge(t0_done, 3 * c + 3)
                for level in range(LEVELS):
                    last = level == LEVELS - 1
                    for f in range(FOURS):
                        at = FOURS * (LEVELS * c + level) + f
                        dve.wait_ge(y_ps, at + 1)
                        dve.tensor_tensor(fours(y_m, f), bank_of_four(f), const(LEVEL0 + level, 4),
                                          ALU.mult).then_inc(y_done, 1)
                    for f in range(FOURS):
                        at = FOURS * (LEVELS * c + level) + f
                        dve.wait_ge(z_ps, at + 1)
                        if not last:
                            dve.tensor_tensor(fours(t_m, f), fours(t_m, f), bank_of_four(3 + f),
                                              ALU.add).then_inc(t_done, 1)
                        dve.tensor_tensor(fours(t_t, f), fours(t_t, f), bank_of_four(f), ALU.add).then_inc(t_done, 1)
                beta_flat = beta_now[:].rearrange("p b h -> p (b h)")
                for odd in range(2):
                    dve.wait_ge(u_ps, 2 * c + odd + 1)
                    dve.tensor_tensor(u_m[:, odd::2, :], bank_of_heads(odd),
                                      along(beta_flat[:, odd::2], HEAD_DIM0), ALU.mult).then_inc(u_done, 1)
                for odd in range(2):
                    dve.wait_ge(o_squared, 2 * c + odd + 1)
                dve.tensor_reduce(o_norm[:], heads(o_square[:]), AX.X, ALU.add).then_inc(o_summed, 1)
                dve.wait_ge(o_summed, 2 * c + 1)
                dve.tensor_scalar(o_norm[:], o_norm[:], 1.0 / HEAD_DIM0, EPS, ALU.mult, ALU.add).then_inc(o_summed, 1)
                dve.wait_ge(state_ps, c + 1)
                dve.tensor_tensor(state[:], state[:], along(e_end[:], HEAD_DIM0), ALU.mult).then_inc(state_done, 1)
                dve.wait_ge(state_done, 2 * c + 3)
                dve.tensor_tensor(state[:], state[:], banks[4][:, 0:KEY].rearrange("p (j d) -> p j d", j=PAIRS),
                                  ALU.add).then_inc(state_done, 1)
                dve.wait_ge(o_norm_done, c + 1)
                for odd in range(2):
                    dve.tensor_tensor(heads(o_n[:])[:, odd::2, :], bank_of_heads(2 + odd),
                                      along(o_norm[:, HEADS0 * odd:HEADS0 * (odd + 1)], HEAD_DIM0),
                                      ALU.mult).then_inc(o_done, 1)
                dve.wait_ge(o_done, 2 * c + 2)
                for b in range(BATCH):
                    row = o_n[:, b:b + 1, :]
                    dve.tensor_tensor(row, row, stream[:, tile_of(b, c), 0:KEY], ALU.mult).then_inc(gated, 1)
                for b in range(BATCH):
                    dve.wait_ge(o_hi_done, 2 * c + b + 1)
                    dve.tensor_tensor(o_lo[:, b], banks[5 + b][:, 0:KEY].rearrange("p (k t) -> p k t", k=CT),
                                      o_hi[:, b].bitcast(F32), ALU.subtract).then_inc(o_lo_done, 1)
                dve.wait_ge(residual_in, 32 * c + 32)
                for b in range(BATCH):
                    dve.wait_ge(out_ps, 2 * c + b + 1)
                    row = stream[:, tile_of(b, c), :]
                    bank = banks[(7, 0)[b]][:].rearrange("p (o n) -> p o n", o=1)
                    dve.tensor_tensor(row, row, bank, ALU.add).then_inc(written, 1)

        @block.tensor
        def _(pe):
            pe.wait_ge(w_lo_done, 1)
            pe.wait_ge(const_done, 2)
            with pe.Fori(0, CHUNKS) as c:
                for b in range(BATCH):
                    pe.wait_ge(raw_done, 2 * c + b + 1)
                    for part in range(3):
                        for k in range(CT):
                            last = pe.transpose(banks[3 * b + part][:, k * P:(k + 1) * P], raw[:, b, CT * part + k, :], ident[:])
                        last.then_inc(turned, 1)
                pe.wait_ge(now_done, 4 * c + 4)
                g = g_now[:].rearrange("p b h -> p (b h)")
                for x, which in enumerate((UPTO, AFTER, ONES)):
                    last = pe.matmul(banks[6][:, BH * x:BH * (x + 1)], mask[:, which, :], g, start=True, stop=True)
                last.then_inc(sums_done, 1)
                pe.wait_ge(g_cols_done, c + 1)
                for f in range(FOURS):
                    if f == 1:
                        pe.wait_ge(e_g_done, c + 1)
                    if f == 2:
                        pe.wait_ge(dec_done, 3 * c + 1)
                    pe.matmul(banks[7 - f % 2][:], mask[:, AFTER, :], fours(g_cols, f).rearrange("p h t -> p (h t)"),
                              start=True, stop=True).then_inc(dlog_done, 1)
                pe.wait_ge(v_done, 2 * c + 2)
                for x, (source, done, count) in enumerate((
                        (k_n, normed, 4 * c + 4), (k_n, normed, 4 * c + 4), (q_n, normed, 4 * c + 4),
                        (q_n, normed, 4 * c + 4), (q_g, scaled, 3 * c + 1), (q_g, scaled, 3 * c + 1))):
                    pe.wait_ge(done, count)
                    for k in range(CT):
                        last = pe.transpose(banks[x][:, k * P:(k + 1) * P], source[:, x % 2, k * P:(k + 1) * P], ident[:])
                    last.then_inc(fm_turned, 1)
                for kind, done in ((0, kk_done), (1, qk_done)):
                    pe.wait_ge(fm_done, 6 * c + 6)
                    for i in (0, 1, 2, 3, 4, 5, 6, 7, 8, 10, 9, 11):
                        b, h = divmod(i, HEADS0)
                        bank, col = (i % 2, i // 2) if i < 8 else (2, i - 8)
                        if i == 9:
                            pe.wait_ge(evens_done, 2 * c + kind + 1)
                        last = pe.matmul(banks[3 * kind + bank][:, col * P:(col + 1) * P],
                                         fm[half_rows(h), 0, b, h // 2, :], fm[half_rows(h), kind, b, h // 2, :],
                                         start=True, stop=True)
                        if i in (6, 7, 11):
                            last.then_inc(done, 1)
                        if i == 10:
                            last.then_inc(evens_done, 1)
                pe.wait_ge(tt_done, 2 * c + 2)
                for f in range(FOURS):
                    for j in range(4):
                        last = pe.transpose(banks[f][:, j * P:(j + 1) * P], t_t[:, 4 * f + j, :], ident[:])
                    last.then_inc(t0_turned, 1)
                for level in range(LEVELS):
                    updates = 2 * FOURS * LEVELS - FOURS
                    for f in range(FOURS):
                        if level == 0:
                            pe.wait_ge(t0_done, 3 * c + f + 1)
                            pe.wait_ge(att_done, 3 * c + 3)
                        else:
                            pe.wait_ge(t_done, updates * c + 2 * (FOURS * (level - 1) + f) + 2)
                        for j in range(4):
                            i = 4 * f + j
                            last = pe.matmul(banks[f][:, j * P:(j + 1) * P], a_t[:, i, :], t_m[:, i, :],
                                             start=True, stop=True)
                        last.then_inc(y_ps, 1)
                    for f in range(FOURS):
                        pe.wait_ge(y_done, FOURS * (LEVELS * c + level) + f + 1)
                        for j in range(4):
                            i = 4 * f + j
                            cols = slice(j * P, (j + 1) * P)
                            if level < LEVELS - 1:
                                pe.matmul(banks[3 + f][:, cols], t_t[:, i, :], y_m[:, i, :], start=True, stop=True)
                            last = pe.matmul(banks[f][:, cols], y_m[:, i, :], t_t[:, i, :], start=True, stop=True)
                        last.then_inc(z_ps, 1)
                pe.wait_ge(t_done, updates * (c + 1))
                pe.wait_ge(scaled, 3 * c + 3)
                for i in range(BH):
                    b, h = divmod(i, HEADS0)
                    last = pe.matmul(banks[6 + b][half_rows(h), (h // 2) * P:(h // 2 + 1) * P],
                                     k_w[:, b, h * HEAD_DIM0:(h + 1) * HEAD_DIM0], t_t[:, i, :], start=True, stop=True)
                    if h == HEADS0 - 1:
                        last.then_inc(w_ps, 1)
                pe.wait_ge(w_done, 2 * c + 2)
                for i in range(BH):
                    b, h = divmod(i, HEADS0)
                    at = slice((i // 2) * HEAD_DIM0, (i // 2 + 1) * HEAD_DIM0)
                    pe.matmul(banks[i % 2][:, at], t_t[:, i, :], v_t[:, b, h * HEAD_DIM0:(h + 1) * HEAD_DIM0],
                              start=True, stop=False)
                    last = pe.matmul(banks[i % 2][:, at], w_t[half_rows(h), i // 2, :], state[half_rows(h), i // 2, :],
                                     start=False, stop=True)
                    if i >= BH - 2:
                        last.then_inc(u_ps, 1)
                for i in range(BH):
                    b, h = divmod(i, HEADS0)
                    at = slice((i // 2) * HEAD_DIM0, (i // 2 + 1) * HEAD_DIM0)
                    pe.wait_ge(u_done, 2 * c + 2)
                    pe.matmul(banks[2 + i % 2][:, at], fm[half_rows(h), 2, b, h // 2, :], state[half_rows(h), i // 2, :],
                              start=True, stop=False)
                    last = pe.matmul(banks[2 + i % 2][:, at], att[:, i, :], u_m[:, i, :], start=False, stop=True)
                    if i >= BH - 2:
                        last.then_inc(o_ps, 1)
                for i in range(BH):
                    b, h = divmod(i, HEADS0)
                    last = pe.matmul(banks[4][half_rows(h), (i // 2) * HEAD_DIM0:(i // 2 + 1) * HEAD_DIM0],
                                     k_d[:, b, h * HEAD_DIM0:(h + 1) * HEAD_DIM0], u_m[:, i, :], start=True, stop=True)
                last.then_inc(state_ps, 1)
                for b in range(BATCH):
                    pe.wait_ge(gated, 2 * c + b + 1)
                    for k in range(CT):
                        last = pe.transpose(banks[5 + b][:, k * P:(k + 1) * P], o_n[:, b, k * P:(k + 1) * P], ident[:])
                    last.then_inc(o_turned, 1)
                for b in range(BATCH):
                    pe.wait_ge(o_lo_done, 2 * c + b + 1)
                    for k in range(CT):
                        last = matmul3(pe, banks[(7, 0)[b]][:], o_hi[:, b, k, :], o_lo[:, b, k, :],
                                       w_hi[:, k, :], w_lo[:, k, :], k == 0, k == CT - 1)
                    last.then_inc(out_ps, 1)


def delta_attention(nc, stream, ident, mask, hidden, w_qkv, conv_w, w_gate, head_rows, w_out):
    with Scope(nc, "da") as keep:
        qkv = keep.sb("qkv", [P, 3 * CT, TOKENS])
        beta, decay = keep.sb("beta", [P, TILES, HEADS0]), keep.sb("decay", [P, TILES, HEADS0])
        with Scope(nc, "daf") as f:
            feat_hi, feat_lo = f.sb("feat_hi", [P, KT, TOKENS], F32R), f.sb("feat_lo", [P, KT, TOKENS], F32R)
            normalise(nc, "n0a", stream, ident, feat_hi, feat_lo, feature_tiles_plain)
            project_conv(nc, feat_hi, feat_lo, w_qkv, conv_w, qkv)
            gates_and_decays(nc, feat_hi, feat_lo, w_gate, head_rows, stream, beta, decay)
        delta_rule(nc, stream, ident, mask, hidden, qkv, beta, decay, w_out)


HEADS1, HALF, HEAD_DIM1, LATENT = 16, 16, 32, 64
QUAD = 4
QUADS = HEADS1 // QUAD
QTILES = SEQ // P
STACK = 4 * HALF


def latents(nc, feat_hi, feat_lo, w_down, w_value, lat_hi, lat_lo, values):
    with Scope(nc, "lat") as s:
        wd32 = s.sb("wd32", [P, KT, P])
        wv32 = s.sb("wv32", [P, DIM])
        wd_hi, wd_lo = s.sb("wd_hi", [P, KT, P], F32R), s.sb("wd_lo", [P, KT, P], F32R)
        wv_hi, wv_lo = s.sb("wv_hi", [P, DIM], F32R), s.sb("wv_lo", [P, DIM], F32R)
        lat_ps = [s.ps(f"lat{b}", [P, TB]) for b in range(2)]
        val_ps = [s.ps(f"val{b}", [P, DIM]) for b in range(2)]
        arrived = s.sem("arrived")
        w_hi_done, w_lo_done = s.sem("w_hi_done"), s.sem("w_lo_done")
        lat_done, val_done = s.sem("lat_done"), s.sem("val_done")
        hi_done, lo_done = s.sem("hi_done"), s.sem("lo_done")
        val_hi_done, val_lo_done = s.sem("val_hi_done"), s.sem("val_lo_done")
        block = s.block()
        KV = slice(LATENT, 2 * LATENT)

        @block.sync
        def _(sp):
            sp.dma_start(wd32[:], w_down.rearrange("(k p) n -> p k n", p=P)).then_inc(arrived, 16)
            sp.dma_start(wv32[KV, :], w_value).then_inc(arrived, 16)

        @block.scalar
        def _(act):
            act.wait_ge(arrived, 32)
            act.copy(wd_hi[:], wd32[:]).then_inc(w_hi_done, 1)
            act.copy(wv_hi[KV, :], wv32[KV, :]).then_inc(w_hi_done, 1)
            for b in range(BLOCKS):
                act.wait_ge(lat_done, b + 1)
                act.copy(lat_hi[:, b * TB:(b + 1) * TB], lat_ps[b % 2][:]).then_inc(hi_done, 1)
            for i in range(TILES):
                act.wait_ge(val_done, i + 1)
                act.copy(values[:, i, :, 0, :], val_ps[i % 2][:].rearrange("p (h d) -> p h d", h=HEADS1))\
                   .then_inc(val_hi_done, 1)

        @block.vector
        def _(dve):
            dve.wait_ge(w_hi_done, 2)
            dve.tensor_tensor(wd_lo[:], wd32[:], wd_hi[:].bitcast(F32), ALU.subtract).then_inc(w_lo_done, 1)
            dve.tensor_tensor(wv_lo[KV, :], wv32[KV, :], wv_hi[KV, :].bitcast(F32),
                              ALU.subtract).then_inc(w_lo_done, 1)
            for b in range(BLOCKS):
                dve.wait_ge(hi_done, b + 1)
                cols = slice(b * TB, (b + 1) * TB)
                dve.tensor_tensor(lat_lo[:, cols], lat_ps[b % 2][:], lat_hi[:, cols].bitcast(F32),
                                  ALU.subtract).then_inc(lo_done, 1)
            for i in range(TILES):
                dve.wait_ge(val_hi_done, i + 1)
                dve.tensor_tensor(values[:, i, :, 1, :], val_ps[i % 2][:].rearrange("p (h d) -> p h d", h=HEADS1),
                                  values[:, i, :, 0, :].bitcast(F32), ALU.subtract).then_inc(val_lo_done, 1)

        @block.tensor
        def _(pe):
            pe.wait_ge(w_hi_done, 2)
            pe.wait_ge(w_lo_done, 2)
            for b in range(BLOCKS):
                if b >= 2:
                    pe.wait_ge(lo_done, b - 1)
                cols = slice(b * TB, (b + 1) * TB)
                for kt in range(KT):
                    last = matmul3(pe, lat_ps[b % 2][:], wd_hi[:, kt, :], wd_lo[:, kt, :],
                                   feat_hi[:, kt, cols], feat_lo[:, kt, cols], kt == 0, kt == KT - 1)
                last.then_inc(lat_done, 1)
            for i in range(TILES):
                if i % SUB == 0:
                    pe.wait_ge(lo_done, i // SUB + 1)
                if i >= 2:
                    pe.wait_ge(val_lo_done, i - 1)
                cols = slice(i * P, (i + 1) * P)
                matmul3(pe, val_ps[i % 2][:], lat_hi[KV, cols], lat_lo[KV, cols], wv_hi[KV, :], wv_lo[KV, :],
                        True, True).then_inc(val_done, 1)


def softmax_heads(nc, ident, lat_hi, lat_lo, values, w_up, cos_sin, mixed):
    with Scope(nc, "att") as s:
        wu32 = s.sb("wu32", [P, 2 * P])
        wu_hi, wu_lo = s.sb("wu_hi", [P, 2 * P], F32R), s.sb("wu_lo", [P, 2 * P], F32R)
        tables = s.sb("tables", [P, 2, SEQ])
        rot_hi, rot_lo = s.sb("rot_hi", [P, SEQ], F32R), s.sb("rot_lo", [P, SEQ], F32R)
        q_stack = [s.sb(f"q_stack{b}", [P, SEQ], F32R) for b in range(2)]
        k_stack = [s.sb(f"k_stack{b}", [P, SEQ], F32R) for b in range(2)]
        head_values = s.sb("head_values", [P, 2, QTILES, 2 * HEAD_DIM1], F32R)
        probs = s.sb("probs", [P, 2, SEQ])
        part = probs
        rot = part[:, 0, :]
        pt_hi, pt_lo = s.sb("pt_hi", [P, 2, QTILES, P], F32R), s.sb("pt_lo", [P, 2, QTILES, P], F32R)
        neg_max, total, inverse = s.sb("neg_max", [P, 4]), s.sb("total", [P, 4]), s.sb("inverse", [P, 4])
        high_part = s.sb("high_part", [P, 2, HEAD_DIM1])
        scores = [s.ps(f"scores{b}", [P, 2, TB]) for b in range(2)]
        turned = [s.ps(f"turned{b}", [P, 4, P]) for b in range(2)]
        out_ps = [s.ps(f"out{b}", [P, 2 * HEAD_DIM1]) for b in range(2)]

        arrived = s.sem("arrived")
        quad_arrived = s.sem("quad_arrived")
        wu_hi_done, wu_lo_done = s.sem("wu_hi_done"), s.sem("wu_lo_done")
        proj_done, part_done, rot_done = s.sem("proj_done"), s.sem("part_done"), s.sem("rot_done")
        rot_hi_done, rot_lo_done = s.sem("rot_hi_done"), s.sem("rot_lo_done")
        stacked = [s.sem(f"stacked{b}") for b in range(2)]
        score_done, max_done, exp_done = s.sem("score_done"), s.sem("max_done"), s.sem("exp_done")
        turned_done, hi_done, lo_done = s.sem("turned_done"), s.sem("hi_done"), s.sem("lo_done")
        out_done, inverse_done, high_part_done, normed = (s.sem(x) for x in ("out_done", "inverse_done", "high_part_done", "normed"))
        values_ready = s.sem("values_ready")
        block = s.block()
        TPI = QUAD * QTILES
        STACK_DMAS = 2 * 2 * 4

        def passes(engine, body):
            with engine.Fori(0, BATCH) as b:
                with engine.Fori(0, QUADS) as quad:
                    body(QUADS * b + quad, b, quad)

        @block.sync
        def _(sp):
            sp.dma_start(tables[:], cos_sin).then_inc(arrived, 16)
            sp.sem_inc(stacked[1], 16 * STACK_DMAS)

            def stack(n, pair):
                for j in (2 * pair, 2 * pair + 1):
                    for m in range(4):
                        rows = slice((j % 2) * STACK + m * HALF, (j % 2) * STACK + (m + 1) * HALF)
                        for first, dst, low in ((0, q_stack[pair], m >= 2), (LATENT, k_stack[pair], m % 2)):
                            src = (rot_lo if low else rot_hi)[first + j * HALF:first + (j + 1) * HALF, :]
                            sp.dma_start(dst[rows, :].bitcast(F32), src.bitcast(F32)).then_inc(stacked[pair], 16)

            def body(n, b, quad):
                sp.wait_ge(wu_lo_done, n + 1)
                sp.dma_start(wu32[:], w_up[bass.ds(quad, 1), :, :].rearrange("q p n -> (q p) n")).then_inc(quad_arrived, 16)
                sp.wait_ge(rot_lo_done, n + 1)
                sp.wait_ge(score_done, TPI * n + TPI // 2)
                stack(n, 0)
                sp.wait_ge(score_done, TPI * n + TPI)
                stack(n, 1)

            passes(sp, body)

        @block.gpsimd
        def _(pool):
            def body(n, b, quad):
                for j in range(QUAD):
                    pool.wait_ge(out_done, TPI * n + QTILES * (j + 1))
                    src = values[:, bass.ts(b, QTILES), bass.ds(QUAD * quad + j, 1), :, :]
                    pool.tensor_copy(head_values[:, j % 2, :, :].rearrange("p t (a d) -> p t a d", a=2),
                                     src.rearrange("p t h a d -> p t (h a) d")).then_inc(values_ready, 1)

            passes(pool, body)

        @block.scalar
        def _(act):
            act.preload_act_table(ACT.Exp)
            act.sem_inc(exp_done, 4)

            def weights(n, quad):
                act.wait_ge(proj_done, 2 * n + 2)
                act.wait_ge(quad_arrived, 16 * n + 16)
                act.copy(wu_hi[:], wu32[:]).then_inc(wu_hi_done, 1)

            def exps(n, t):
                at = TPI * n + t
                act.wait_ge(max_done, at + 1)
                act.wait_ge(turned_done, 2 * (at + 1))
                act.wait_ge(inverse_done, at + 1)
                act.activation(probs[:, t % 2, :], scores[t % 2][:], ACT.Exp, bias=neg_max[:, t % 4:t % 4 + 1],
                               accum_out=total[:, t % 4:t % 4 + 1]).then_inc(exp_done, 1)

            def highs(n, t):
                at = TPI * n + t
                act.wait_ge(out_done, at + QTILES * 2 - 1)
                for half in range(2):
                    act.wait_ge(turned_done, 2 * at + half + 5)
                    act.copy(pt_hi[:, t % 2, 4 * half:4 * half + 4, :], turned[half][:]).then_inc(hi_done, 1)

            def body(n, b, quad):
                weights(n, quad)
                act.wait_ge(rot_done, n + 1)
                act.wait_ge(stacked[1], 16 * STACK_DMAS * (n + 1))
                act.copy(rot_hi[:], rot).then_inc(rot_hi_done, 1)
                for t in range(TPI):
                    exps(n, t)
                    if t:
                        highs(n, t - 1)
                highs(n, TPI - 1)

            passes(act, body)

        @block.vector
        def _(dve):
            dve.sem_inc(inverse_done, 4)
            dve.sem_inc(lo_done, 2)
            dve.sem_inc(normed, 2)

            def maxima(n, t):
                at = TPI * n + t
                dve.wait_ge(score_done, at + TPI + 1)
                dve.wait_ge(exp_done, at + 1)
                dve.tensor_reduce(neg_max[:, t % 4:t % 4 + 1], scores[t % 2][:], AX.XY, ALU.max,
                                  negate=True).then_inc(max_done, 1)

            def lows(n, t):
                at = TPI * n + t
                for half in range(2):
                    dve.wait_ge(hi_done, 2 * at + half + 1)
                    dve.tensor_tensor(pt_lo[:, t % 2, 4 * half:4 * half + 4, :], turned[half][:],
                                      pt_hi[:, t % 2, 4 * half:4 * half + 4, :].bitcast(F32),
                                      ALU.subtract).then_inc(lo_done, 1)
                dve.wait_ge(exp_done, at + 5)
                dve.reciprocal(inverse[:, t % 4:t % 4 + 1], total[:, t % 4:t % 4 + 1]).then_inc(inverse_done, 1)

            def normalise_out(n, b, quad, t):
                at = TPI * n + t
                dve.wait_ge(out_done, at + 2 * QTILES + 1)
                dve.wait_ge(inverse_done, at + 5)
                dve.wait_ge(normed, at + 1)
                scale = inverse[:, t % 4:t % 4 + 1]
                dve.tensor_scalar(high_part[:, t % 2, :], out_ps[t % 2][:, 0:HEAD_DIM1], scale, None,
                                  ALU.mult).then_inc(high_part_done, 1)
                dve.wait_ge(high_part_done, at + 1)
                j, tile = t // QTILES, t % QTILES
                dst = mixed[:, bass.ds(QTILES * b + tile, 1), bass.ds(P * quad + HEAD_DIM1 * j, HEAD_DIM1)]
                dve.scalar_tensor_tensor(out=dst, in0=out_ps[t % 2][:, HEAD_DIM1:], scalar=scale,
                                         in1=high_part[:, t % 2, :], op0=ALU.mult, op1=ALU.add).then_inc(normed, 1)

            def body(n, b, quad):
                dve.wait_ge(wu_hi_done, n + 1)
                dve.tensor_tensor(wu_lo[:], wu32[:], wu_hi[:].bitcast(F32),
                                  ALU.subtract).then_inc(wu_lo_done, 1)
                for x in range(2):
                    dve.wait_ge(proj_done, 2 * n + x + 3)
                    dve.tensor_tensor(part[:, x, :], scores[x][:].rearrange("p a t -> p (a t)"), tables[:, x, :],
                                      ALU.mult).then_inc(part_done, 1)
                dve.wait_ge(part_done, 2 * n + 2)
                dve.tensor_tensor(rot, part[:, 0, :], part[:, 1, :], ALU.add).then_inc(rot_done, 1)
                dve.wait_ge(rot_hi_done, n + 1)
                dve.tensor_tensor(rot_lo[:], rot, rot_hi[:].bitcast(F32), ALU.subtract).then_inc(rot_lo_done, 1)
                maxima(n, 0)
                for t in range(TPI):
                    if t + 1 < TPI:
                        maxima(n, t + 1)
                    if t:
                        lows(n, t - 1)
                    if t >= 2:
                        normalise_out(n, b, quad, t - 2)
                lows(n, TPI - 1)
                normalise_out(n, b, quad, TPI - 2)
                normalise_out(n, b, quad, TPI - 1)

            dve.sem_inc(wu_lo_done, 1)
            dve.wait_ge(arrived, 16)
            passes(dve, body)

        @block.tensor
        def _(pe):
            pe.sem_inc(score_done, TPI)
            pe.sem_inc(out_done, 2 * QTILES)
            pe.sem_inc(turned_done, 4)
            pe.sem_inc(proj_done, 2)

            def score(n, t):
                at = TPI * n + t
                j, tile = t // QTILES, t % QTILES
                if t % (2 * QTILES) == 0:
                    pair = j // 2
                    pe.wait_ge(stacked[pair], 16 * STACK_DMAS * (n + 1 + pair))
                if t >= 2:
                    pe.wait_ge(exp_done, at + 3)
                rows = slice((j % 2) * STACK, (j % 2 + 1) * STACK)
                for half in range(2):
                    last = pe.matmul(scores[t % 2][:, half, :], q_stack[j // 2][rows, tile * P:(tile + 1) * P],
                                     k_stack[j // 2][rows, half * TB:(half + 1) * TB], start=True, stop=True)
                last.then_inc(score_done, 1)

            def turn(n, t):
                at = TPI * n + t
                pe.wait_ge(exp_done, at + 5)
                for half in range(2):
                    pe.wait_ge(lo_done, 2 * at + half + 1)
                    for k in range(4):
                        at_key = (4 * half + k) * P
                        last = pe.transpose(turned[half][:, k, :], probs[:, t % 2, at_key:at_key + P], ident[:])
                    last.then_inc(turned_done, 1)

            def output(n, t):
                at = TPI * n + t
                j = t // QTILES
                if t % QTILES == 0:
                    pe.wait_ge(values_ready, QUAD * n + j + 1)
                pe.wait_ge(lo_done, 2 * at + 4)
                pe.wait_ge(normed, at + 1)
                for k in range(QTILES):
                    for half in (pt_hi, pt_lo):
                        last = pe.matmul(out_ps[t % 2][:], half[:, t % 2, k, :], head_values[:, j % 2, k, :],
                                         start=(k == 0 and half is pt_hi), stop=(k == QTILES - 1 and half is pt_lo))
                last.then_inc(out_done, 1)

            def body(n, b, quad):
                pe.wait_ge(wu_lo_done, n + 2)
                for x in range(2):
                    for half in range(2):
                        cols = bass.ds(b * SEQ + half * TB, TB)
                        last = matmul3(pe, scores[x][:, half, :], wu_hi[:, x * P:(x + 1) * P],
                                       wu_lo[:, x * P:(x + 1) * P], lat_hi[:, cols], lat_lo[:, cols], True, True)
                    last.then_inc(proj_done, 1)
                pe.wait_ge(part_done, 2 * n + 2)
                score(n, 0)
                score(n, 1)
                for t in range(TPI):
                    if t + 2 < TPI:
                        score(n, t + 2)
                    turn(n, t)
                    if t:
                        output(n, t - 1)
                output(n, TPI - 1)

            passes(pe, body)


def project_out(nc, prefix, stream, ident, mixed, w_out, width):
    kts = width // P
    with Scope(nc, prefix) as s:
        w32 = s.sb("w32", [P, kts, DIM])
        w_hi, w_lo = s.sb("w_hi", [P, kts, DIM], F32R), s.sb("w_lo", [P, kts, DIM], F32R)
        source = s.sb("source", [P, 2, width])
        x_hi, x_lo = s.sb("x_hi", [P, 2, kts, P], F32R), s.sb("x_lo", [P, 2, kts, P], F32R)
        turned = [s.ps(f"turned{b}", [P, kts, P]) for b in range(2)]
        out_ps = [s.ps(f"out{b}", [P, DIM]) for b in range(2)]
        arrived, w_hi_done, w_lo_done = s.sem("arrived"), s.sem("w_hi_done"), s.sem("w_lo_done")
        source_done, turned_done = s.sem("source_done"), s.sem("turned_done")
        hi_done, lo_done, out_done, added = (s.sem(x) for x in ("hi_done", "lo_done", "out_done", "added"))
        block = s.block()

        @block.sync
        def _(sp):
            sp.dma_start(w32[:], w_out.rearrange("(k p) n -> p k n", p=P)).then_inc(arrived, 16)

        @block.gpsimd
        def _(pool):
            with pool.Fori(0, TILES // 2) as i:
                for b in range(2):
                    pool.wait_ge(turned_done, 2 * i + b + 1)
                    pool.tensor_copy(source[:, b, :], mixed[:, bass.ds(2 * i + b, 1), :]).then_inc(source_done, 1)

        @block.scalar
        def _(act):
            act.wait_ge(arrived, 16)
            act.copy(w_hi[:], w32[:]).then_inc(w_hi_done, 1)
            with act.Fori(0, TILES // 2) as i:
                for b in range(2):
                    act.wait_ge(turned_done, 2 * i + b + 3)
                    act.wait_ge(out_done, 2 * i + b + 1)
                    act.copy(x_hi[:, b], turned[b][:]).then_inc(hi_done, 1)

        @block.vector
        def _(dve):
            dve.wait_ge(w_hi_done, 1)
            dve.tensor_tensor(w_lo[:], w32[:], w_hi[:].bitcast(F32), ALU.subtract).then_inc(w_lo_done, 1)
            dve.sem_inc(lo_done, 2)
            dve.sem_inc(added, 2)
            with dve.Fori(0, TILES // 2) as i:
                for b in range(2):
                    dve.wait_ge(hi_done, 2 * i + b + 1)
                    dve.tensor_tensor(x_lo[:, b], turned[b][:], x_hi[:, b].bitcast(F32),
                                      ALU.subtract).then_inc(lo_done, 1)
                for b in range(2):
                    dve.wait_ge(out_done, 2 * i + b + 3)
                    tile = stream[:, bass.ds(2 * i + b, 1), :]
                    dve.tensor_tensor(tile, tile, out_ps[b][:], ALU.add).then_inc(added, 1)

        @block.tensor
        def _(pe):
            pe.sem_inc(turned_done, 2)
            pe.sem_inc(out_done, 2)
            pe.wait_ge(w_lo_done, 1)
            with pe.Fori(0, TILES // 2) as i:
                for b in range(2):
                    pe.wait_ge(source_done, 2 * i + b + 1)
                    pe.wait_ge(lo_done, 2 * i + b + 1)
                    for k in range(kts):
                        last = pe.transpose(turned[b][:, k, :], source[:, b, k * P:(k + 1) * P], ident[:])
                    last.then_inc(turned_done, 1)
                for b in range(2):
                    pe.wait_ge(lo_done, 2 * i + b + 3)
                    pe.wait_ge(added, 2 * i + b + 1)
                    for k in range(kts):
                        last = matmul3(pe, out_ps[b][:], x_hi[:, b, k, :], x_lo[:, b, k, :],
                                       w_hi[:, k, :], w_lo[:, k, :], k == 0, k == kts - 1)
                    last.then_inc(out_done, 1)


def latent_attention(nc, stream, ident, w_down, w_value, w_up, cos_sin, w_out):
    with Scope(nc, "la") as keep:
        lat_hi, lat_lo = keep.sb("lat_hi", [P, TOKENS], F32R), keep.sb("lat_lo", [P, TOKENS], F32R)
        with Scope(nc, "lav") as kv:
            values = kv.sb("values", [P, TILES, HEADS1, 2, HEAD_DIM1], F32R)
            with Scope(nc, "laf") as f:
                feat_hi, feat_lo = f.sb("feat_hi", [P, KT, TOKENS], F32R), f.sb("feat_lo", [P, KT, TOKENS], F32R)
                normalise(nc, "n1a", stream, ident, feat_hi, feat_lo, feature_tiles_plain)
                latents(nc, feat_hi, feat_lo, w_down, w_value, lat_hi, lat_lo, values)
            mixed = kv.sb("mixed", [P, TILES, DIM])
            softmax_heads(nc, ident, lat_hi, lat_lo, values, w_up, cos_sin, mixed)
            project_out(nc, "po1", stream, ident, mixed, w_out, DIM)


SPARSE_HIDDEN = 2048
SPARSE_GROUP = 4 * P
SPARSE_GROUPS = SPARSE_HIDDEN // SPARSE_GROUP


def sparse_feed_forward(nc, stream, feat_hi, feat_lo, weights):
    with Scope(nc, "sp") as s:
        WIDE = 4 * DIM
        staged = [s.sb(f"staged{b}", [P, WIDE]) for b in range(2)]
        w_hi = [s.sb(f"w_hi{q}", [P, WIDE], F32R) for q in range(3)]
        w_lo = [s.sb(f"w_lo{q}", [P, WIDE], F32R) for q in range(3)]
        silu = s.sb("silu", [P, 2, TB])
        hidden = s.sb("hidden", [P, 4, TB])
        size = s.sb("size", [P, 4, TB])
        beats = s.sb("beats", [P, 6, TB], BF16)
        wins = s.sb("wins", [P, 4, TB], BF16)
        h_hi = s.sb("h_hi", [P, 4, TB], F32R)
        h_lo = s.sb("h_lo", [P, 4, TB], F32R)
        gate_ps = [s.ps(f"gate{b}", [P, TB]) for b in range(2)]
        up_ps = [s.ps(f"up{b}", [P, TB]) for b in range(2)]
        down_ps = [s.ps(f"down{b}", [P, DIM]) for b in range(SUB)]

        arrived = [s.sem(f"arrived{q}") for q in range(3)]
        w_hi_done, w_lo_done = s.sem("w_hi_done"), s.sem("w_lo_done")
        gate_done, up_done = s.sem("gate_done"), s.sem("up_done")
        silu_done, product_done, size_done = s.sem("silu_done"), s.sem("product_done"), s.sem("size_done")
        beats_done, half_done, wins_done, kept = (s.sem(x) for x in ("beats_done", "half_done", "wins_done", "kept"))
        h_hi_done, h_lo_done = s.sem("h_hi_done"), s.sem("h_lo_done")
        down_done, added = s.sem("down_done"), s.sem("added")
        block = s.block()

        @block.sync
        def _(sp):
            def load(group, part, slot):
                sp.dma_start(staged[slot][:], weights[bass.ds(group, 1), part, :, :]
                             .rearrange("g p c -> (g p) c")).then_inc(arrived[part], 16)

            load(0, 0, 0)
            load(0, 1, 1)
            for g in range(SPARSE_GROUPS - 1):
                sp.wait_ge(w_lo_done, 3 * g + 1)
                load(g, 2, 0)
                sp.wait_ge(w_lo_done, 3 * g + 2)
                load(g + 1, 1, 1)
                sp.wait_ge(w_lo_done, 3 * g + 3)
                load(g + 1, 0, 0)
            sp.wait_ge(w_lo_done, 3 * (SPARSE_GROUPS - 1) + 1)
            load(SPARSE_GROUPS - 1, 2, 0)

        @block.vector
        def _(dve):
            dve.sem_inc(added, SUB)
            dve.sem_inc(product_done, 2)
            dve.sem_inc(h_lo_done, 1)

            def low_weights(g, part):
                dve.wait_ge(w_hi_done, 3 * g + part + 1)
                dve.tensor_tensor(w_lo[part][:], staged[part % 2][:], w_hi[part][:].bitcast(F32),
                                  ALU.subtract).then_inc(w_lo_done, 1)

            def add(n, tb):
                for j in range(SUB):
                    dve.wait_ge(down_done, SUB * (n + 1) + j + 1)
                    tile = stream[:, tb * SUB + j, :]
                    dve.tensor_tensor(tile, tile, down_ps[j][:], ALU.add).then_inc(added, 1)

            def body(g, first, last):
                for tb in range(BLOCKS):
                    n = BLOCKS * g + tb
                    dve.wait_ge(h_lo_done, n + 1)
                    for r in range(4):
                        dve.wait_ge(up_done, 4 * n + r + 1)
                        dve.wait_ge(silu_done, 4 * n + r + 1)
                        dve.tensor_tensor(hidden[:, r, :], silu[:, r % 2, :], up_ps[r % 2][:],
                                          ALU.mult).then_inc(product_done, 1)
                    if tb == BLOCKS - 1 and not last:
                        low_weights(g + 1, 0)
                        low_weights(g + 1, 1)
                    dve.wait_ge(size_done, 4 * n + 4)
                    for a, at in ((0, 0), (1, 3), (2, 5)):
                        count = 3 - a
                        dve.tensor_tensor(beats[:, at:at + count, :],
                                          size[:, a:a + 1, :].broadcast_to([P, count, TB]),
                                          size[:, a + 1:4, :], ALU.is_ge).then_inc(beats_done, 1)
                    dve.wait_ge(beats_done, 3 * n + 3)
                    for r, (x, y, op) in enumerate(((0, 1, ALU.add), (3, 4, ALU.add), (5, 1, ALU.subtract),
                                                    (2, 4, ALU.add))):
                        dve.tensor_tensor(wins[:, r, :], beats[:, x, :], beats[:, y, :], op).then_inc(half_done, 1)
                    for r, (x, op) in enumerate(((2, ALU.add), (0, ALU.subtract), (3, ALU.subtract), (5, ALU.add))):
                        dve.wait_ge(half_done, 4 * n + r + 1)
                        dve.tensor_tensor(wins[:, r, :], wins[:, r, :], beats[:, x, :], op).then_inc(wins_done, 1)
                    for r, (limit, op) in enumerate(((2.0, ALU.is_ge), (1.0, ALU.is_ge), (0.0, ALU.is_ge),
                                                     (1.0, ALU.is_le))):
                        dve.wait_ge(wins_done, 4 * n + r + 1)
                        dve.scalar_tensor_tensor(out=hidden[:, r, :], in0=wins[:, r, :], scalar=limit,
                                                 in1=hidden[:, r, :], op0=op, op1=ALU.mult).then_inc(kept, 1)
                    if not (first and tb == 0):
                        add(n - 1, (tb - 1) % BLOCKS)
                    if tb == 0:
                        low_weights(g, 2)
                    dve.wait_ge(h_hi_done, n + 1)
                    dve.tensor_tensor(h_lo[:], hidden[:], h_hi[:].bitcast(F32), ALU.subtract).then_inc(h_lo_done, 1)

            low_weights(0, 0)
            low_weights(0, 1)
            body(0, True, False)
            with dve.Fori(1, SPARSE_GROUPS - 1) as g:
                body(g, False, False)
            body(SPARSE_GROUPS - 1, False, True)
            add(SPARSE_GROUPS * BLOCKS - 1, BLOCKS - 1)

        @block.scalar
        def _(act):
            act.preload_act_table(ACT.Silu)

            def high_weights(g, part):
                act.wait_ge(arrived[part], 16 * g + 16)
                act.copy(w_hi[part][:], staged[part % 2][:]).then_inc(w_hi_done, 1)

            def body(g, last):
                for tb in range(BLOCKS):
                    n = BLOCKS * g + tb

                    def magnitude(r):
                        act.wait_ge(product_done, 4 * n + r + 3)
                        act.activation(size[:, r, :], hidden[:, r, :], ACT.Abs).then_inc(size_done, 1)

                    for r in range(4):
                        act.wait_ge(gate_done, 4 * n + r + 1)
                        act.wait_ge(product_done, 4 * n + r + 1)
                        act.activation(silu[:, r % 2, :], gate_ps[r % 2][:], ACT.Silu).then_inc(silu_done, 1)
                        if r:
                            magnitude(r - 1)
                    magnitude(3)
                    if tb == BLOCKS - 1 and not last:
                        act.wait_ge(up_done, 4 * n + 4)
                        high_weights(g + 1, 0)
                        high_weights(g + 1, 1)
                    act.wait_ge(down_done, SUB * (n + 1))
                    if tb == 0:
                        high_weights(g, 2)
                    act.wait_ge(kept, 4 * n + 4)
                    act.copy(h_hi[:], hidden[:]).then_inc(h_hi_done, 1)

            high_weights(0, 0)
            high_weights(0, 1)
            with act.Fori(0, SPARSE_GROUPS - 1) as g:
                body(g, False)
            body(SPARSE_GROUPS - 1, True)

        @block.tensor
        def _(pe):
            pe.sem_inc(down_done, SUB)

            def gate_up(n, g, tb):
                pe.wait_ge(w_hi_done, 3 * g + 2)
                pe.wait_ge(w_lo_done, 3 * g + 2)
                cols = slice(tb * TB, (tb + 1) * TB)
                for r in range(4):
                    for part, ps in ((0, gate_ps[r % 2]), (1, up_ps[r % 2])):
                        if part == 0 and not (isinstance(n, int) and 4 * n + r < 2):
                            pe.wait_ge(silu_done, 4 * n + r - 1)
                        if part == 1:
                            pe.wait_ge(product_done, 4 * n + r + 1)
                        for kt in range(KT):
                            at = kt * DIM + r * P
                            last = matmul3(pe, ps[:], w_hi[part][:, at:at + P], w_lo[part][:, at:at + P],
                                           feat_hi[:, kt, cols], feat_lo[:, kt, cols], kt == 0, kt == KT - 1)
                        last.then_inc((gate_done, up_done)[part], 1)

            def down(n, g, tb):
                if tb == 0:
                    pe.wait_ge(w_lo_done, 3 * g + 3)
                pe.wait_ge(h_lo_done, n + 2)
                for j in range(SUB):
                    pe.wait_ge(added, SUB * n + j + 1)
                    rows = slice(j * P, (j + 1) * P)
                    for r in range(4):
                        at = slice(r * DIM, (r + 1) * DIM)
                        last = matmul3(pe, down_ps[j][:], h_hi[:, r, rows], h_lo[:, r, rows],
                                       w_hi[2][:, at], w_lo[2][:, at], r == 0, r == 3)
                    last.then_inc(down_done, 1)

            def body(g, last):
                for tb in range(BLOCKS):
                    n = BLOCKS * g + tb
                    nxt = tb + 1
                    if not (last and nxt == BLOCKS):
                        gate_up(n + 1, g + nxt // BLOCKS, nxt % BLOCKS)
                    down(n, g, tb)

            gate_up(0, 0, 0)
            with pe.Fori(0, SPARSE_GROUPS - 1) as g:
                body(g, False)
            body(SPARSE_GROUPS - 1, True)


def four_sublayers(nc, hidden, ident_in, masks_in, w_qkv, conv_w, w_gate, head_rows, w_out0, codes, scales,
                   w_down1, w_value1, w_up1, cos_sin, w_out1, w_sparse, out):
    with Scope(nc, "k") as s:
        stream = s.sb("stream", [P, TILES, DIM])
        ident = s.sb("ident", [P, P])
        arrived, stored = s.sem("arrived"), s.sem("stored")
        with Scope(nc, "l0") as l0:
            mask = l0.sb("mask", [P, N_MASKS, P])
            with nc.Block() as block:
                @block.sync
                def _(sp):
                    sp.dma_start(stream[:], hidden.rearrange("(i p) d -> p i d", p=P)).then_inc(arrived, 16)
                    sp.dma_start(ident[:], ident_in).then_inc(arrived, 16)
                    sp.dma_start(mask[:], masks_in).then_inc(arrived, 16)
                    sp.wait_ge(arrived, 48)
            delta_attention(nc, stream, ident, mask, hidden, w_qkv, conv_w, w_gate, head_rows, w_out0)
        with Scope(nc, "f0") as f:
            feat_hi, feat_lo = f.sb("feat_hi", [P, KT, TOKENS], F32R), f.sb("feat_lo", [P, KT, TOKENS], F32R)
            normalise(nc, "n0f", stream, ident, feat_hi, feat_lo, feature_tiles_nibbles)
            nvfp4_feed_forward(nc, stream, feat_hi, feat_lo, codes, scales)
        latent_attention(nc, stream, ident, w_down1, w_value1, w_up1, cos_sin, w_out1)
        with Scope(nc, "f1") as f:
            feat_hi, feat_lo = f.sb("feat_hi", [P, KT, TOKENS], F32R), f.sb("feat_lo", [P, KT, TOKENS], F32R)
            normalise(nc, "n1f", stream, ident, feat_hi, feat_lo, feature_tiles_plain)
            sparse_feed_forward(nc, stream, feat_hi, feat_lo, w_sparse)
        with nc.Block() as block:
            @block.sync
            def _(sp):
                sp.dma_start(out.rearrange("(i p) d -> p i d", p=P), stream[:]).then_inc(stored, 16)
                sp.wait_ge(stored, 16)


def rotary_tables():
    inverse = (1.0 / 10000.0 ** (np.arange(0, HALF, 2, dtype=np.float32) / HALF)).astype(np.float32)
    angle = (np.arange(SEQ, dtype=np.float32)[:, None] * inverse[None]).astype(np.float32)
    angle = np.concatenate([angle, angle], -1).T
    sign = np.where(np.arange(HALF) < HALF // 2, -1, 1)[:, None]
    table = np.stack([np.tile(np.cos(angle), (P // HALF, 1)), np.tile(np.sin(angle) * sign, (P // HALF, 1))], 1)
    table = table.astype(np.float32)
    table[:P // 2] *= HALF ** -0.5
    return np.ascontiguousarray(table)


def delta_layout(x):
    names = "qkv"
    w = np.stack([x[f"L0_attn_W{n}"] for n in names]).reshape(3, CT, P, KT, P)
    conv = np.stack([x[f"L0_attn_conv_{n}"] for n in names]).reshape(3, CT, P, CONV)
    gate = np.concatenate([x["L0_attn_Wg"].T, x["L0_attn_Wb"].T, x["L0_attn_Wa"].T], 1)
    return (w.transpose(1, 0, 4, 3, 2).reshape(CT, 3, P, KT * P), conv.transpose(2, 1, 0, 3).reshape(P, CT, 3 * CONV),
            gate.reshape(KT, P, GATE_COLS),
            np.concatenate([np.tile(x["L0_attn_o_norm_w"], HEADS0), x["L0_attn_dt_bias"], x["L0_attn_A_log"]]),
            x["L0_attn_Wo"].T)


def nvfp4_layout(x):
    def rows(a):
        inner = a.shape[1] // 2
        a = a.reshape(FP4_GROUPS, P, 2, 2, inner)
        return a.transpose(0, 4, 3, 2, 1).reshape(FP4_GROUPS, inner, 2 * FP4_GROUP)

    def down(a):
        return a.T.reshape(FP4_GROUPS, a.shape[1] // FP4_GROUPS, DIM)

    return tuple(np.concatenate([rows(x[f"L0_ffn_gate_{n}"]), rows(x[f"L0_ffn_up_{n}"]), down(x[f"L0_ffn_down_{n}"])], 2)
                 for n in ("W_packed", "scales"))


def latent_up_layout(x):
    swapped = [(d + HALF // 2) % HALF for d in range(HALF)]
    up = np.zeros((P, QUADS, 2, P), np.float32)
    for side, name in enumerate(("L1_attn_wq_u", "L1_attn_wk_u")):
        w = x[name].reshape(LATENT, QUADS, QUAD, HALF)
        at = slice(side * LATENT, (side + 1) * LATENT)
        for which, cols in enumerate((w, w[..., swapped])):
            up[at, :, which, at] = cols.reshape(LATENT, QUADS, QUAD * HALF)
    return up.reshape(P, QUADS, 2 * P).transpose(1, 0, 2)


def sparse_layout(x):
    def into(w):
        w = w.reshape(KT, P, SPARSE_GROUPS, P, 4)
        return w.transpose(2, 1, 0, 4, 3).reshape(SPARSE_GROUPS, 1, P, 4 * DIM)
    down = x["L1_ffn_w_down"].reshape(SPARSE_GROUPS, 1, P, 4 * DIM)
    return np.concatenate([into(x["L1_ffn_w_gate"]), into(x["L1_ffn_w_up"]), down], 1)


def kernel(**inputs):
    import concourse.bacc as bacc
    from concourse.bass_utils import run_bass_kernel_spmd

    x = {name: np.asarray(a) for name, a in inputs.items()}
    w_qkv, conv_w, w_gate, head_rows, w_out0 = delta_layout(x)
    codes, scales = nvfp4_layout(x)
    arrays = {
        "hidden": x["L0_attn_hidden_states"].reshape(TOKENS, DIM),
        "ident_in": np.eye(P, dtype=np.float32), "masks_in": masks(),
        "w_qkv": w_qkv, "conv_w": conv_w, "w_gate": w_gate, "head_rows": head_rows, "w_out0": w_out0,
        "codes": codes, "scales": scales,
        "w_down1": np.concatenate([x["L1_attn_wq_d"], x["L1_attn_wkv_d"]], 1), "w_value1": x["L1_attn_wv_u"],
        "w_up1": latent_up_layout(x), "cos_sin": rotary_tables(), "w_out1": x["L1_attn_wo"],
        "w_sparse": sparse_layout(x),
    }
    arrays = {name: np.ascontiguousarray(a) for name, a in arrays.items()}
    nc = bacc.Bacc("TRN2", target_bir_lowering=False, num_devices=1)
    args = {name: nc.dram_tensor(name, a.shape, mybir.dt.from_np(a.dtype), kind="ExternalInput").ap()
            for name, a in arrays.items()}
    out = nc.dram_tensor("out", (TOKENS, DIM), F32, kind="ExternalOutput").ap()
    four_sublayers(nc, out=out, **args)
    result = run_bass_kernel_spmd(nc, [arrays], core_ids=[0])
    return result.results[0]["out"].reshape(BATCH, SEQ, DIM)
```

```python
from contextlib import ExitStack

import numpy as np
import concourse.bass as bass
from concourse import mybir

F32 = mybir.dt.float32
F32R = mybir.dt.float32r
F16 = mybir.dt.float16
BF16 = mybir.dt.bfloat16
I32 = mybir.dt.int32
ALU = mybir.AluOpType
ACT = mybir.ActivationFunctionType
AX = mybir.AxisListType

P = 128
BATCH, SEQ, DIM = 2, 1024, 512
TOKENS = BATCH * SEQ
TILES = TOKENS // P
KT = DIM // P
TB = 512
BLOCKS = TOKENS // TB
SUB = TB // P
EPS = 1e-5


class Scope:

    def __init__(self, nc, prefix):
        self.nc, self.prefix, self.stack, self.sems = nc, prefix, ExitStack(), []

    def __enter__(self):
        self.stack.__enter__()
        return self

    def __exit__(self, *a):
        self.stack.__exit__(*a)
        if self.sems:
            self.nc.clear_and_free_semaphores(self.sems)
            self.nc.all_engine_barrier()

    def sb(self, name, shape, dt=F32):
        return self.stack.enter_context(self.nc.sbuf_tensor(f"{self.prefix}_{name}", shape, dt))

    def ps(self, name, shape, dt=F32):
        return self.stack.enter_context(self.nc.psum_tensor(f"{self.prefix}_{name}", shape, dt))

    def sem(self, name):
        self.sems.append(self.nc.alloc_semaphore(name=f"{self.prefix}_{name}"))
        return self.sems[-1]

    def block(self):
        return self.stack.enter_context(self.nc.Block())


def matmul3(pe, out, w_hi, w_lo, x_hi, x_lo, start, stop):
    pe.matmul(out, w_hi, x_hi, start=start, stop=False)
    pe.matmul(out, w_hi, x_lo, start=False, stop=False)
    return pe.matmul(out, w_lo, x_hi, start=False, stop=stop)


def feature_tiles_plain(kt):
    return slice(kt * P, (kt + 1) * P)


def feature_tiles_nibbles(kt):
    return slice(2 * P * (kt // 2) + kt % 2, 2 * P * (kt // 2 + 1), 2)


def normalise(nc, prefix, stream, ident, feat_hi, feat_lo, feature_tiles):
    with Scope(nc, prefix) as s:
        raw = s.sb("raw_stats", [P, TILES, 6])
        mean, gap, var = (s.sb(x, [P, TILES]) for x in ("mean", "gap", "var"))
        power = s.sb("power", [P, TILES])
        rstd = s.sb("rstd", [P, TILES])
        normed = s.sb("normed", [P, 2, DIM])
        turned = [s.ps(f"turned{b}", [P, KT, P]) for b in range(2)]
        stats_done, moments, rstd_done = s.sem("stats_done"), s.sem("moments"), s.sem("rstd_done")
        const_ready = s.sem("const_ready")
        normed_done, turned_done = s.sem("normed_done"), s.sem("turned_done")
        hi_done, lo_done = s.sem("hi_done"), s.sem("lo_done")
        block = s.block()

        @block.gpsimd
        def _(pool):
            pool.memset(power[:], -0.5).then_inc(const_ready, 1)
            pool.wait_ge(const_ready, 1)
            pool.wait_ge(moments, 7)
            pool.tensor_tensor(rstd[:], var[:], power[:], ALU.pow).then_inc(rstd_done, 1)

        @block.vector
        def _(dve):
            with dve.Fori(0, TILES) as i:
                dve.bn_stats(raw[:, bass.ds(i, 1), :], stream[:, bass.ds(i, 1), :]).then_inc(stats_done, 1)
            dve.wait_ge(stats_done, TILES)
            dve.tensor_tensor(mean[:], raw[:, :, 1], raw[:, :, 4], ALU.add).then_inc(moments, 1)
            dve.tensor_tensor(gap[:], raw[:, :, 1], raw[:, :, 4], ALU.subtract).then_inc(moments, 1)
            dve.tensor_tensor(var[:], raw[:, :, 2], raw[:, :, 5], ALU.add).then_inc(moments, 1)
            dve.wait_ge(moments, 3)
            dve.tensor_scalar(mean[:], mean[:], 0.5, None, ALU.mult).then_inc(moments, 1)
            dve.scalar_tensor_tensor(out=gap[:], in0=gap[:], scalar=0.25, in1=gap[:],
                                     op0=ALU.mult, op1=ALU.mult).then_inc(moments, 1)
            dve.tensor_scalar(var[:], var[:], 1.0 / DIM, EPS, ALU.mult, ALU.add).then_inc(moments, 1)
            dve.wait_ge(moments, 6)
            dve.tensor_tensor(var[:], var[:], gap[:], ALU.add).then_inc(moments, 1)
            dve.wait_ge(rstd_done, 1)
            dve.sem_inc(lo_done, 2)

            def scale(i, b):
                dve.wait_ge(turned_done, i + 1)
                dve.tensor_scalar(normed[:, b, :], stream[:, bass.ds(i, 1), :],
                                  mean[:, bass.ds(i, 1)], rstd[:, bass.ds(i, 1)],
                                  ALU.subtract, ALU.mult).then_inc(normed_done, 1)

            def low(i, b):
                dve.wait_ge(hi_done, i + 1)
                cols = bass.ts(i, P)
                dve.tensor_tensor(feat_lo[:, :, cols], turned[b][:], feat_hi[:, :, cols].bitcast(F32),
                                  ALU.subtract).then_inc(lo_done, 1)

            with dve.Fori(0, TILES // 2) as i:
                for b in range(2):
                    scale(2 * i + b, b)
                for b in range(2):
                    low(2 * i + b, b)

        @block.tensor
        def _(pe):
            pe.sem_inc(turned_done, 2)
            with pe.Fori(0, TILES // 2) as i:
                for b in range(2):
                    pe.wait_ge(normed_done, 2 * i + b + 1)
                    pe.wait_ge(lo_done, 2 * i + b + 1)
                    for kt in range(KT):
                        last = pe.transpose(turned[b][:, kt, :], normed[:, b, feature_tiles(kt)], ident[:])
                    last.then_inc(turned_done, 1)

        @block.scalar
        def _(act):
            with act.Fori(0, TILES // 2) as i:
                for b in range(2):
                    act.wait_ge(turned_done, 2 * i + b + 3)
                    act.copy(feat_hi[:, :, bass.ts(2 * i + b, P)], turned[b][:]).then_inc(hi_done, 1)


FP4_GROUP = 2 * P
FP4_HIDDEN = 4096
FP4_GROUPS = FP4_HIDDEN // FP4_GROUP
FP4_BLOCK = 32
FP4_COLS = 2 * 2 * FP4_GROUP + DIM


def nvfp4_feed_forward(nc, stream, feat_hi, feat_lo, codes, scales):
    with Scope(nc, "fp4") as s:
        words = s.sb("words", [P, FP4_COLS], I32)
        scale = s.sb("scale", [P, FP4_COLS])
        bits = s.sb("bits", [P, FP4_COLS], I32)
        weight = s.sb("weight", [P, 2, FP4_COLS])
        w_hi = [s.sb(f"w_hi{b}", [P, 2, FP4_COLS], F32R) for b in range(2)]
        w_lo = [s.sb(f"w_lo{b}", [P, 2, FP4_COLS], F32R) for b in range(2)]
        gelu = s.sb("gelu", [P, 2, TB])
        hidden = s.sb("hidden", [P, 2, TB])
        h_hi = s.sb("h_hi", [P, 2, 2, TB], F32R)
        h_lo = s.sb("h_lo", [P, 2, 2, TB], F32R)
        gate_ps = [s.ps(f"gate{b}", [P, TB]) for b in range(2)]
        up_ps = [s.ps(f"up{b}", [P, TB]) for b in range(2)]
        down_ps = [s.ps(f"down{b}", [P, DIM]) for b in range(SUB)]

        loaded = s.sem("loaded")
        dve_step = s.sem("dve_step")
        w_hi_done, w_lo_done = s.sem("w_hi_done"), s.sem("w_lo_done")
        gate_done, up_done = s.sem("gate_done"), s.sem("up_done")
        gelu_done, product_done = s.sem("gelu_done"), s.sem("product_done")
        h_hi_done, h_lo_done = s.sem("h_hi_done"), s.sem("h_lo_done")
        down_done, added = s.sem("down_done"), s.sem("added")
        block = s.block()
        LOOPS = FP4_GROUPS // 2
        STEPS = 2 * BLOCKS

        @block.sync
        def _(sp):
            def load(group):
                sp.dma_start(words[:], codes[bass.ds(group, 1), :, :].rearrange("g p c -> (g p) c")).then_inc(loaded, 16)
                src = scales[bass.ds(group, 1), :, :]
                rows = bass.AP(tensor=src.tensor, offset=src.offset,
                               ap=[[FP4_COLS, P // 16], [0, 16], [1, FP4_COLS]])
                sp.dma_start(scale[:], rows).then_inc(loaded, 16)

            load(0)
            with sp.Fori(0, FP4_GROUPS - 1) as group:
                sp.wait_ge(dve_step, 6 * group + 7)
                load(group + 1)

        def bits_of(dve, nibble, n):
            dve.wait_ge(dve_step, 3 * n + 1)
            dve.tensor_scalar(bits[:], words[:], 28 - 4 * nibble, 3,
                              ALU.logical_shift_left, ALU.arith_shift_right).then_inc(dve_step, 1)
            dve.wait_ge(dve_step, 3 * n + 2)
            dve.tensor_scalar(bits[:], bits[:], 0x8E000000 - (1 << 32), None,
                              ALU.bitwise_and).then_inc(dve_step, 1)
            dve.wait_ge(dve_step, 3 * n + 3)
            dve.wait_ge(w_lo_done, n + 1)
            dve.scalar_tensor_tensor(out=weight[:, nibble, :], in0=bits[:].bitcast(F16)[:, 1::2],
                                     scalar=16384.0, in1=scale[:], op0=ALU.mult,
                                     op1=ALU.mult).then_inc(dve_step, 1)

        def low_weights(dve, group, b, nibble):
            n = 2 * group + nibble
            dve.wait_ge(w_hi_done, n + 3)
            dve.tensor_tensor(w_lo[b][:, nibble, :], weight[:, nibble, :],
                              w_hi[b][:, nibble, :].bitcast(F32), ALU.subtract).then_inc(w_lo_done, 1)

        @block.vector
        def _(dve):
            dve.sem_inc(dve_step, 1)
            dve.sem_inc(added, SUB)
            dve.sem_inc(product_done, 2)
            dve.sem_inc(h_lo_done, 2)
            dve.sem_inc(w_lo_done, 2)

            def prepare(group, nibble):
                if nibble == 0:
                    dve.wait_ge(loaded, 32 * group + 32)
                bits_of(dve, nibble, 2 * group + nibble)

            def add(n, tb):
                for j in range(SUB):
                    dve.wait_ge(down_done, SUB * (n + 2) + j + 1)
                    tile = stream[:, tb * SUB + j, :]
                    dve.tensor_tensor(tile, tile, down_ps[j][:], ALU.add).then_inc(added, 1)

            def body(it, first, last):
                for t in range(STEPS):
                    n = STEPS * it + t
                    b, tb = t // BLOCKS, t % BLOCKS
                    for c in range(2):
                        chunk = 2 * n + c
                        dve.wait_ge(up_done, chunk + 1)
                        dve.wait_ge(gelu_done, chunk + 1)
                        dve.wait_ge(h_lo_done, chunk + 1)
                        dve.tensor_tensor(hidden[:, c, :], gelu[:, c, :], up_ps[c][:],
                                          ALU.mult).then_inc(product_done, 1)
                    for c in range(2):
                        chunk = 2 * n + c
                        dve.wait_ge(h_hi_done, chunk + 3)
                        dve.tensor_tensor(h_lo[:, t % 2, c, :], hidden[:, c, :],
                                          h_hi[:, t % 2, c, :].bitcast(F32), ALU.subtract).then_inc(h_lo_done, 1)
                    if not (first and t == 0):
                        add(n - 1, (tb - 1) % BLOCKS)
                    if not (last and b == 1):
                        group = 2 * it + b + 1
                        if tb == 1:
                            dve.wait_ge(down_done, SUB * (2 + STEPS * it + BLOCKS * b))
                            prepare(group, 0)
                        if tb == 2:
                            low_weights(dve, group, 1 - b, 0)
                            prepare(group, 1)
                        if tb == 3:
                            low_weights(dve, group, 1 - b, 1)

            for nibble in range(2):
                prepare(0, nibble)
                low_weights(dve, 0, 0, nibble)
            body(0, True, False)
            with dve.Fori(1, LOOPS - 1) as it:
                body(it, False, False)
            body(LOOPS - 1, False, True)
            add(STEPS * LOOPS - 1, BLOCKS - 1)

        @block.scalar
        def _(act):
            act.preload_act_table(ACT.Gelu_apprx_tanh)
            act.sem_inc(w_hi_done, 2)
            act.sem_inc(h_hi_done, 2)

            def high_weights(group, b, nibble):
                n = 2 * group + nibble
                act.wait_ge(dve_step, 3 * n + 4)
                act.copy(w_hi[b][:, nibble, :], weight[:, nibble, :]).then_inc(w_hi_done, 1)

            def body(it, last):
                for t in range(STEPS):
                    n = STEPS * it + t
                    b, tb = t // BLOCKS, t % BLOCKS
                    for c in range(2):
                        chunk = 2 * n + c
                        act.wait_ge(gate_done, chunk + 1)
                        act.wait_ge(product_done, chunk + 1)
                        act.activation(gelu[:, c, :], gate_ps[c][:], ACT.Gelu_apprx_tanh).then_inc(gelu_done, 1)
                    for c in range(2):
                        chunk = 2 * n + c
                        act.wait_ge(product_done, chunk + 3)
                        act.wait_ge(down_done, SUB * (n + 1))
                        act.copy(h_hi[:, t % 2, c, :], hidden[:, c, :]).then_inc(h_hi_done, 1)
                    if not (last and b == 1) and tb in (1, 2):
                        high_weights(2 * it + b + 1, 1 - b, tb - 1)

            high_weights(0, 0, 0)
            high_weights(0, 0, 1)
            with act.Fori(0, LOOPS - 1) as it:
                body(it, False)
            body(LOOPS - 1, True)

        @block.tensor
        def _(pe):
            pe.sem_inc(down_done, 2 * SUB)

            def gate_up(n, group, b, tb):
                pe.wait_ge(w_hi_done, 2 * group + 4)
                pe.wait_ge(w_lo_done, 2 * group + 4)
                cols = slice(tb * TB, (tb + 1) * TB)
                for c in range(2):
                    for part, ps in ((0, gate_ps[c]), (1, up_ps[c])):
                        if part == 0 and not (isinstance(n, int) and n == 0):
                            pe.wait_ge(gelu_done, 2 * n + c - 1)
                        if part == 1:
                            pe.wait_ge(product_done, 2 * n + c + 1)
                        for kt in range(KT):
                            at = part * 2 * FP4_GROUP + (kt // 2) * FP4_GROUP + c * P
                            last = matmul3(pe, ps[:], w_hi[b][:, kt % 2, at:at + P], w_lo[b][:, kt % 2, at:at + P],
                                           feat_hi[:, kt, cols], feat_lo[:, kt, cols], kt == 0, kt == KT - 1)
                        last.then_inc((gate_done, up_done)[part], 1)

            def down(n, b, t):
                pe.wait_ge(h_hi_done, 2 * n + 4)
                pe.wait_ge(h_lo_done, 2 * n + 4)
                for j in range(SUB):
                    pe.wait_ge(added, SUB * n + j + 1)
                    rows = slice(j * P, (j + 1) * P)
                    for c in range(2):
                        last = matmul3(pe, down_ps[j][:], h_hi[:, t % 2, c, rows], h_lo[:, t % 2, c, rows],
                                       w_hi[b][:, c, 4 * FP4_GROUP:], w_lo[b][:, c, 4 * FP4_GROUP:],
                                       c == 0, c == 1)
                    last.then_inc(down_done, 1)

            def body(it, last):
                for t in range(STEPS):
                    n = STEPS * it + t
                    if not (last and t == STEPS - 1):
                        nxt = t + 1
                        gate_up(n + 1, 2 * it + nxt // BLOCKS, (nxt // BLOCKS) % 2, nxt % BLOCKS)
                    down(n, t // BLOCKS, t)

            gate_up(0, 0, 0, 0)
            with pe.Fori(0, LOOPS - 1) as it:
                body(it, False)
            body(LOOPS - 1, True)


HEADS0, HEAD_DIM0, CONV = 6, 64, 4
KEY = HEADS0 * HEAD_DIM0
CT = KEY // P
CHUNK = P
CHUNKS = SEQ // CHUNK
BH = BATCH * HEADS0
LOGITS = 2 * HEADS0
GATE_COLS = KEY + LOGITS
LEVELS = 6


def masks():
    r, c = np.arange(P)[:, None], np.arange(P)[None, :]
    below = [-((r // n % 2 == 1) & (c // n == r // n - 1)).astype(np.float32) for n in (1, 2, 4, 8, 16, 32, 64)]
    out = [r <= c, r > c, np.ones((P, P)), r < c, below[0].T] + below[1:]
    return np.ascontiguousarray(np.stack([np.asarray(m, np.float32) for m in out], 1))


UPTO, AFTER, ONES, BEFORE, PAIR_T, LEVEL0 = range(6)
N_MASKS = LEVEL0 + LEVELS


def project_conv(nc, feat_hi, feat_lo, w_qkv, conv_w, qkv):
    with Scope(nc, "pc") as s:
        taps = s.sb("taps", [P, CT * 3 * CONV])
        w32 = [s.sb(f"w32_{q}", [P, KT * P]) for q in range(3)]
        w_hi = [s.sb(f"w_hi{q}", [P, KT * P], F32R) for q in range(3)]
        w_lo = [s.sb(f"w_lo{q}", [P, KT * P], F32R) for q in range(3)]
        padded = s.sb("padded", [P, BATCH, CONV - 1 + SEQ])
        banks = [s.ps(f"bank{b}", [P, TB]) for b in range(BLOCKS)]
        arrived_w = [s.sem(f"arrived_w{q}") for q in range(3)]
        arrived = s.sem("arrived")
        zeroed = s.sem("zeroed")
        w_hi_done, w_lo_done = s.sem("w_hi_done"), s.sem("w_lo_done")
        product_done, copied = s.sem("product_done"), s.sem("copied")
        taps_done, silu_done = s.sem("taps_done"), s.sem("silu_done")
        block = s.block()

        @block.sync
        def _(sp):
            sp.dma_start(taps[:], conv_w.rearrange("p i t -> p (i t)")).then_inc(arrived, 16)
            for tile in range(CT):
                for q in range(3):
                    if tile:
                        sp.wait_ge(w_lo_done, 3 * (tile - 1) + q + 1)
                    sp.dma_start(w32[q][:], w_qkv[tile, q]).then_inc(arrived_w[q], 16)

        @block.gpsimd
        def _(pool):
            pool.memset(padded[:, :, 0:CONV - 1], 0.0).then_inc(zeroed, 1)

        @block.scalar
        def _(act):
            act.preload_act_table(ACT.Silu)
            act.sem_inc(copied, BLOCKS)

            def high_weights(tile, q):
                act.wait_ge(arrived_w[q], 16 * tile + 16)
                act.wait_ge(product_done, 4 * (3 * tile + q) + 4)
                act.copy(w_hi[q][:], w32[q][:]).then_inc(w_hi_done, 1)

            def body(tile, last):
                for q in range(3):
                    n = 3 * tile + q
                    if not (last and q == 2):
                        high_weights(tile + (q == 2), (q + 1) % 3)
                    act.wait_ge(taps_done, 4 * n + 4)
                    for blk in range(BLOCKS):
                        act.wait_ge(product_done, 4 * n + blk + 13)
                        b, half = divmod(blk, SEQ // TB)
                        at = CONV - 1 + half * TB
                        act.copy(padded[:, b, at:at + TB], banks[blk][:]).then_inc(copied, 1)
                    act.wait_ge(taps_done, 4 * n + 8)
                    row = qkv[:, bass.ds(3 * q + tile, 1), :]
                    act.activation(row, row, ACT.Silu).then_inc(silu_done, 1)

            high_weights(0, 0)
            with act.Fori(0, CT - 1) as tile:
                body(tile, False)
            body(CT - 1, True)

        @block.vector
        def _(dve):
            dve.sem_inc(taps_done, 4)
            dve.wait_ge(arrived, 16)
            dve.wait_ge(zeroed, 1)

            def low_weights(tile, q):
                dve.wait_ge(w_hi_done, 3 * tile + q + 1)
                dve.tensor_tensor(w_lo[q][:], w32[q][:], w_hi[q][:].bitcast(F32),
                                  ALU.subtract).then_inc(w_lo_done, 1)

            def body(tile, last):
                for q in range(3):
                    n = 3 * tile + q
                    if not (last and q == 2):
                        low_weights(tile + (q == 2), (q + 1) % 3)
                    dve.wait_ge(copied, 4 * n + 8)
                    row = qkv[:, bass.ds(3 * q + tile, 1), :].rearrange("p o (b t) -> p (o b) t", b=BATCH)
                    for i in range(CONV):
                        at = 3 * CONV * tile + CONV * q + i
                        tap = taps[:, bass.ds(at, 1)]
                        src = padded[:, :, i:i + SEQ]
                        if i == 0:
                            dve.tensor_scalar(row, src, tap, None, ALU.mult).then_inc(taps_done, 1)
                        else:
                            dve.wait_ge(taps_done, 4 * n + 4 + i)
                            dve.scalar_tensor_tensor(out=row, in0=src, scalar=tap, in1=row,
                                                     op0=ALU.mult, op1=ALU.add).then_inc(taps_done, 1)

            low_weights(0, 0)
            with dve.Fori(0, CT - 1) as tile:
                body(tile, False)
            body(CT - 1, True)

        @block.tensor
        def _(pe):
            pe.sem_inc(product_done, 12)
            with pe.Fori(0, CT) as tile:
                for q in range(3):
                    n = 3 * tile + q
                    pe.wait_ge(w_lo_done, n + 1)
                    for blk in range(BLOCKS):
                        pe.wait_ge(copied, 4 * n + blk + 1)
                        cols = slice(blk * TB, (blk + 1) * TB)
                        for kt in range(KT):
                            at = slice(kt * P, (kt + 1) * P)
                            last = matmul3(pe, banks[blk][:], w_hi[q][:, at], w_lo[q][:, at],
                                           feat_hi[:, kt, cols], feat_lo[:, kt, cols], kt == 0, kt == KT - 1)
                        last.then_inc(product_done, 1)


def gates_and_decays(nc, feat_hi, feat_lo, w_gate, head_rows, gate, beta, decay):
    with Scope(nc, "gd") as s:
        w32 = s.sb("w32", [P, KT, GATE_COLS])
        w_hi, w_lo = s.sb("w_hi", [P, KT, GATE_COLS], F32R), s.sb("w_lo", [P, KT, GATE_COLS], F32R)
        rows = s.sb("rows", [P, KEY + 2 * HEADS0])
        tile_hi, tile_lo = s.sb("tile_hi", [P, 2, KT, P], F32R), s.sb("tile_lo", [P, 2, KT, P], F32R)
        logits = s.sb("logits", [P, TILES, LOGITS])
        soft = s.sb("soft", [P, TILES, HEADS0])
        rate = s.sb("rate", [P, HEADS0])
        banks = [s.ps(f"bank{b}", [P, GATE_COLS]) for b in range(2)]
        arrived = s.sem("arrived")
        w_hi_done, w_lo_done = s.sem("w_hi_done"), s.sem("w_lo_done")
        tiled, product_done, silu_done, logits_done, weighted = (
            s.sem(x) for x in ("tiled", "product_done", "silu_done", "logits_done", "weighted"))
        act_step, dve_step = s.sem("act_step"), s.sem("dve_step")
        block = s.block()

        @block.sync
        def _(sp):
            sp.dma_start(w32[:], w_gate.rearrange("k p n -> p k n")).then_inc(arrived, 16)
            sp.dma_start(rows[:], head_rows.partition_broadcast(P)).then_inc(arrived, 16)

        @block.gpsimd
        def _(pool):
            with pool.Fori(0, TILES // 2) as i:
                for b in range(2):
                    pool.wait_ge(product_done, 2 * i + b + 1)
                    cols = bass.ts(2 * i + b, P)
                    pool.tensor_copy(tile_hi[:, b], feat_hi[:, :, cols]).then_inc(tiled, 1)
                    pool.tensor_copy(tile_lo[:, b], feat_lo[:, :, cols]).then_inc(tiled, 1)

        @block.tensor
        def _(pe):
            pe.sem_inc(product_done, 2)
            pe.wait_ge(w_lo_done, 1)
            with pe.Fori(0, TILES // 2) as i:
                for b in range(2):
                    pe.wait_ge(tiled, 4 * i + 2 * b + 2)
                    pe.wait_ge(logits_done, 2 * i + b + 1)
                    for kt in range(KT):
                        last = matmul3(pe, banks[b][:], tile_hi[:, b, kt, :], tile_lo[:, b, kt, :],
                                       w_hi[:, kt, :], w_lo[:, kt, :], kt == 0, kt == KT - 1)
                    last.then_inc(product_done, 1)

        @block.scalar
        def _(act):
            act.preload_act_table(ACT.Silu)
            act.sem_inc(logits_done, 2)
            act.wait_ge(arrived, 32)
            act.copy(w_hi[:], w32[:]).then_inc(w_hi_done, 1)
            with act.Fori(0, TILES // 2) as i:
                for b in range(2):
                    act.wait_ge(product_done, 2 * i + b + 3)
                    at = bass.ds(2 * i + b, 1)
                    act.activation(gate[:, at, 0:KEY], banks[b][:, 0:KEY], ACT.Silu).then_inc(silu_done, 1)
                    act.copy(logits[:, at, :], banks[b][:, KEY:]).then_inc(logits_done, 1)
            act.preload_act_table_set("natural_log_exp_and_others")
            act.activation(rate[:], rows[:, KEY + HEADS0:], ACT.Exp).then_inc(act_step, 1)
            act.wait_ge(logits_done, TILES + 2)
            act.activation(beta[:], logits[:, :, 0:HEADS0], ACT.Exp, scale=-1.0).then_inc(act_step, 1)
            act.wait_ge(dve_step, 2)
            act.activation(soft[:], soft[:], ACT.Exp, scale=-1.0).then_inc(act_step, 1)
            act.wait_ge(dve_step, 3)
            act.activation(soft[:], soft[:], ACT.Ln).then_inc(act_step, 1)

        @block.vector
        def _(dve):
            dve.wait_ge(w_hi_done, 1)
            dve.tensor_tensor(w_lo[:], w32[:], w_hi[:].bitcast(F32), ALU.subtract).then_inc(w_lo_done, 1)
            norm_weight = rows[:, 0:KEY].rearrange("p (o n) -> p o n", o=1)
            with dve.Fori(0, TILES) as i:
                dve.wait_ge(silu_done, i + 1)
                row = gate[:, bass.ds(i, 1), 0:KEY]
                dve.tensor_tensor(row, row, norm_weight, ALU.mult).then_inc(weighted, 1)
            dve.wait_ge(logits_done, TILES + 2)
            z = logits[:, :, HEADS0:]
            bias = rows[:, KEY:KEY + HEADS0].rearrange("p (o h) -> p o h", o=1).broadcast_to([P, TILES, HEADS0])
            dve.tensor_tensor(z, z, bias, ALU.add).then_inc(dve_step, 1)
            dve.wait_ge(dve_step, 1)
            dve.scalar_tensor_tensor(out=soft[:], in0=z, scalar=-1.0, in1=z, op0=ALU.mult,
                                     op1=ALU.max).then_inc(dve_step, 1)
            dve.wait_ge(act_step, 3)
            dve.tensor_scalar(soft[:], soft[:], 1.0, None, ALU.add).then_inc(dve_step, 1)
            dve.tensor_scalar(beta[:], beta[:], 1.0, None, ALU.add).then_inc(dve_step, 1)
            dve.wait_ge(dve_step, 4)
            dve.reciprocal(beta[:], beta[:]).then_inc(dve_step, 1)
            dve.wait_ge(act_step, 4)
            dve.scalar_tensor_tensor(out=soft[:], in0=z, scalar=0.0, in1=soft[:],
                                     op0=ALU.max, op1=ALU.add).then_inc(dve_step, 1)
            dve.wait_ge(dve_step, 6)
            spread = rate[:].rearrange("p (o h) -> p o h", o=1).broadcast_to([P, TILES, HEADS0])
            dve.tensor_tensor(decay[:], soft[:], spread, ALU.mult).then_inc(dve_step, 1)
            dve.wait_ge(dve_step, 7)
            dve.tensor_scalar(decay[:], decay[:], -1.0, None, ALU.mult).then_inc(dve_step, 1)


def delta_rule(nc, stream, ident, mask, hidden, qkv, beta, decay, w_out):
    with Scope(nc, "dr") as s:
        FOURS = BH // 4
        PAIRS = BH // 2
        w_hi, w_lo = s.sb("w_hi", [P, CT, DIM], F32R), s.sb("w_lo", [P, CT, DIM], F32R)
        raw = s.sb("raw", [P, BATCH, 3 * CT, P])
        norm, power = (s.sb(x, [P, BATCH, 2, HEADS0]) for x in ("norm", "power"))
        q_n, k_n, k_d, v_t = (s.sb(x, [P, BATCH, KEY]) for x in ("q_n", "k_n", "k_d", "v_t"))
        o_n = q_n
        o_hi, o_lo = s.sb("o_hi", [P, BATCH, CT, P], F32R), s.sb("o_lo", [P, BATCH, CT, P], F32R)
        q_g = s.sb("q_g", [P, BATCH, KEY])
        o_square = q_g
        k_w = raw[:].rearrange("p b i t -> p (b i t)")[:, 0:BATCH * KEY].rearrange("p (b n) -> p b n", b=BATCH)
        fm = s.sb("fm", [P, 3, BATCH, CT, P])
        g_now, beta_now = s.sb("g_now", [P, BATCH, HEADS0]), s.sb("beta_now", [P, BATCH, HEADS0])
        g_cols = s.sb("g_cols", [P, BH, P])
        w32 = g_cols[:].rearrange("p h t -> p (h t)").rearrange("p (k n) -> p k n", k=CT)
        e_g = s.sb("e_g", [P, 3, BH])
        minus_e_g = s.sb("minus_e_g", [P, BH])
        e_end = s.sb("e_end", [P, PAIRS])
        att = s.sb("att", [P, BH, P])
        a_t = s.sb("a_t", [P, BH, P])
        t_m, t_t, y_m = (s.sb(x, [P, BH, P]) for x in ("t_m", "t_t", "y_m"))
        square = y_m[:].rearrange("p h t -> p (h t)").rearrange("p (b a n) -> p b a n", b=BATCH, a=2)
        w_t = s.sb("w_t", [P, PAIRS, P])
        u_m = s.sb("u_m", [P, BH, HEAD_DIM0])
        state = s.sb("state", [P, PAIRS, HEAD_DIM0])
        o_norm = s.sb("o_norm", [P, BH])
        banks = [s.ps(f"bank{b}", [P, TB]) for b in range(8)]

        arrived, residual_in = s.sem("arrived"), s.sem("residual_in")
        w_hi_done, w_lo_done, const_done = s.sem("w_hi_done"), s.sem("w_lo_done"), s.sem("const_done")
        raw_done, now_done, g_cols_done, norm_done, masked, beta_in, o_norm_done = (
            s.sem(x) for x in ("raw_done", "now_done", "g_cols_done", "norm_done", "masked", "beta_in", "o_norm_done"))
        turned, sums_done, dlog_done, fm_turned, kk_done, qk_done, t0_turned = (
            s.sem(x) for x in ("turned", "sums_done", "dlog_done", "fm_turned", "kk_done", "qk_done", "t0_turned"))
        y_ps, z_ps, w_ps, u_ps, o_ps, state_ps, o_turned, out_ps = (
            s.sem(x) for x in ("y_ps", "z_ps", "w_ps", "u_ps", "o_ps", "state_ps", "o_turned", "out_ps"))
        e_g_done, squared, v_done, dec_done, fm_done, t0_done, w_done, o_squared, o_hi_done = (
            s.sem(x) for x in ("e_g_done", "squared", "v_done", "dec_done", "fm_done", "t0_done", "w_done",
                               "o_squared", "o_hi_done"))
        summed, normed, scaled, small, a_done, att_done, tt_done, y_done, t_done = (
            s.sem(x) for x in ("summed", "normed", "scaled", "small", "a_done", "att_done", "tt_done", "y_done", "t_done"))
        evens_done = s.sem("evens_done")
        u_done, state_done, o_summed, o_done, gated, o_lo_done, written = (
            s.sem(x) for x in ("u_done", "state_done", "o_summed", "o_done", "gated", "o_lo_done", "written"))
        block = s.block()

        def const(which, heads):
            return mask[:, which:which + 1, :].broadcast_to([P, heads, P])

        def fours(ap, f):
            return ap[:, 4 * f:4 * f + 4, :]

        def product_heads(ap, f):
            return ap[:, (slice(0, 8, 2), slice(1, 8, 2), slice(8, 12))[f], :]

        def bank_of_four(b):
            return banks[b][:].rearrange("p (h t) -> p h t", h=4)

        def bank_of_heads(b):
            return banks[b][:, 0:KEY].rearrange("p (h d) -> p h d", h=HEADS0)

        def heads(ap):
            if len(ap.shape) == 2:
                return ap.rearrange("p (h d) -> p h d", d=HEAD_DIM0)
            return ap.rearrange("p b (h d) -> p (b h) d", d=HEAD_DIM0)

        def along(ap, width):
            return ap.unsqueeze(2).broadcast_to([P, ap.shape[1], width])

        def tile_of(b, c):
            return bass.ds(b * CHUNKS + c, 1)

        def half_rows(h):
            return slice((h % 2) * HEAD_DIM0, (h % 2 + 1) * HEAD_DIM0)

        @block.sync
        def _(sp):
            sp.dma_start(w32, w_out.rearrange("(k p) n -> p k n", p=P)).then_inc(arrived, 16)
            with sp.Fori(0, CHUNKS) as c:
                for b in range(BATCH):
                    sp.wait_ge(gated, 2 * c + b + 1)
                    rows = hidden[bass.ds((b * CHUNKS + c) * P, P), :]
                    sp.dma_start(stream[:, tile_of(b, c), :], rows).then_inc(residual_in, 16)

        @block.gpsimd
        def _(pool):
            pool.memset(power[:], -0.5).then_inc(const_done, 1)
            pool.memset(state[:], 0.0).then_inc(const_done, 1)
            pool.wait_ge(const_done, 2)
            pool.wait_ge(w_lo_done, 1)
            with pool.Fori(0, CHUNKS) as c:
                pool.wait_ge(written, 2 * c + 2)
                pool.wait_ge(state_done, 2 * c + 2)
                for b in range(BATCH):
                    cols = bass.ds(b * SEQ + c * CHUNK, CHUNK)
                    pool.tensor_copy(raw[:, b], qkv[:, :, cols]).then_inc(raw_done, 1)
                for b in range(BATCH):
                    pool.tensor_copy(g_now[:, b, :], decay[:, tile_of(b, c), :]).then_inc(now_done, 1)
                    pool.tensor_copy(beta_now[:, b, :], beta[:, tile_of(b, c), :]).then_inc(now_done, 1)
                pool.wait_ge(now_done, 4 * c + 4)
                g_flat = g_now[:].rearrange("p b h -> p (b h)")
                beta_flat = beta_now[:].rearrange("p b h -> p (b h)")
                pool.tensor_tensor(g_cols[:], const(UPTO, BH), along(g_flat, P), ALU.mult).then_inc(g_cols_done, 1)
                pool.wait_ge(summed, 2 * c + 2)
                pool.tensor_tensor(norm[:], norm[:], power[:], ALU.pow).then_inc(norm_done, 1)
                pool.wait_ge(dec_done, 3 * c + 3)
                pool.tensor_tensor(a_t[:], att[:], const(BEFORE, BH), ALU.mult).then_inc(masked, 1)
                pool.wait_ge(masked, 2 * c + 1)
                pool.tensor_tensor(a_t[:], a_t[:], along(beta_flat, P), ALU.mult).then_inc(beta_in, 1)
                pool.tensor_tensor(att[:], att[:], const(UPTO, BH), ALU.mult).then_inc(masked, 1)
                pool.wait_ge(o_summed, 2 * c + 2)
                pool.tensor_tensor(o_norm[:], o_norm[:], power[:].rearrange("p b a h -> p (b a h)")[:, 0:BH],
                                   ALU.pow).then_inc(o_norm_done, 1)

        @block.scalar
        def _(act):
            act.preload_act_table(ACT.Exp)
            act.wait_ge(arrived, 16)
            act.copy(w_hi[:], w32).then_inc(w_hi_done, 1)
            with act.Fori(0, CHUNKS) as c:
                for b in range(BATCH):
                    for part in range(2):
                        act.wait_ge(turned, 6 * c + 3 * b + part + 1)
                        act.activation(square[:, b, part, :], banks[3 * b + part][:, 0:KEY],
                                       ACT.Square).then_inc(squared, 1)
                    act.wait_ge(turned, 6 * c + 3 * b + 3)
                    act.copy(v_t[:, b, :], banks[3 * b + 2][:, 0:KEY]).then_inc(v_done, 1)
                act.wait_ge(sums_done, c + 1)
                act.activation(e_g[:], banks[6][:, 0:3 * BH], ACT.Exp).then_inc(e_g_done, 1)
                for f in range(FOURS):
                    act.wait_ge(dlog_done, 3 * c + f + 1)
                    act.activation(fours(att, f), bank_of_four(7 - f % 2), ACT.Exp).then_inc(dec_done, 1)
                for x in range(6):
                    act.wait_ge(fm_turned, 6 * c + x + 1)
                    act.copy(fm[:, x // 2, x % 2], banks[x][:, 0:KEY].rearrange("p (k t) -> p k t", k=CT))\
                       .then_inc(fm_done, 1)
                for f in range(FOURS):
                    act.wait_ge(t0_turned, 3 * c + f + 1)
                    act.copy(fours(t_m, f), bank_of_four(f)).then_inc(t0_done, 1)
                for b in range(BATCH):
                    act.wait_ge(w_ps, 2 * c + b + 1)
                    act.copy(w_t[:, CT * b:CT * b + CT, :], banks[6 + b][:, 0:KEY].rearrange("p (k t) -> p k t", k=CT))\
                       .then_inc(w_done, 1)
                for odd in range(2):
                    act.wait_ge(o_ps, 2 * c + odd + 1)
                    act.activation(o_square[:, odd, :], banks[2 + odd][:, 0:KEY], ACT.Square).then_inc(o_squared, 1)
                for b in range(BATCH):
                    act.wait_ge(o_turned, 2 * c + b + 1)
                    act.copy(o_hi[:, b], banks[5 + b][:, 0:KEY].rearrange("p (k t) -> p k t", k=CT))\
                       .then_inc(o_hi_done, 1)

        @block.vector
        def _(dve):
            dve.wait_ge(w_hi_done, 1)
            dve.tensor_tensor(w_lo[:], w32, w_hi[:].bitcast(F32), ALU.subtract).then_inc(w_lo_done, 1)
            dve.sem_inc(written, 2)
            dve.sem_inc(state_done, 2)
            with dve.Fori(0, CHUNKS) as c:
                dve.wait_ge(squared, 4 * c + 4)
                dve.tensor_reduce(norm[:].rearrange("p b a h -> p (b a h)"),
                                  square.rearrange("p b a (h d) -> p (b a h) d", d=HEAD_DIM0),
                                  AX.X, ALU.add).then_inc(summed, 1)
                dve.wait_ge(summed, 2 * c + 1)
                dve.tensor_scalar(norm[:], norm[:], 1e-6, None, ALU.add).then_inc(summed, 1)
                dve.wait_ge(norm_done, c + 1)
                dve.tensor_scalar(norm[:, :, 0, :], norm[:, :, 0, :], HEAD_DIM0 ** -0.5, None,
                                  ALU.mult).then_inc(small, 1)
                dve.wait_ge(e_g_done, c + 1)
                dve.tensor_scalar(minus_e_g[:], e_g[:, 0, :], -1.0, None, ALU.mult).then_inc(small, 1)
                dve.tensor_copy(e_end[0:HEAD_DIM0, :], e_g[0:HEAD_DIM0, 2, 0::2]).then_inc(small, 1)
                dve.tensor_copy(e_end[HEAD_DIM0:, :], e_g[HEAD_DIM0:, 2, 1::2]).then_inc(small, 1)
                dve.wait_ge(small, 4 * c + 4)
                for b in range(BATCH):
                    dve.tensor_tensor(heads(k_n[:, b, :]), bank_of_heads(3 * b + 1),
                                      along(norm[:, b, 1, :], HEAD_DIM0), ALU.mult).then_inc(normed, 1)
                    dve.tensor_tensor(heads(q_n[:, b, :]), bank_of_heads(3 * b),
                                      along(norm[:, b, 0, :], HEAD_DIM0), ALU.mult).then_inc(normed, 1)
                dve.wait_ge(normed, 4 * c + 4)
                dve.tensor_tensor(heads(q_g[:]), heads(q_n[:]), along(e_g[:, 0, :], HEAD_DIM0), ALU.mult).then_inc(scaled, 1)
                dve.tensor_tensor(heads(k_w), heads(k_n[:]), along(minus_e_g[:], HEAD_DIM0), ALU.mult).then_inc(scaled, 1)
                dve.tensor_tensor(heads(k_d[:]), heads(k_n[:]), along(e_g[:, 1, :], HEAD_DIM0), ALU.mult).then_inc(scaled, 1)
                dve.wait_ge(beta_in, c + 1)
                for f in range(FOURS):
                    dve.wait_ge(kk_done, 3 * c + f + 1)
                    dve.tensor_tensor(product_heads(a_t, f), bank_of_four(f), product_heads(a_t, f), ALU.mult).then_inc(a_done, 1)
                dve.wait_ge(a_done, 3 * c + 3)
                dve.tensor_tensor(t_t[:], a_t[:], const(PAIR_T, BH), ALU.mult).then_inc(tt_done, 1)
                dve.wait_ge(tt_done, 2 * c + 1)
                dve.tensor_tensor(t_t[:], t_t[:], ident[:].unsqueeze(1).broadcast_to([P, BH, P]), ALU.add).then_inc(tt_done, 1)
                dve.wait_ge(masked, 2 * c + 2)
                for f in range(FOURS):
                    dve.wait_ge(qk_done, 3 * c + f + 1)
                    dve.tensor_tensor(product_heads(att, f), bank_of_four(3 + f), product_heads(att, f), ALU.mult).then_inc(att_done, 1)
                dve.wait_ge(t0_done, 3 * c + 3)
                for level in range(LEVELS):
                    last = level == LEVELS - 1
                    for f in range(FOURS):
                        at = FOURS * (LEVELS * c + level) + f
                        dve.wait_ge(y_ps, at + 1)
                        dve.tensor_tensor(fours(y_m, f), bank_of_four(f), const(LEVEL0 + level, 4),
                                          ALU.mult).then_inc(y_done, 1)
                    for f in range(FOURS):
                        at = FOURS * (LEVELS * c + level) + f
                        dve.wait_ge(z_ps, at + 1)
                        if not last:
                            dve.tensor_tensor(fours(t_m, f), fours(t_m, f), bank_of_four(3 + f),
                                              ALU.add).then_inc(t_done, 1)
                        dve.tensor_tensor(fours(t_t, f), fours(t_t, f), bank_of_four(f), ALU.add).then_inc(t_done, 1)
                beta_flat = beta_now[:].rearrange("p b h -> p (b h)")
                for odd in range(2):
                    dve.wait_ge(u_ps, 2 * c + odd + 1)
                    dve.tensor_tensor(u_m[:, odd::2, :], bank_of_heads(odd),
                                      along(beta_flat[:, odd::2], HEAD_DIM0), ALU.mult).then_inc(u_done, 1)
                for odd in range(2):
                    dve.wait_ge(o_squared, 2 * c + odd + 1)
                dve.tensor_reduce(o_norm[:], heads(o_square[:]), AX.X, ALU.add).then_inc(o_summed, 1)
                dve.wait_ge(o_summed, 2 * c + 1)
                dve.tensor_scalar(o_norm[:], o_norm[:], 1.0 / HEAD_DIM0, EPS, ALU.mult, ALU.add).then_inc(o_summed, 1)
                dve.wait_ge(state_ps, c + 1)
                dve.tensor_tensor(state[:], state[:], along(e_end[:], HEAD_DIM0), ALU.mult).then_inc(state_done, 1)
                dve.wait_ge(state_done, 2 * c + 3)
                dve.tensor_tensor(state[:], state[:], banks[4][:, 0:KEY].rearrange("p (j d) -> p j d", j=PAIRS),
                                  ALU.add).then_inc(state_done, 1)
                dve.wait_ge(o_norm_done, c + 1)
                for odd in range(2):
                    dve.tensor_tensor(heads(o_n[:])[:, odd::2, :], bank_of_heads(2 + odd),
                                      along(o_norm[:, HEADS0 * odd:HEADS0 * (odd + 1)], HEAD_DIM0),
                                      ALU.mult).then_inc(o_done, 1)
                dve.wait_ge(o_done, 2 * c + 2)
                for b in range(BATCH):
                    row = o_n[:, b:b + 1, :]
                    dve.tensor_tensor(row, row, stream[:, tile_of(b, c), 0:KEY], ALU.mult).then_inc(gated, 1)
                for b in range(BATCH):
                    dve.wait_ge(o_hi_done, 2 * c + b + 1)
                    dve.tensor_tensor(o_lo[:, b], banks[5 + b][:, 0:KEY].rearrange("p (k t) -> p k t", k=CT),
                                      o_hi[:, b].bitcast(F32), ALU.subtract).then_inc(o_lo_done, 1)
                dve.wait_ge(residual_in, 32 * c + 32)
                for b in range(BATCH):
                    dve.wait_ge(out_ps, 2 * c + b + 1)
                    row = stream[:, tile_of(b, c), :]
                    bank = banks[(7, 0)[b]][:].rearrange("p (o n) -> p o n", o=1)
                    dve.tensor_tensor(row, row, bank, ALU.add).then_inc(written, 1)

        @block.tensor
        def _(pe):
            pe.wait_ge(w_lo_done, 1)
            pe.wait_ge(const_done, 2)
            with pe.Fori(0, CHUNKS) as c:
                for b in range(BATCH):
                    pe.wait_ge(raw_done, 2 * c + b + 1)
                    for part in range(3):
                        for k in range(CT):
                            last = pe.transpose(banks[3 * b + part][:, k * P:(k + 1) * P], raw[:, b, CT * part + k, :], ident[:])
                        last.then_inc(turned, 1)
                pe.wait_ge(now_done, 4 * c + 4)
                g = g_now[:].rearrange("p b h -> p (b h)")
                for x, which in enumerate((UPTO, AFTER, ONES)):
                    last = pe.matmul(banks[6][:, BH * x:BH * (x + 1)], mask[:, which, :], g, start=True, stop=True)
                last.then_inc(sums_done, 1)
                pe.wait_ge(g_cols_done, c + 1)
                for f in range(FOURS):
                    if f == 1:
                        pe.wait_ge(e_g_done, c + 1)
                    if f == 2:
                        pe.wait_ge(dec_done, 3 * c + 1)
                    pe.matmul(banks[7 - f % 2][:], mask[:, AFTER, :], fours(g_cols, f).rearrange("p h t -> p (h t)"),
                              start=True, stop=True).then_inc(dlog_done, 1)
                pe.wait_ge(v_done, 2 * c + 2)
                for x, (source, done, count) in enumerate((
                        (k_n, normed, 4 * c + 4), (k_n, normed, 4 * c + 4), (q_n, normed, 4 * c + 4),
                        (q_n, normed, 4 * c + 4), (q_g, scaled, 3 * c + 1), (q_g, scaled, 3 * c + 1))):
                    pe.wait_ge(done, count)
                    for k in range(CT):
                        last = pe.transpose(banks[x][:, k * P:(k + 1) * P], source[:, x % 2, k * P:(k + 1) * P], ident[:])
                    last.then_inc(fm_turned, 1)
                for kind, done in ((0, kk_done), (1, qk_done)):
                    pe.wait_ge(fm_done, 6 * c + 6)
                    for i in (0, 1, 2, 3, 4, 5, 6, 7, 8, 10, 9, 11):
                        b, h = divmod(i, HEADS0)
                        bank, col = (i % 2, i // 2) if i < 8 else (2, i - 8)
                        if i == 9:
                            pe.wait_ge(evens_done, 2 * c + kind + 1)
                        last = pe.matmul(banks[3 * kind + bank][:, col * P:(col + 1) * P],
                                         fm[half_rows(h), 0, b, h // 2, :], fm[half_rows(h), kind, b, h // 2, :],
                                         start=True, stop=True)
                        if i in (6, 7, 11):
                            last.then_inc(done, 1)
                        if i == 10:
                            last.then_inc(evens_done, 1)
                pe.wait_ge(tt_done, 2 * c + 2)
                for f in range(FOURS):
                    for j in range(4):
                        last = pe.transpose(banks[f][:, j * P:(j + 1) * P], t_t[:, 4 * f + j, :], ident[:])
                    last.then_inc(t0_turned, 1)
                for level in range(LEVELS):
                    updates = 2 * FOURS * LEVELS - FOURS
                    for f in range(FOURS):
                        if level == 0:
                            pe.wait_ge(t0_done, 3 * c + f + 1)
                            pe.wait_ge(att_done, 3 * c + 3)
                        else:
                            pe.wait_ge(t_done, updates * c + 2 * (FOURS * (level - 1) + f) + 2)
                        for j in range(4):
                            i = 4 * f + j
                            last = pe.matmul(banks[f][:, j * P:(j + 1) * P], a_t[:, i, :], t_m[:, i, :],
                                             start=True, stop=True)
                        last.then_inc(y_ps, 1)
                    for f in range(FOURS):
                        pe.wait_ge(y_done, FOURS * (LEVELS * c + level) + f + 1)
                        for j in range(4):
                            i = 4 * f + j
                            cols = slice(j * P, (j + 1) * P)
                            if level < LEVELS - 1:
                                pe.matmul(banks[3 + f][:, cols], t_t[:, i, :], y_m[:, i, :], start=True, stop=True)
                            last = pe.matmul(banks[f][:, cols], y_m[:, i, :], t_t[:, i, :], start=True, stop=True)
                        last.then_inc(z_ps, 1)
                pe.wait_ge(t_done, updates * (c + 1))
                pe.wait_ge(scaled, 3 * c + 3)
                for i in range(BH):
                    b, h = divmod(i, HEADS0)
                    last = pe.matmul(banks[6 + b][half_rows(h), (h // 2) * P:(h // 2 + 1) * P],
                                     k_w[:, b, h * HEAD_DIM0:(h + 1) * HEAD_DIM0], t_t[:, i, :], start=True, stop=True)
                    if h == HEADS0 - 1:
                        last.then_inc(w_ps, 1)
                pe.wait_ge(w_done, 2 * c + 2)
                for i in range(BH):
                    b, h = divmod(i, HEADS0)
                    at = slice((i // 2) * HEAD_DIM0, (i // 2 + 1) * HEAD_DIM0)
                    pe.matmul(banks[i % 2][:, at], t_t[:, i, :], v_t[:, b, h * HEAD_DIM0:(h + 1) * HEAD_DIM0],
                              start=True, stop=False)
                    last = pe.matmul(banks[i % 2][:, at], w_t[half_rows(h), i // 2, :], state[half_rows(h), i // 2, :],
                                     start=False, stop=True)
                    if i >= BH - 2:
                        last.then_inc(u_ps, 1)
                for i in range(BH):
                    b, h = divmod(i, HEADS0)
                    at = slice((i // 2) * HEAD_DIM0, (i // 2 + 1) * HEAD_DIM0)
                    pe.wait_ge(u_done, 2 * c + 2)
                    pe.matmul(banks[2 + i % 2][:, at], fm[half_rows(h), 2, b, h // 2, :], state[half_rows(h), i // 2, :],
                              start=True, stop=False)
                    last = pe.matmul(banks[2 + i % 2][:, at], att[:, i, :], u_m[:, i, :], start=False, stop=True)
                    if i >= BH - 2:
                        last.then_inc(o_ps, 1)
                for i in range(BH):
                    b, h = divmod(i, HEADS0)
                    last = pe.matmul(banks[4][half_rows(h), (i // 2) * HEAD_DIM0:(i // 2 + 1) * HEAD_DIM0],
                                     k_d[:, b, h * HEAD_DIM0:(h + 1) * HEAD_DIM0], u_m[:, i, :], start=True, stop=True)
                last.then_inc(state_ps, 1)
                for b in range(BATCH):
                    pe.wait_ge(gated, 2 * c + b + 1)
                    for k in range(CT):
                        last = pe.transpose(banks[5 + b][:, k * P:(k + 1) * P], o_n[:, b, k * P:(k + 1) * P], ident[:])
                    last.then_inc(o_turned, 1)
                for b in range(BATCH):
                    pe.wait_ge(o_lo_done, 2 * c + b + 1)
                    for k in range(CT):
                        last = matmul3(pe, banks[(7, 0)[b]][:], o_hi[:, b, k, :], o_lo[:, b, k, :],
                                       w_hi[:, k, :], w_lo[:, k, :], k == 0, k == CT - 1)
                    last.then_inc(out_ps, 1)


def delta_attention(nc, stream, ident, mask, hidden, w_qkv, conv_w, w_gate, head_rows, w_out):
    with Scope(nc, "da") as keep:
        qkv = keep.sb("qkv", [P, 3 * CT, TOKENS])
        beta, decay = keep.sb("beta", [P, TILES, HEADS0]), keep.sb("decay", [P, TILES, HEADS0])
        with Scope(nc, "daf") as f:
            feat_hi, feat_lo = f.sb("feat_hi", [P, KT, TOKENS], F32R), f.sb("feat_lo", [P, KT, TOKENS], F32R)
            normalise(nc, "n0a", stream, ident, feat_hi, feat_lo, feature_tiles_plain)
            project_conv(nc, feat_hi, feat_lo, w_qkv, conv_w, qkv)
            gates_and_decays(nc, feat_hi, feat_lo, w_gate, head_rows, stream, beta, decay)
        delta_rule(nc, stream, ident, mask, hidden, qkv, beta, decay, w_out)


HEADS1, HALF, HEAD_DIM1, LATENT = 16, 16, 32, 64
QUAD = 4
QUADS = HEADS1 // QUAD
QTILES = SEQ // P
STACK = 4 * HALF


def latents(nc, feat_hi, feat_lo, w_down, w_value, lat_hi, lat_lo, values):
    with Scope(nc, "lat") as s:
        wd32 = s.sb("wd32", [P, KT, P])
        wv32 = s.sb("wv32", [P, DIM])
        wd_hi, wd_lo = s.sb("wd_hi", [P, KT, P], F32R), s.sb("wd_lo", [P, KT, P], F32R)
        wv_hi, wv_lo = s.sb("wv_hi", [P, DIM], F32R), s.sb("wv_lo", [P, DIM], F32R)
        lat_ps = [s.ps(f"lat{b}", [P, TB]) for b in range(2)]
        val_ps = [s.ps(f"val{b}", [P, DIM]) for b in range(2)]
        arrived = s.sem("arrived")
        w_hi_done, w_lo_done = s.sem("w_hi_done"), s.sem("w_lo_done")
        lat_done, val_done = s.sem("lat_done"), s.sem("val_done")
        hi_done, lo_done = s.sem("hi_done"), s.sem("lo_done")
        val_hi_done, val_lo_done = s.sem("val_hi_done"), s.sem("val_lo_done")
        block = s.block()
        KV = slice(LATENT, 2 * LATENT)

        def values_of(i, half):
            b, tile = divmod(i, QTILES)
            return values[:, QUADS * b:QUADS * (b + 1), tile, :, half * HEAD_DIM1:(half + 1) * HEAD_DIM1]

        @block.sync
        def _(sp):
            sp.dma_start(wd32[:], w_down.rearrange("(k p) n -> p k n", p=P)).then_inc(arrived, 16)
            sp.dma_start(wv32[KV, :], w_value).then_inc(arrived, 16)

        @block.scalar
        def _(act):
            act.wait_ge(arrived, 32)
            act.copy(wd_hi[:], wd32[:]).then_inc(w_hi_done, 1)
            act.copy(wv_hi[KV, :], wv32[KV, :]).then_inc(w_hi_done, 1)
            for b in range(BLOCKS):
                act.wait_ge(lat_done, b + 1)
                act.copy(lat_hi[:, b * TB:(b + 1) * TB], lat_ps[b % 2][:]).then_inc(hi_done, 1)
            for i in range(TILES):
                act.wait_ge(val_done, i + 1)
                act.copy(values_of(i, 0), val_ps[i % 2][:].rearrange("p (q h d) -> p q h d", q=QUADS, h=QUAD))\
                   .then_inc(val_hi_done, 1)

        @block.vector
        def _(dve):
            dve.wait_ge(w_hi_done, 2)
            dve.tensor_tensor(wd_lo[:], wd32[:], wd_hi[:].bitcast(F32), ALU.subtract).then_inc(w_lo_done, 1)
            dve.tensor_tensor(wv_lo[KV, :], wv32[KV, :], wv_hi[KV, :].bitcast(F32),
                              ALU.subtract).then_inc(w_lo_done, 1)
            for b in range(BLOCKS):
                dve.wait_ge(hi_done, b + 1)
                cols = slice(b * TB, (b + 1) * TB)
                dve.tensor_tensor(lat_lo[:, cols], lat_ps[b % 2][:], lat_hi[:, cols].bitcast(F32),
                                  ALU.subtract).then_inc(lo_done, 1)
            for i in range(TILES):
                dve.wait_ge(val_hi_done, i + 1)
                dve.tensor_tensor(values_of(i, 1), val_ps[i % 2][:].rearrange("p (q h d) -> p q h d", q=QUADS, h=QUAD),
                                  values_of(i, 0).bitcast(F32), ALU.subtract).then_inc(val_lo_done, 1)

        @block.tensor
        def _(pe):
            pe.wait_ge(w_hi_done, 2)
            pe.wait_ge(w_lo_done, 2)
            for b in range(BLOCKS):
                if b >= 2:
                    pe.wait_ge(lo_done, b - 1)
                cols = slice(b * TB, (b + 1) * TB)
                for kt in range(KT):
                    last = matmul3(pe, lat_ps[b % 2][:], wd_hi[:, kt, :], wd_lo[:, kt, :],
                                   feat_hi[:, kt, cols], feat_lo[:, kt, cols], kt == 0, kt == KT - 1)
                last.then_inc(lat_done, 1)
            for i in range(TILES):
                if i % SUB == 0:
                    pe.wait_ge(lo_done, i // SUB + 1)
                if i >= 2:
                    pe.wait_ge(val_lo_done, i - 1)
                cols = slice(i * P, (i + 1) * P)
                matmul3(pe, val_ps[i % 2][:], lat_hi[KV, cols], lat_lo[KV, cols], wv_hi[KV, :], wv_lo[KV, :],
                        True, True).then_inc(val_done, 1)


def rotated_heads(nc, lat_hi, lat_lo, w_up, cos_sin, rotated):
    with Scope(nc, "rot") as s:
        wu32 = s.sb("wu32", [P, QUADS, 2 * P])
        wu_hi, wu_lo = s.sb("wu_hi", [P, QUADS, 2 * P], F32R), s.sb("wu_lo", [P, QUADS, 2 * P], F32R)
        tables = s.sb("tables", [P, 2, SEQ])
        part = s.sb("part", [P, 2, SEQ])
        rot = s.sb("rot", [P, 2, SEQ])
        rot_hi, rot_lo = s.sb("rot_hi", [P, 2, SEQ], F32R), s.sb("rot_lo", [P, 2, SEQ], F32R)
        product = [s.ps(f"product{b}", [P, 2, TB]) for b in range(4)]
        arrived, wu_hi_done, wu_lo_done = s.sem("arrived"), s.sem("wu_hi_done"), s.sem("wu_lo_done")
        proj_done, part_done, rot_done = s.sem("proj_done"), s.sem("part_done"), s.sem("rot_done")
        rot_hi_done, rot_lo_done = s.sem("rot_hi_done"), s.sem("rot_lo_done")
        stored = [s.sem(f"stored{x}") for x in range(2)]
        block = s.block()

        def passes(engine, body):
            with engine.Fori(0, BATCH) as b:
                for quad in range(QUADS):
                    body(QUADS * b + quad, b, quad)

        @block.sync
        def _(sp):
            sp.dma_start(wu32[:], w_up.rearrange("q p n -> p q n")).then_inc(arrived, 16)
            sp.dma_start(tables[:], cos_sin).then_inc(arrived, 16)
            for x in range(2):
                sp.sem_inc(stored[x], 32)
            for n in range(BATCH * QUADS):
                for which, half, done in ((0, rot_hi, rot_hi_done), (1, rot_lo, rot_lo_done)):
                    sp.wait_ge(done, n + 1)
                    sp.dma_start(rotated[n, which], half[:, n % 2, :].bitcast(F32)).then_inc(stored[n % 2], 16)
            for x in range(2):
                sp.wait_ge(stored[x], 32 * BATCH * QUADS // 2 + 32)

        @block.tensor
        def _(pe):
            pe.sem_inc(proj_done, 4)
            pe.wait_ge(wu_lo_done, 1)

            def body(n, b, quad):
                for x in range(2):
                    pe.wait_ge(part_done, 2 * n + x + 1)
                    bank = product[2 * (quad % 2) + x]
                    for half in range(2):
                        cols = bass.ds(b * SEQ + half * TB, TB)
                        last = matmul3(pe, bank[:, half, :], wu_hi[:, quad, x * P:(x + 1) * P],
                                       wu_lo[:, quad, x * P:(x + 1) * P], lat_hi[:, cols], lat_lo[:, cols], True, True)
                    last.then_inc(proj_done, 1)

            passes(pe, body)

        @block.vector
        def _(dve):
            dve.wait_ge(wu_hi_done, 1)
            dve.tensor_tensor(wu_lo[:], wu32[:], wu_hi[:].bitcast(F32), ALU.subtract).then_inc(wu_lo_done, 1)
            dve.sem_inc(part_done, 4)

            def body(n, b, quad):
                for x in range(2):
                    dve.wait_ge(proj_done, 2 * n + x + 5)
                    dve.wait_ge(rot_done, n + 1)
                    dve.tensor_tensor(part[:, x, :], product[2 * (quad % 2) + x][:].rearrange("p a t -> p (a t)"),
                                      tables[:, x, :], ALU.mult).then_inc(part_done, 1)
                dve.wait_ge(rot_hi_done, n + 1)
                dve.tensor_tensor(rot_lo[:, quad % 2, :], rot[:, quad % 2, :], rot_hi[:, quad % 2, :].bitcast(F32),
                                  ALU.subtract).then_inc(rot_lo_done, 1)

            passes(dve, body)

        @block.gpsimd
        def _(pool):
            pool.sem_inc(rot_done, 1)

            def body(n, b, quad):
                pool.wait_ge(part_done, 2 * n + 6)
                pool.wait_ge(stored[quad % 2], 32 * (QUADS // 2 * b + quad // 2) + 32)
                pool.tensor_tensor(rot[:, quad % 2, :], part[:, 0, :], part[:, 1, :], ALU.add).then_inc(rot_done, 1)

            passes(pool, body)

        @block.scalar
        def _(act):
            act.wait_ge(arrived, 32)
            act.copy(wu_hi[:], wu32[:]).then_inc(wu_hi_done, 1)

            def body(n, b, quad):
                act.wait_ge(rot_done, n + 2)
                act.copy(rot_hi[:, quad % 2, :], rot[:, quad % 2, :]).then_inc(rot_hi_done, 1)

            passes(act, body)


OUT_ROWS = 2 * HEAD_DIM1 + 1
OUT_COLS = OUT_ROWS + 1
LOW_POOL = 640
AHEAD = QTILES + 2


def softmax_heads(nc, ident, values, rotated, mixed):
    with Scope(nc, "att") as s:
        q_stack = [s.sb(f"q_stack{j}", [P, SEQ], F32R) for j in range(QUAD)]
        k_stack = [s.sb(f"k_stack{j}", [P, SEQ], F32R) for j in range(QUAD)]
        top = [s.sb(f"top{b}", [P, STACK + QTILES]) for b in range(2)]
        head_values = s.sb("head_values", [P, 2, QTILES, OUT_COLS], F32R)
        probs = s.sb("probs", [P, 2, SEQ])
        p_hi, p_lo = s.sb("p_hi", [P, 2, SEQ], F32R), s.sb("p_lo", [P, 2, SEQ], F32R)
        out_t = s.sb("out_t", [P, 2, TB])
        inverse = s.sb("inverse", [P, QTILES])
        parts = s.sb("parts", [P, 2, QTILES, HEAD_DIM1])
        q_scores, k_scores = s.ps("q_scores", [P, 2, TB]), s.ps("k_scores", [P, 2, TB])
        out_ps = [s.ps(f"out{b}", [P, TB]) for b in range(2)]
        turned = s.ps("turned", [P, 2, TB])

        loaded = [s.sem(f"loaded{j}") for j in range(QUAD)]
        ones_done = s.sem("ones_done")
        a_done, max_done, top_turned, top_done = (s.sem(x) for x in ("a_done", "max_done", "top_turned", "top_done"))
        b_done, exp_done, hi_done, lo_dve, lo_pool = (s.sem(x) for x in ("b_done", "exp_done", "hi_done", "lo_dve", "lo_pool"))
        values_ready, out_done, copied_act, copied_dve = (s.sem(x) for x in ("values_ready", "out_done", "copied_act", "copied_dve"))
        out_turned, inverse_done, parts_done, mixed_done = (s.sem(x) for x in ("out_turned", "inverse_done", "parts_done", "mixed_done"))
        block = s.block()
        PASSES = BATCH * QUADS
        T = QTILES
        TOP = slice(STACK, STACK + T)

        def passes(engine, body):
            body(0, True, False)
            with engine.Fori(1, PASSES - 1) as n:
                body(n, False, False)
            body(PASSES - 1, False, True)

        @block.sync
        def _(sp):
            for n in range(PASSES):
                for j in range(QUAD):
                    if n:
                        sp.wait_ge(b_done, T * (QUAD * (n - 1) + j + 1))
                    for first, dst, which, copies in ((0, q_stack[j], 0, 0), (0, q_stack[j], 1, 0),
                                                      (LATENT, k_stack[j], 0, P * SEQ), (LATENT, k_stack[j], 1, P * SEQ)):
                        at = rotated[n, 0 if copies else which, first + HALF * j:first + HALF * (j + 1), :]
                        src = bass.AP(tensor=at.tensor, offset=at.offset, ap=[[copies, 2], [SEQ, HALF], [1, SEQ]])
                        rows = slice(which * STACK // 2, (which + 1) * STACK // 2)
                        sp.dma_start(dst[rows, :].bitcast(F32), src).then_inc(loaded[j], 16)

        @block.gpsimd
        def _(pool):
            def values_of(n, j, buffer):
                pool.tensor_copy(head_values[:, buffer, :, 0:2 * HEAD_DIM1],
                                 values[:, bass.ds(n, 1), :, j, :].rearrange("p o t d -> p (o t) d"))\
                    .then_inc(values_ready, 1)

            def low(n, j, t):
                at = T * (QUAD * n + j) + t
                pool.wait_ge(hi_done, at + 1)
                pool.tensor_tensor(p_lo[:, t % 2, 0:LOW_POOL], probs[:, t % 2, 0:LOW_POOL],
                                   p_hi[:, t % 2, 0:LOW_POOL].bitcast(F32), ALU.subtract).then_inc(lo_pool, 1)

            def add_parts(n, j):
                g = QUAD * n + j
                pool.wait_ge(parts_done, 2 * g + 2)
                dst = mixed[:, bass.ds(n, 1), :, HEAD_DIM1 * j:HEAD_DIM1 * (j + 1)].rearrange("p o t d -> p (o t) d")
                pool.tensor_tensor(dst, parts[:, 0], parts[:, 1], ALU.add).then_inc(mixed_done, 1)

            def body(n, first, last):
                for j in range(QUAD):
                    g = QUAD * n + j
                    for t in range(T):
                        low(n, j, t)
                        if t == 1 and not (last and j == QUAD - 1):
                            if not (first and j == 0):
                                pool.wait_ge(out_done, T * g)
                            values_of(n + (j + 1) // QUAD, (j + 1) % QUAD, (j + 1) % 2)
                        if t == 4 and not (first and j == 0):
                            add_parts(n + (j - 1) // QUAD, (j - 1) % QUAD)

            values_of(0, 0, 0)
            passes(pool, body)
            add_parts(PASSES - 1, QUAD - 1)

        @block.scalar
        def _(act):
            act.preload_act_table(ACT.Exp)

            def copy_out(g, first):
                act.wait_ge(out_done, T * (g + 1))
                if not first:
                    act.wait_ge(out_turned, g)
                act.copy(out_t[0:OUT_COLS, 0, :], out_ps[0][0:OUT_COLS, :]).then_inc(copied_act, 1)

            def body(n, first, last):
                for j in range(QUAD):
                    g = QUAD * n + j
                    for t in range(T):
                        at = T * g + t
                        early = first and j == 0
                        act.wait_ge(b_done, at + 1)
                        if not (early and t < 2):
                            act.wait_ge(lo_dve, at - 1)
                            act.wait_ge(lo_pool, at - 1)
                        act.activation(probs[:, t % 2, :], k_scores[:], ACT.Exp).then_inc(exp_done, 1)
                        if t == 1 and not early:
                            copy_out(g - 1, first and j == 1)
                        act.wait_ge(exp_done, at + 1)
                        if not (early and t < 2):
                            act.wait_ge(out_done, at - 1)
                        act.copy(p_hi[:, t % 2, :], probs[:, t % 2, :]).then_inc(hi_done, 1)

            passes(act, body)
            copy_out(QUAD * PASSES - 1, False)

        @block.vector
        def _(dve):
            ones = probs[:, 0, :]
            dve.memset(ones, 1.0).then_inc(ones_done, 1)
            for b in range(2):
                dve.memset(top[b][:], 0.0).then_inc(ones_done, 1)
            dve.wait_ge(ones_done, 3)
            for j in range(QUAD):
                dve.tensor_copy(k_stack[j][TOP, :], ones[TOP, :]).then_inc(ones_done, 1)
            extra = head_values[:, :, :, 2 * HEAD_DIM1:].rearrange("p b t x -> p (b t) x")
            dve.tensor_copy(extra, ones[:, 0:4 * T].rearrange("p (t x) -> p t x", x=2)).then_inc(ones_done, 1)

            def maximum(g, buffer, t, first):
                if t == 0 and not first:
                    dve.wait_ge(top_turned, g - 1)
                dve.wait_ge(a_done, T * g + t + 1)
                dve.tensor_reduce(top[buffer][:, STACK + t:STACK + t + 1], q_scores[:], AX.XY, ALU.max,
                                  negate=True).then_inc(max_done, 1)

            def spread_top(g, j):
                dve.wait_ge(top_turned, g + 1)
                tile = turned[TOP, 0, 0:P].unsqueeze(1).broadcast_to([T, T, P])
                own = ident[TOP, TOP].unsqueeze(2).broadcast_to([T, T, P])
                dve.tensor_tensor(q_stack[j][TOP, :].rearrange("r (t q) -> r t q", t=T), tile, own,
                                  ALU.mult).then_inc(top_done, 1)

            def low(at, buffer):
                dve.wait_ge(hi_done, at + 1)
                dve.tensor_tensor(p_lo[:, buffer, LOW_POOL:], probs[:, buffer, LOW_POOL:],
                                  p_hi[:, buffer, LOW_POOL:].bitcast(F32), ALU.subtract).then_inc(lo_dve, 1)

            def copy_out(g, first):
                dve.wait_ge(out_done, T * (g + 1))
                if not first:
                    dve.wait_ge(out_turned, g)
                dve.tensor_copy(out_t[0:OUT_COLS, 1, :], out_ps[1][0:OUT_COLS, :]).then_inc(copied_dve, 1)

            def normalise_out(g, first):
                dve.wait_ge(out_turned, g + 1)
                out = turned[:, :, 0:T // 2 * OUT_COLS].rearrange("p a (t d) -> p a t d", d=OUT_COLS)
                by_tile = "p (a t) d -> p a t d"
                if not first:
                    dve.wait_ge(parts_done, 2 * g)
                    dve.wait_ge(mixed_done, g)
                dve.reciprocal(inverse[:].rearrange("p (a t) -> p a t", a=2), out[:, :, :, OUT_ROWS - 1])\
                   .then_inc(inverse_done, 1)
                dve.wait_ge(inverse_done, g + 1)
                spread = inverse[:].unsqueeze(2).broadcast_to([P, T, HEAD_DIM1]).rearrange(by_tile, a=2)
                for x in range(2):
                    dve.tensor_tensor(parts[:, x].rearrange(by_tile, a=2),
                                      out[:, :, :, HEAD_DIM1 * x:HEAD_DIM1 * (x + 1)], spread,
                                      ALU.mult).then_inc(parts_done, 1)

            def body(n, first, last):
                for j in range(QUAD):
                    g = QUAD * n + j
                    early = first and j == 0
                    for t in range(T):
                        if not (early and t == 0):
                            low(T * g + t - 1, (t - 1) % 2)
                        ahead, tile = divmod(t + AHEAD, T)
                        if t == 1 and not early:
                            copy_out(g - 1, first and j == 1)
                        if not (last and j + ahead >= QUAD):
                            maximum(g + ahead, (j + ahead) % 2, tile, first and j + ahead < 2)
                        if t == 3 and not early:
                            normalise_out(g - 1, first and j == 1)
                        if t == 6 and not (last and j == QUAD - 1):
                            spread_top(g + 1, (j + 1) % QUAD)

            for t in range(T):
                maximum(0, 0, t, True)
            spread_top(0, 0)
            for t in range(AHEAD - T):
                maximum(1, 1, t, True)
            passes(dve, body)
            low(T * QUAD * PASSES - 1, 1)
            copy_out(QUAD * PASSES - 1, False)
            normalise_out(QUAD * PASSES - 1, False)

        @block.tensor
        def _(pe):
            pe.wait_ge(ones_done, 3 + QUAD + 1)

            def query_scores(g, n, j, t, first):
                if t == 0:
                    pe.wait_ge(loaded[j], 64 * (n + 1))
                if not (first and t == 0):
                    pe.wait_ge(max_done, T * g + t)
                for half in range(2):
                    last = pe.matmul(q_scores[:, half, :], q_stack[j][0:STACK, t * P:(t + 1) * P],
                                     k_stack[j][0:STACK, half * TB:(half + 1) * TB], start=True, stop=True)
                last.then_inc(a_done, 1)

            def turn_top(g, buffer, first):
                pe.wait_ge(max_done, T * (g + 1))
                if not first:
                    pe.wait_ge(parts_done, 2 * (g - 1))
                pe.transpose(turned[0:STACK + T, 0, 0:P], top[buffer][:], ident[:]).then_inc(top_turned, 1)

            def key_scores(g, j, t, first):
                if t == 0:
                    pe.wait_ge(top_done, g + 1)
                if not (first and t == 0):
                    pe.wait_ge(exp_done, T * g + t)
                for half in range(2):
                    last = pe.matmul(k_scores[:, half, :], k_stack[j][0:STACK + T, t * P:(t + 1) * P],
                                     q_stack[j][0:STACK + T, half * TB:(half + 1) * TB], start=True, stop=True)
                last.then_inc(b_done, 1)

            def output(g, buffer, t, first):
                at = T * g + t
                if t == 0:
                    pe.wait_ge(values_ready, g + 1)
                    if not first:
                        pe.wait_ge(copied_act, g)
                        pe.wait_ge(copied_dve, g)
                pe.wait_ge(hi_done, at + 1)
                pe.wait_ge(lo_dve, at + 1)
                pe.wait_ge(lo_pool, at + 1)
                for which, part in enumerate((p_hi, p_lo)):
                    for half in range(2):
                        last = pe.matmul(out_ps[half][0:OUT_COLS, :], head_values[:, buffer, t, :],
                                         part[:, t % 2, half * TB:(half + 1) * TB],
                                         start=(t == 0 and which == 0), stop=(t == T - 1 and which == 1))
                last.then_inc(out_done, 1)

            def turn_out(g):
                pe.wait_ge(copied_act, g + 1)
                pe.wait_ge(copied_dve, g + 1)
                for t in range(T):
                    half, at = divmod(t, T // 2)
                    last = pe.transpose(turned[:, half, at * OUT_COLS:(at + 1) * OUT_COLS],
                                        out_t[0:OUT_COLS, half, at * P:(at + 1) * P], ident[0:OUT_COLS, 0:OUT_COLS])
                last.then_inc(out_turned, 1)

            def body(n, first, last):
                for j in range(QUAD):
                    g = QUAD * n + j
                    early = first and j == 0
                    for t in range(T):
                        ahead, tile = divmod(t + AHEAD, T)
                        if not (last and j + ahead >= QUAD):
                            query_scores(g + ahead, n + (j + ahead) // QUAD, (j + ahead) % QUAD, tile, False)
                        if t == 6 and not (last and j == QUAD - 1):
                            turn_top(g + 1, (j + 1) % 2, early)
                        if not (last and j == QUAD - 1 and t == T - 1):
                            key_scores(g + (t + 1) // T, (j + (t + 1) // T) % QUAD, (t + 1) % T, False)
                        if not (early and t == 0):
                            output(g + (t - 1) // T, (j + (t - 1) // T) % 2, (t - 1) % T, early)
                        if t == 2 and not early:
                            turn_out(g - 1)

            for t in range(T):
                query_scores(0, 0, 0, t, True)
            turn_top(0, 0, True)
            for t in range(AHEAD - T):
                query_scores(1, 0, 1, t, False)
            key_scores(0, 0, 0, True)
            passes(pe, body)
            output(QUAD * PASSES - 1, 1, T - 1, False)
            turn_out(QUAD * PASSES - 1)


def project_out(nc, prefix, stream, ident, mixed, w_out, width):
    kts = width // P
    with Scope(nc, prefix) as s:
        w32 = s.sb("w32", [P, kts, DIM])
        w_hi, w_lo = s.sb("w_hi", [P, kts, DIM], F32R), s.sb("w_lo", [P, kts, DIM], F32R)
        source = s.sb("source", [P, 2, width])
        x_hi, x_lo = s.sb("x_hi", [P, 2, kts, P], F32R), s.sb("x_lo", [P, 2, kts, P], F32R)
        turned = [s.ps(f"turned{b}", [P, kts, P]) for b in range(2)]
        out_ps = [s.ps(f"out{b}", [P, DIM]) for b in range(2)]
        arrived, w_hi_done, w_lo_done = s.sem("arrived"), s.sem("w_hi_done"), s.sem("w_lo_done")
        source_done, turned_done = s.sem("source_done"), s.sem("turned_done")
        hi_done, lo_done, out_done, added = (s.sem(x) for x in ("hi_done", "lo_done", "out_done", "added"))
        block = s.block()

        @block.sync
        def _(sp):
            sp.dma_start(w32[:], w_out.rearrange("(k p) n -> p k n", p=P)).then_inc(arrived, 16)

        @block.gpsimd
        def _(pool):
            with pool.Fori(0, BATCH) as sequence:
                with pool.Fori(0, QTILES // 2) as pair:
                    for b in range(2):
                        tile = 2 * pair + b
                        pool.wait_ge(turned_done, QTILES * sequence + tile + 1)
                        src = mixed[:, bass.ts(sequence, QUADS), bass.ds(tile, 1), :].rearrange("p q o d -> p (q o) d")
                        pool.tensor_copy(source[:, b, :].rearrange("p (q d) -> p q d", q=QUADS), src)\
                            .then_inc(source_done, 1)

        @block.scalar
        def _(act):
            act.wait_ge(arrived, 16)
            act.copy(w_hi[:], w32[:]).then_inc(w_hi_done, 1)
            with act.Fori(0, TILES // 2) as i:
                for b in range(2):
                    act.wait_ge(turned_done, 2 * i + b + 3)
                    act.wait_ge(out_done, 2 * i + b + 1)
                    act.copy(x_hi[:, b], turned[b][:]).then_inc(hi_done, 1)

        @block.vector
        def _(dve):
            dve.wait_ge(w_hi_done, 1)
            dve.tensor_tensor(w_lo[:], w32[:], w_hi[:].bitcast(F32), ALU.subtract).then_inc(w_lo_done, 1)
            dve.sem_inc(lo_done, 2)
            dve.sem_inc(added, 2)
            with dve.Fori(0, TILES // 2) as i:
                for b in range(2):
                    dve.wait_ge(hi_done, 2 * i + b + 1)
                    dve.tensor_tensor(x_lo[:, b], turned[b][:], x_hi[:, b].bitcast(F32),
                                      ALU.subtract).then_inc(lo_done, 1)
                for b in range(2):
                    dve.wait_ge(out_done, 2 * i + b + 3)
                    tile = stream[:, bass.ds(2 * i + b, 1), :]
                    dve.tensor_tensor(tile, tile, out_ps[b][:], ALU.add).then_inc(added, 1)

        @block.tensor
        def _(pe):
            pe.sem_inc(turned_done, 2)
            pe.sem_inc(out_done, 2)
            pe.wait_ge(w_lo_done, 1)
            with pe.Fori(0, TILES // 2) as i:
                for b in range(2):
                    pe.wait_ge(source_done, 2 * i + b + 1)
                    pe.wait_ge(lo_done, 2 * i + b + 1)
                    for k in range(kts):
                        last = pe.transpose(turned[b][:, k, :], source[:, b, k * P:(k + 1) * P], ident[:])
                    last.then_inc(turned_done, 1)
                for b in range(2):
                    pe.wait_ge(lo_done, 2 * i + b + 3)
                    pe.wait_ge(added, 2 * i + b + 1)
                    for k in range(kts):
                        last = matmul3(pe, out_ps[b][:], x_hi[:, b, k, :], x_lo[:, b, k, :],
                                       w_hi[:, k, :], w_lo[:, k, :], k == 0, k == kts - 1)
                    last.then_inc(out_done, 1)


def latent_attention(nc, stream, ident, w_down, w_value, w_up, cos_sin, w_out):
    rotated = nc.dram_tensor("rotated", (BATCH * QUADS, 2, P, SEQ), F32).ap()
    with Scope(nc, "la") as keep:
        values = keep.sb("values", [P, BATCH * QUADS, QTILES, QUAD, 2 * HEAD_DIM1], F32R)
        with Scope(nc, "lal") as l:
            lat_hi, lat_lo = l.sb("lat_hi", [P, TOKENS], F32R), l.sb("lat_lo", [P, TOKENS], F32R)
            with Scope(nc, "laf") as f:
                feat_hi, feat_lo = f.sb("feat_hi", [P, KT, TOKENS], F32R), f.sb("feat_lo", [P, KT, TOKENS], F32R)
                normalise(nc, "n1a", stream, ident, feat_hi, feat_lo, feature_tiles_plain)
                latents(nc, feat_hi, feat_lo, w_down, w_value, lat_hi, lat_lo, values)
            rotated_heads(nc, lat_hi, lat_lo, w_up, cos_sin, rotated)
        mixed = keep.sb("mixed", [P, BATCH * QUADS, QTILES, QUAD * HEAD_DIM1])
        softmax_heads(nc, ident, values, rotated, mixed)
        project_out(nc, "po1", stream, ident, mixed, w_out, DIM)


SPARSE_HIDDEN = 2048
SPARSE_GROUP = 4 * P
SPARSE_GROUPS = SPARSE_HIDDEN // SPARSE_GROUP


def sparse_feed_forward(nc, stream, feat_hi, feat_lo, weights):
    with Scope(nc, "sp") as s:
        WIDE = 4 * DIM
        staged = [s.sb(f"staged{b}", [P, WIDE]) for b in range(2)]
        w_hi = [s.sb(f"w_hi{q}", [P, WIDE], F32R) for q in range(3)]
        w_lo = [s.sb(f"w_lo{q}", [P, WIDE], F32R) for q in range(3)]
        silu = s.sb("silu", [P, 2, TB])
        hidden = s.sb("hidden", [P, 4, TB])
        size = s.sb("size", [P, 4, TB])
        beats = s.sb("beats", [P, 6, TB], BF16)
        wins = s.sb("wins", [P, 4, TB], BF16)
        h_hi = s.sb("h_hi", [P, 4, TB], F32R)
        h_lo = s.sb("h_lo", [P, 4, TB], F32R)
        gate_ps = [s.ps(f"gate{b}", [P, TB]) for b in range(2)]
        up_ps = [s.ps(f"up{b}", [P, TB]) for b in range(2)]
        down_ps = [s.ps(f"down{b}", [P, DIM]) for b in range(SUB)]

        arrived = [s.sem(f"arrived{q}") for q in range(3)]
        w_hi_done, w_lo_done = s.sem("w_hi_done"), s.sem("w_lo_done")
        gate_done, up_done = s.sem("gate_done"), s.sem("up_done")
        silu_done, product_done, size_done = s.sem("silu_done"), s.sem("product_done"), s.sem("size_done")
        beats_done, half_done, wins_done, kept = (s.sem(x) for x in ("beats_done", "half_done", "wins_done", "kept"))
        h_hi_done, h_lo_done = s.sem("h_hi_done"), s.sem("h_lo_done")
        down_done, added = s.sem("down_done"), s.sem("added")
        block = s.block()

        @block.sync
        def _(sp):
            def load(group, part, slot):
                sp.dma_start(staged[slot][:], weights[bass.ds(group, 1), part, :, :]
                             .rearrange("g p c -> (g p) c")).then_inc(arrived[part], 16)

            load(0, 0, 0)
            load(0, 1, 1)
            for g in range(SPARSE_GROUPS - 1):
                sp.wait_ge(w_lo_done, 3 * g + 1)
                load(g, 2, 0)
                sp.wait_ge(w_lo_done, 3 * g + 2)
                load(g + 1, 1, 1)
                sp.wait_ge(w_lo_done, 3 * g + 3)
                load(g + 1, 0, 0)
            sp.wait_ge(w_lo_done, 3 * (SPARSE_GROUPS - 1) + 1)
            load(SPARSE_GROUPS - 1, 2, 0)

        @block.vector
        def _(dve):
            dve.sem_inc(added, SUB)
            dve.sem_inc(product_done, 2)
            dve.sem_inc(h_lo_done, 1)

            def low_weights(g, part):
                dve.wait_ge(w_hi_done, 3 * g + part + 1)
                dve.tensor_tensor(w_lo[part][:], staged[part % 2][:], w_hi[part][:].bitcast(F32),
                                  ALU.subtract).then_inc(w_lo_done, 1)

            def add(n, tb):
                for j in range(SUB):
                    dve.wait_ge(down_done, SUB * (n + 1) + j + 1)
                    tile = stream[:, tb * SUB + j, :]
                    dve.tensor_tensor(tile, tile, down_ps[j][:], ALU.add).then_inc(added, 1)

            def body(g, first, last):
                for tb in range(BLOCKS):
                    n = BLOCKS * g + tb
                    dve.wait_ge(h_lo_done, n + 1)
                    for r in range(4):
                        dve.wait_ge(up_done, 4 * n + r + 1)
                        dve.wait_ge(silu_done, 4 * n + r + 1)
                        dve.tensor_tensor(hidden[:, r, :], silu[:, r % 2, :], up_ps[r % 2][:],
                                          ALU.mult).then_inc(product_done, 1)
                    if tb == BLOCKS - 1 and not last:
                        low_weights(g + 1, 0)
                        low_weights(g + 1, 1)
                    dve.wait_ge(size_done, 4 * n + 4)
                    for a, at in ((0, 0), (1, 3), (2, 5)):
                        count = 3 - a
                        dve.tensor_tensor(beats[:, at:at + count, :],
                                          size[:, a:a + 1, :].broadcast_to([P, count, TB]),
                                          size[:, a + 1:4, :], ALU.is_ge).then_inc(beats_done, 1)
                    dve.wait_ge(beats_done, 3 * n + 3)
                    for r, (x, y, op) in enumerate(((0, 1, ALU.add), (3, 4, ALU.add), (5, 1, ALU.subtract),
                                                    (2, 4, ALU.add))):
                        dve.tensor_tensor(wins[:, r, :], beats[:, x, :], beats[:, y, :], op).then_inc(half_done, 1)
                    for r, (x, op) in enumerate(((2, ALU.add), (0, ALU.subtract), (3, ALU.subtract), (5, ALU.add))):
                        dve.wait_ge(half_done, 4 * n + r + 1)
                        dve.tensor_tensor(wins[:, r, :], wins[:, r, :], beats[:, x, :], op).then_inc(wins_done, 1)
                    for r, (limit, op) in enumerate(((2.0, ALU.is_ge), (1.0, ALU.is_ge), (0.0, ALU.is_ge),
                                                     (1.0, ALU.is_le))):
                        dve.wait_ge(wins_done, 4 * n + r + 1)
                        dve.scalar_tensor_tensor(out=hidden[:, r, :], in0=wins[:, r, :], scalar=limit,
                                                 in1=hidden[:, r, :], op0=op, op1=ALU.mult).then_inc(kept, 1)
                    if not (first and tb == 0):
                        add(n - 1, (tb - 1) % BLOCKS)
                    if tb == 0:
                        low_weights(g, 2)
                    dve.wait_ge(h_hi_done, n + 1)
                    dve.tensor_tensor(h_lo[:], hidden[:], h_hi[:].bitcast(F32), ALU.subtract).then_inc(h_lo_done, 1)

            low_weights(0, 0)
            low_weights(0, 1)
            body(0, True, False)
            with dve.Fori(1, SPARSE_GROUPS - 1) as g:
                body(g, False, False)
            body(SPARSE_GROUPS - 1, False, True)
            add(SPARSE_GROUPS * BLOCKS - 1, BLOCKS - 1)

        @block.scalar
        def _(act):
            act.preload_act_table(ACT.Silu)

            def high_weights(g, part):
                act.wait_ge(arrived[part], 16 * g + 16)
                act.copy(w_hi[part][:], staged[part % 2][:]).then_inc(w_hi_done, 1)

            def body(g, last):
                for tb in range(BLOCKS):
                    n = BLOCKS * g + tb

                    def magnitude(r):
                        act.wait_ge(product_done, 4 * n + r + 3)
                        act.activation(size[:, r, :], hidden[:, r, :], ACT.Abs).then_inc(size_done, 1)

                    for r in range(4):
                        act.wait_ge(gate_done, 4 * n + r + 1)
                        act.wait_ge(product_done, 4 * n + r + 1)
                        act.activation(silu[:, r % 2, :], gate_ps[r % 2][:], ACT.Silu).then_inc(silu_done, 1)
                        if r:
                            magnitude(r - 1)
                    magnitude(3)
                    if tb == BLOCKS - 1 and not last:
                        act.wait_ge(up_done, 4 * n + 4)
                        high_weights(g + 1, 0)
                        high_weights(g + 1, 1)
                    act.wait_ge(down_done, SUB * (n + 1))
                    if tb == 0:
                        high_weights(g, 2)
                    act.wait_ge(kept, 4 * n + 4)
                    act.copy(h_hi[:], hidden[:]).then_inc(h_hi_done, 1)

            high_weights(0, 0)
            high_weights(0, 1)
            with act.Fori(0, SPARSE_GROUPS - 1) as g:
                body(g, False)
            body(SPARSE_GROUPS - 1, True)

        @block.tensor
        def _(pe):
            pe.sem_inc(down_done, SUB)

            def gate_up(n, g, tb):
                pe.wait_ge(w_hi_done, 3 * g + 2)
                pe.wait_ge(w_lo_done, 3 * g + 2)
                cols = slice(tb * TB, (tb + 1) * TB)
                for r in range(4):
                    for part, ps in ((0, gate_ps[r % 2]), (1, up_ps[r % 2])):
                        if part == 0 and not (isinstance(n, int) and 4 * n + r < 2):
                            pe.wait_ge(silu_done, 4 * n + r - 1)
                        if part == 1:
                            pe.wait_ge(product_done, 4 * n + r + 1)
                        for kt in range(KT):
                            at = kt * DIM + r * P
                            last = matmul3(pe, ps[:], w_hi[part][:, at:at + P], w_lo[part][:, at:at + P],
                                           feat_hi[:, kt, cols], feat_lo[:, kt, cols], kt == 0, kt == KT - 1)
                        last.then_inc((gate_done, up_done)[part], 1)

            def down(n, g, tb):
                if tb == 0:
                    pe.wait_ge(w_lo_done, 3 * g + 3)
                pe.wait_ge(h_lo_done, n + 2)
                for j in range(SUB):
                    pe.wait_ge(added, SUB * n + j + 1)
                    rows = slice(j * P, (j + 1) * P)
                    for r in range(4):
                        at = slice(r * DIM, (r + 1) * DIM)
                        last = matmul3(pe, down_ps[j][:], h_hi[:, r, rows], h_lo[:, r, rows],
                                       w_hi[2][:, at], w_lo[2][:, at], r == 0, r == 3)
                    last.then_inc(down_done, 1)

            def body(g, last):
                for tb in range(BLOCKS):
                    n = BLOCKS * g + tb
                    nxt = tb + 1
                    if not (last and nxt == BLOCKS):
                        gate_up(n + 1, g + nxt // BLOCKS, nxt % BLOCKS)
                    down(n, g, tb)

            gate_up(0, 0, 0)
            with pe.Fori(0, SPARSE_GROUPS - 1) as g:
                body(g, False)
            body(SPARSE_GROUPS - 1, True)


def four_sublayers(nc, hidden, ident_in, masks_in, w_qkv, conv_w, w_gate, head_rows, w_out0, codes, scales,
                   w_down1, w_value1, w_up1, cos_sin, w_out1, w_sparse, out):
    with Scope(nc, "k") as s:
        stream = s.sb("stream", [P, TILES, DIM])
        ident = s.sb("ident", [P, P])
        arrived, stored = s.sem("arrived"), s.sem("stored")
        with Scope(nc, "l0") as l0:
            mask = l0.sb("mask", [P, N_MASKS, P])
            with nc.Block() as block:
                @block.sync
                def _(sp):
                    sp.dma_start(stream[:], hidden.rearrange("(i p) d -> p i d", p=P)).then_inc(arrived, 16)
                    sp.dma_start(ident[:], ident_in).then_inc(arrived, 16)
                    sp.dma_start(mask[:], masks_in).then_inc(arrived, 16)
                    sp.wait_ge(arrived, 48)
            delta_attention(nc, stream, ident, mask, hidden, w_qkv, conv_w, w_gate, head_rows, w_out0)
        with Scope(nc, "f0") as f:
            feat_hi, feat_lo = f.sb("feat_hi", [P, KT, TOKENS], F32R), f.sb("feat_lo", [P, KT, TOKENS], F32R)
            normalise(nc, "n0f", stream, ident, feat_hi, feat_lo, feature_tiles_nibbles)
            nvfp4_feed_forward(nc, stream, feat_hi, feat_lo, codes, scales)
        latent_attention(nc, stream, ident, w_down1, w_value1, w_up1, cos_sin, w_out1)
        with Scope(nc, "f1") as f:
            feat_hi, feat_lo = f.sb("feat_hi", [P, KT, TOKENS], F32R), f.sb("feat_lo", [P, KT, TOKENS], F32R)
            normalise(nc, "n1f", stream, ident, feat_hi, feat_lo, feature_tiles_plain)
            sparse_feed_forward(nc, stream, feat_hi, feat_lo, w_sparse)
        with nc.Block() as block:
            @block.sync
            def _(sp):
                sp.dma_start(out.rearrange("(i p) d -> p i d", p=P), stream[:]).then_inc(stored, 16)
                sp.wait_ge(stored, 16)


def rotary_tables():
    inverse = (1.0 / 10000.0 ** (np.arange(0, HALF, 2, dtype=np.float32) / HALF)).astype(np.float32)
    angle = (np.arange(SEQ, dtype=np.float32)[:, None] * inverse[None]).astype(np.float32)
    angle = np.concatenate([angle, angle], -1).T
    sign = np.where(np.arange(HALF) < HALF // 2, -1, 1)[:, None]
    table = np.stack([np.tile(np.cos(angle), (P // HALF, 1)), np.tile(np.sin(angle) * sign, (P // HALF, 1))], 1)
    table = table.astype(np.float32)
    table[:P // 2] *= HALF ** -0.5
    return np.ascontiguousarray(table)


def delta_layout(x):
    names = "qkv"
    w = np.stack([x[f"L0_attn_W{n}"] for n in names]).reshape(3, CT, P, KT, P)
    conv = np.stack([x[f"L0_attn_conv_{n}"] for n in names]).reshape(3, CT, P, CONV)
    gate = np.concatenate([x["L0_attn_Wg"].T, x["L0_attn_Wb"].T, x["L0_attn_Wa"].T], 1)
    return (w.transpose(1, 0, 4, 3, 2).reshape(CT, 3, P, KT * P), conv.transpose(2, 1, 0, 3).reshape(P, CT, 3 * CONV),
            gate.reshape(KT, P, GATE_COLS),
            np.concatenate([np.tile(x["L0_attn_o_norm_w"], HEADS0), x["L0_attn_dt_bias"], x["L0_attn_A_log"]]),
            x["L0_attn_Wo"].T)


def nvfp4_layout(x):
    def rows(a):
        inner = a.shape[1] // 2
        a = a.reshape(FP4_GROUPS, P, 2, 2, inner)
        return a.transpose(0, 4, 3, 2, 1).reshape(FP4_GROUPS, inner, 2 * FP4_GROUP)

    def down(a):
        return a.T.reshape(FP4_GROUPS, a.shape[1] // FP4_GROUPS, DIM)

    return tuple(np.concatenate([rows(x[f"L0_ffn_gate_{n}"]), rows(x[f"L0_ffn_up_{n}"]), down(x[f"L0_ffn_down_{n}"])], 2)
                 for n in ("W_packed", "scales"))


def latent_up_layout(x):
    swapped = [(d + HALF // 2) % HALF for d in range(HALF)]
    up = np.zeros((P, QUADS, 2, P), np.float32)
    for side, name in enumerate(("L1_attn_wq_u", "L1_attn_wk_u")):
        w = x[name].reshape(LATENT, QUADS, QUAD, HALF)
        at = slice(side * LATENT, (side + 1) * LATENT)
        for which, cols in enumerate((w, w[..., swapped])):
            up[at, :, which, at] = cols.reshape(LATENT, QUADS, QUAD * HALF)
    return up.reshape(P, QUADS, 2 * P).transpose(1, 0, 2)


def sparse_layout(x):
    def into(w):
        w = w.reshape(KT, P, SPARSE_GROUPS, P, 4)
        return w.transpose(2, 1, 0, 4, 3).reshape(SPARSE_GROUPS, 1, P, 4 * DIM)
    down = x["L1_ffn_w_down"].reshape(SPARSE_GROUPS, 1, P, 4 * DIM)
    return np.concatenate([into(x["L1_ffn_w_gate"]), into(x["L1_ffn_w_up"]), down], 1)


def kernel(**inputs):
    import concourse.bacc as bacc
    from concourse.bass_utils import run_bass_kernel_spmd

    x = {name: np.asarray(a) for name, a in inputs.items()}
    w_qkv, conv_w, w_gate, head_rows, w_out0 = delta_layout(x)
    codes, scales = nvfp4_layout(x)
    arrays = {
        "hidden": x["L0_attn_hidden_states"].reshape(TOKENS, DIM),
        "ident_in": np.eye(P, dtype=np.float32), "masks_in": masks(),
        "w_qkv": w_qkv, "conv_w": conv_w, "w_gate": w_gate, "head_rows": head_rows, "w_out0": w_out0,
        "codes": codes, "scales": scales,
        "w_down1": np.concatenate([x["L1_attn_wq_d"], x["L1_attn_wkv_d"]], 1), "w_value1": x["L1_attn_wv_u"],
        "w_up1": latent_up_layout(x), "cos_sin": rotary_tables(), "w_out1": x["L1_attn_wo"],
        "w_sparse": sparse_layout(x),
    }
    arrays = {name: np.ascontiguousarray(a) for name, a in arrays.items()}
    nc = bacc.Bacc("TRN2", target_bir_lowering=False, num_devices=1)
    args = {name: nc.dram_tensor(name, a.shape, mybir.dt.from_np(a.dtype), kind="ExternalInput").ap()
            for name, a in arrays.items()}
    out = nc.dram_tensor("out", (TOKENS, DIM), F32, kind="ExternalOutput").ap()
    four_sublayers(nc, out=out, **args)
    result = run_bass_kernel_spmd(nc, [arrays], core_ids=[0])
    return result.results[0]["out"].reshape(BATCH, SEQ, DIM)
```

```python
from contextlib import ExitStack

import numpy as np
import concourse.bass as bass
from concourse import mybir

F32 = mybir.dt.float32
F32R = mybir.dt.float32r
F16 = mybir.dt.float16
BF16 = mybir.dt.bfloat16
I32 = mybir.dt.int32
ALU = mybir.AluOpType
ACT = mybir.ActivationFunctionType
AX = mybir.AxisListType

P = 128
BATCH, SEQ, DIM = 2, 1024, 512
TOKENS = BATCH * SEQ
TILES = TOKENS // P
KT = DIM // P
TB = 512
BLOCKS = TOKENS // TB
SUB = TB // P
EPS = 1e-5


class Scope:

    def __init__(self, nc, prefix, give_back=False):
        self.nc, self.prefix, self.stack = nc, prefix, ExitStack()
        self.give_back, self.sems = give_back, []

    def __enter__(self):
        self.stack.__enter__()
        return self

    def __exit__(self, *a):
        self.stack.__exit__(*a)
        if self.give_back:
            self.nc.clear_and_free_semaphores(self.sems)
            self.nc.all_engine_barrier()

    def sb(self, name, shape, dt=F32):
        return self.stack.enter_context(self.nc.sbuf_tensor(f"{self.prefix}_{name}", shape, dt))

    def ps(self, name, shape, dt=F32):
        return self.stack.enter_context(self.nc.psum_tensor(f"{self.prefix}_{name}", shape, dt))

    def sem(self, name):
        self.sems.append(self.nc.alloc_semaphore(name=f"{self.prefix}_{name}"))
        return self.sems[-1]

    def block(self):
        return self.stack.enter_context(self.nc.Block())


def matmul3(pe, out, w_hi, w_lo, x_hi, x_lo, start, stop):
    pe.matmul(out, w_hi, x_hi, start=start, stop=False)
    pe.matmul(out, w_hi, x_lo, start=False, stop=False)
    return pe.matmul(out, w_lo, x_hi, start=False, stop=stop)


def feature_tiles_plain(kt):
    return slice(kt * P, (kt + 1) * P)


def feature_tiles_nibbles(kt):
    return slice(2 * P * (kt // 2) + kt % 2, 2 * P * (kt // 2 + 1), 2)


def normalise(nc, prefix, stream, ident, feat_hi, feat_lo, feature_tiles, arrivals=None,
              prefetch=None):
    with Scope(nc, prefix) as s:
        raw = s.sb("raw_stats", [P, TILES, 6])
        mean, gap, var = (s.sb(x, [P, TILES]) for x in ("mean", "gap", "var"))
        power = s.sb("power", [P, TILES])
        rstd = s.sb("rstd", [P, TILES])
        BUFFERS = 4
        normed = s.sb("normed", [P, BUFFERS, DIM])
        turned = [s.ps(f"turned{b}", [P, KT, P]) for b in range(BUFFERS)]
        stats_done, moments, rstd_done = s.sem("stats_done"), s.sem("moments"), s.sem("rstd_done")
        const_ready = s.sem("const_ready")
        normed_done, turned_done = s.sem("normed_done"), s.sem("turned_done")
        hi_done, lo_done = s.sem("hi_done"), s.sem("lo_done")
        block = s.block()

        @block.sync
        def _(sp):
            if prefetch:
                prefetch(sp)

        @block.gpsimd
        def _(pool):
            pool.memset(power[:], -0.5).then_inc(const_ready, 1)
            pool.wait_ge(const_ready, 1)
            pool.wait_ge(moments, 7)
            pool.tensor_tensor(rstd[:], var[:], power[:], ALU.pow).then_inc(rstd_done, 1)

        @block.vector
        def _(dve):
            for q in range(BLOCKS):
                if arrivals:
                    dve.wait_ge(arrivals[0][q], 16)
                with dve.Fori(q * SUB, (q + 1) * SUB) as i:
                    dve.bn_stats(raw[:, bass.ds(i, 1), :], stream[:, bass.ds(i, 1), :]).then_inc(stats_done, 1)
            dve.wait_ge(stats_done, TILES)
            dve.tensor_tensor(mean[:], raw[:, :, 1], raw[:, :, 4], ALU.add).then_inc(moments, 1)
            dve.tensor_tensor(gap[:], raw[:, :, 1], raw[:, :, 4], ALU.subtract).then_inc(moments, 1)
            dve.tensor_tensor(var[:], raw[:, :, 2], raw[:, :, 5], ALU.add).then_inc(moments, 1)
            dve.wait_ge(moments, 3)
            dve.tensor_scalar(mean[:], mean[:], 0.5, None, ALU.mult).then_inc(moments, 1)
            dve.scalar_tensor_tensor(out=gap[:], in0=gap[:], scalar=0.25, in1=gap[:],
                                     op0=ALU.mult, op1=ALU.mult).then_inc(moments, 1)
            dve.tensor_scalar(var[:], var[:], 1.0 / DIM, EPS, ALU.mult, ALU.add).then_inc(moments, 1)
            dve.wait_ge(moments, 6)
            dve.tensor_tensor(var[:], var[:], gap[:], ALU.add).then_inc(moments, 1)
            dve.wait_ge(rstd_done, 1)
            dve.sem_inc(lo_done, BUFFERS)

            def scale(i, b):
                dve.wait_ge(turned_done, i + 1)
                dve.tensor_scalar(normed[:, b, :], stream[:, bass.ds(i, 1), :],
                                  mean[:, bass.ds(i, 1)], rstd[:, bass.ds(i, 1)],
                                  ALU.subtract, ALU.mult).then_inc(normed_done, 1)

            def low(i, b):
                dve.wait_ge(hi_done, i + 1)
                cols = bass.ts(i, P)
                dve.tensor_tensor(feat_lo[:, :, cols], turned[b][:], feat_hi[:, :, cols].bitcast(F32),
                                  ALU.subtract).then_inc(lo_done, 1)

            def body(i, last):
                for pair in range(2):
                    for b in range(2):
                        ahead = 2 * pair + 2 + b
                        if not (last and ahead >= BUFFERS):
                            scale(BUFFERS * i + ahead, ahead % BUFFERS)
                    for b in range(2):
                        low(BUFFERS * i + 2 * pair + b, 2 * pair + b)

            scale(0, 0)
            scale(1, 1)
            with dve.Fori(0, TILES // BUFFERS - 1) as i:
                body(i, False)
            body(TILES // BUFFERS - 1, True)

        @block.tensor
        def _(pe):
            pe.sem_inc(turned_done, BUFFERS)
            if arrivals:
                pe.wait_ge(arrivals[1], arrivals[2])
            with pe.Fori(0, TILES // BUFFERS) as i:
                for b in range(BUFFERS):
                    pe.wait_ge(normed_done, BUFFERS * i + b + 1)
                    pe.wait_ge(lo_done, BUFFERS * i + b + 1)
                    for kt in range(KT):
                        last = pe.transpose(turned[b][:, kt, :], normed[:, b, feature_tiles(kt)], ident[:])
                    last.then_inc(turned_done, 1)

        @block.scalar
        def _(act):
            with act.Fori(0, TILES // BUFFERS) as i:
                for b in range(BUFFERS):
                    act.wait_ge(turned_done, BUFFERS * i + b + BUFFERS + 1)
                    act.copy(feat_hi[:, :, bass.ts(BUFFERS * i + b, P)], turned[b][:]).then_inc(hi_done, 1)


FP4_GROUP = 2 * P
FP4_HIDDEN = 4096
FP4_GROUPS = FP4_HIDDEN // FP4_GROUP
FP4_BLOCK = 32
FP4_COLS = 2 * 2 * FP4_GROUP + DIM


def load_codes(sp, staging, codes, scales, group):
    words, scale, loaded = staging
    sp.dma_start(words[:], codes[bass.ds(group, 1), :, :].rearrange("g p c -> (g p) c")).then_inc(loaded, 16)
    src = scales[bass.ds(group, 1), :, :]
    rows = bass.AP(tensor=src.tensor, offset=src.offset,
                   ap=[[FP4_COLS, P // 16], [0, 16], [1, FP4_COLS]])
    sp.dma_start(scale[:], rows).then_inc(loaded, 16)


def nvfp4_feed_forward(nc, stream, feat_hi, feat_lo, codes, scales, staging):
    words, scale, loaded = staging
    with Scope(nc, "fp4") as s:
        bits = s.sb("bits", [P, FP4_COLS], I32)
        weight = s.sb("weight", [P, 2, FP4_COLS])
        w_hi = [s.sb(f"w_hi{b}", [P, 2, FP4_COLS], F32R) for b in range(2)]
        w_lo = [s.sb(f"w_lo{b}", [P, 2, FP4_COLS], F32R) for b in range(2)]
        gelu = s.sb("gelu", [P, 2, TB])
        hidden = s.sb("hidden", [P, 2, TB])
        h_hi = s.sb("h_hi", [P, 2, 2, TB], F32R)
        h_lo = s.sb("h_lo", [P, 2, 2, TB], F32R)
        gate_ps = [s.ps(f"gate{b}", [P, TB]) for b in range(2)]
        up_ps = [s.ps(f"up{b}", [P, TB]) for b in range(2)]
        down_ps = [s.ps(f"down{b}", [P, DIM]) for b in range(SUB)]

        dve_step = s.sem("dve_step")
        w_hi_done, w_lo_done = s.sem("w_hi_done"), s.sem("w_lo_done")
        gate_done, up_done = s.sem("gate_done"), s.sem("up_done")
        gelu_done, product_done = s.sem("gelu_done"), s.sem("product_done")
        h_hi_done, h_lo_done = s.sem("h_hi_done"), s.sem("h_lo_done")
        down_done, added = s.sem("down_done"), s.sem("added")
        block = s.block()
        LOOPS = FP4_GROUPS // 2
        STEPS = 2 * BLOCKS

        @block.sync
        def _(sp):
            with sp.Fori(0, FP4_GROUPS - 1) as group:
                sp.wait_ge(dve_step, 6 * group + 7)
                load_codes(sp, staging, codes, scales, group + 1)

        def bits_of(dve, nibble, n):
            dve.wait_ge(dve_step, 3 * n + 1)
            dve.tensor_scalar(bits[:], words[:], 28 - 4 * nibble, 3,
                              ALU.logical_shift_left, ALU.arith_shift_right).then_inc(dve_step, 1)
            dve.wait_ge(dve_step, 3 * n + 2)
            dve.tensor_scalar(bits[:], bits[:], 0x8E000000 - (1 << 32), None,
                              ALU.bitwise_and).then_inc(dve_step, 1)
            dve.wait_ge(dve_step, 3 * n + 3)
            dve.wait_ge(w_lo_done, n + 1)
            dve.scalar_tensor_tensor(out=weight[:, nibble, :], in0=bits[:].bitcast(F16)[:, 1::2],
                                     scalar=16384.0, in1=scale[:], op0=ALU.mult,
                                     op1=ALU.mult).then_inc(dve_step, 1)

        def low_weights(dve, group, b, nibble):
            n = 2 * group + nibble
            dve.wait_ge(w_hi_done, n + 3)
            dve.tensor_tensor(w_lo[b][:, nibble, :], weight[:, nibble, :],
                              w_hi[b][:, nibble, :].bitcast(F32), ALU.subtract).then_inc(w_lo_done, 1)

        @block.vector
        def _(dve):
            dve.sem_inc(dve_step, 1)
            dve.sem_inc(added, SUB)
            dve.sem_inc(product_done, 2)
            dve.sem_inc(h_lo_done, 2)
            dve.sem_inc(w_lo_done, 2)

            def prepare(group, nibble):
                if nibble == 0:
                    dve.wait_ge(loaded, 32 * group + 32)
                bits_of(dve, nibble, 2 * group + nibble)

            def add(n, tb):
                for j in range(SUB):
                    dve.wait_ge(down_done, SUB * (n + 2) + j + 1)
                    tile = stream[:, tb * SUB + j, :]
                    dve.tensor_tensor(tile, tile, down_ps[j][:], ALU.add).then_inc(added, 1)

            def body(it, first, last):
                for t in range(STEPS):
                    n = STEPS * it + t
                    b, tb = t // BLOCKS, t % BLOCKS
                    for c in range(2):
                        chunk = 2 * n + c
                        dve.wait_ge(up_done, chunk + 1)
                        dve.wait_ge(gelu_done, chunk + 1)
                        dve.wait_ge(h_lo_done, chunk + 1)
                        dve.tensor_tensor(hidden[:, c, :], gelu[:, c, :], up_ps[c][:],
                                          ALU.mult).then_inc(product_done, 1)
                    for c in range(2):
                        chunk = 2 * n + c
                        dve.wait_ge(h_hi_done, chunk + 3)
                        dve.tensor_tensor(h_lo[:, t % 2, c, :], hidden[:, c, :],
                                          h_hi[:, t % 2, c, :].bitcast(F32), ALU.subtract).then_inc(h_lo_done, 1)
                    if not (first and t == 0):
                        add(n - 1, (tb - 1) % BLOCKS)
                    if not (last and b == 1):
                        group = 2 * it + b + 1
                        if tb == 0:
                            dve.wait_ge(down_done, SUB * (2 + STEPS * it + BLOCKS * b))
                            prepare(group, 0)
                        if tb == 1:
                            low_weights(dve, group, 1 - b, 0)
                            prepare(group, 1)
                        if tb == 2:
                            low_weights(dve, group, 1 - b, 1)

            for nibble in range(2):
                prepare(0, nibble)
            for nibble in range(2):
                low_weights(dve, 0, 0, nibble)
            body(0, True, False)
            with dve.Fori(1, LOOPS - 1) as it:
                body(it, False, False)
            body(LOOPS - 1, False, True)
            add(STEPS * LOOPS - 1, BLOCKS - 1)

        @block.scalar
        def _(act):
            act.preload_act_table(ACT.Gelu_apprx_tanh)
            act.sem_inc(w_hi_done, 2)
            act.sem_inc(h_hi_done, 2)

            def high_weights(group, b, nibble):
                n = 2 * group + nibble
                act.wait_ge(dve_step, 3 * n + 4)
                act.copy(w_hi[b][:, nibble, :], weight[:, nibble, :]).then_inc(w_hi_done, 1)

            def body(it, last):
                for t in range(STEPS):
                    n = STEPS * it + t
                    b, tb = t // BLOCKS, t % BLOCKS
                    for c in range(2):
                        chunk = 2 * n + c
                        act.wait_ge(gate_done, chunk + 1)
                        act.wait_ge(product_done, chunk + 1)
                        act.activation(gelu[:, c, :], gate_ps[c][:], ACT.Gelu_apprx_tanh).then_inc(gelu_done, 1)
                    for c in range(2):
                        chunk = 2 * n + c
                        act.wait_ge(product_done, chunk + 3)
                        act.wait_ge(down_done, SUB * (n + 1))
                        act.copy(h_hi[:, t % 2, c, :], hidden[:, c, :]).then_inc(h_hi_done, 1)
                    if not (last and b == 1) and tb in (0, 1):
                        high_weights(2 * it + b + 1, 1 - b, tb)

            high_weights(0, 0, 0)
            high_weights(0, 0, 1)
            with act.Fori(0, LOOPS - 1) as it:
                body(it, False)
            body(LOOPS - 1, True)

        @block.tensor
        def _(pe):
            pe.sem_inc(down_done, 2 * SUB)

            def gate_up(n, group, b, tb):
                pe.wait_ge(w_hi_done, 2 * group + 4)
                pe.wait_ge(w_lo_done, 2 * group + 4)
                cols = slice(tb * TB, (tb + 1) * TB)
                for c in range(2):
                    for part, ps in ((0, gate_ps[c]), (1, up_ps[c])):
                        if part == 0 and not (isinstance(n, int) and n == 0):
                            pe.wait_ge(gelu_done, 2 * n + c - 1)
                        if part == 1:
                            pe.wait_ge(product_done, 2 * n + c + 1)
                        for kt in range(KT):
                            at = part * 2 * FP4_GROUP + (kt // 2) * FP4_GROUP + c * P
                            last = matmul3(pe, ps[:], w_hi[b][:, kt % 2, at:at + P], w_lo[b][:, kt % 2, at:at + P],
                                           feat_hi[:, kt, cols], feat_lo[:, kt, cols], kt == 0, kt == KT - 1)
                        last.then_inc((gate_done, up_done)[part], 1)

            def down(n, b, t):
                pe.wait_ge(h_hi_done, 2 * n + 4)
                pe.wait_ge(h_lo_done, 2 * n + 4)
                for j in range(SUB):
                    pe.wait_ge(added, SUB * n + j + 1)
                    rows = slice(j * P, (j + 1) * P)
                    for c in range(2):
                        last = matmul3(pe, down_ps[j][:], h_hi[:, t % 2, c, rows], h_lo[:, t % 2, c, rows],
                                       w_hi[b][:, c, 4 * FP4_GROUP:], w_lo[b][:, c, 4 * FP4_GROUP:],
                                       c == 0, c == 1)
                    last.then_inc(down_done, 1)

            def body(it, last):
                for t in range(STEPS):
                    n = STEPS * it + t
                    if not (last and t == STEPS - 1):
                        nxt = t + 1
                        gate_up(n + 1, 2 * it + nxt // BLOCKS, (nxt // BLOCKS) % 2, nxt % BLOCKS)
                    down(n, t // BLOCKS, t)

            gate_up(0, 0, 0, 0)
            with pe.Fori(0, LOOPS - 1) as it:
                body(it, False)
            body(LOOPS - 1, True)


HEADS0, HEAD_DIM0, CONV = 6, 64, 4
KEY = HEADS0 * HEAD_DIM0
CT = KEY // P
CHUNK = P
CHUNKS = SEQ // CHUNK
BH = BATCH * HEADS0
LOGITS = 2 * HEADS0
GATE_COLS = KEY + LOGITS
LEVELS = 6


def masks():
    r, c = np.arange(P)[:, None], np.arange(P)[None, :]
    below = [-((r // n % 2 == 1) & (c // n == r // n - 1)).astype(np.float32) for n in (1, 2, 4, 8, 16, 32, 64)]
    out = [r <= c, r > c, np.ones((P, P)), r < c] + [m.T for m in below]
    return np.ascontiguousarray(np.stack([np.asarray(m, np.float32) for m in out], 1))


UPTO, AFTER, ONES, BEFORE, PAIR_T, LEVEL0 = range(6)
N_MASKS = LEVEL0 + LEVELS


def project_conv(nc, feat_hi, feat_lo, w_qkv, conv_w, qkv, prefetch):
    with Scope(nc, "pc") as s:
        taps = s.sb("taps", [P, CT * 3 * CONV])
        w32 = [s.sb(f"w32_{q}", [P, KT * P]) for q in range(3)]
        w_hi = [s.sb(f"w_hi{q}", [P, KT * P], F32R) for q in range(3)]
        w_lo = [s.sb(f"w_lo{q}", [P, KT * P], F32R) for q in range(3)]
        padded = s.sb("padded", [P, 3, BATCH, CONV - 1 + SEQ])
        rows = [s.sb(f"rows{q}", [P, BATCH, SEQ]) for q in range(3)]
        banks = [s.ps(f"bank{b}", [P, TB]) for b in range(BLOCKS)]
        arrived_w = [s.sem(f"arrived_w{q}") for q in range(3)]
        stored = [s.sem(f"stored{q}") for q in range(3)]
        arrived = s.sem("arrived")
        zeroed = s.sem("zeroed")
        w_hi_done, w_lo_done = s.sem("w_hi_done"), s.sem("w_lo_done")
        product_done, copied = s.sem("product_done"), s.sem("copied")
        taps_done, silu_done = s.sem("taps_done"), s.sem("silu_done")
        block = s.block()

        @block.sync
        def _(sp):
            sp.dma_start(taps[:], conv_w.rearrange("p i t -> p (i t)")).then_inc(arrived, 16)
            prefetch(sp)
            for q in range(3):
                sp.sem_inc(stored[q], 16)
                sp.dma_start(w32[q][:], w_qkv[0, q]).then_inc(arrived_w[q], 16)
            for n in range(3 * CT):
                tile, q = divmod(n, 3)
                sp.wait_ge(silu_done, n + 1)
                sp.dma_start(qkv[CT * q + tile], rows[q][:].rearrange("p b t -> p (b t)")).then_inc(stored[q], 16)
                if tile < CT - 1:
                    sp.wait_ge(w_lo_done, n + 1)
                    sp.dma_start(w32[q][:], w_qkv[tile + 1, q]).then_inc(arrived_w[q], 16)
            for q in range(3):
                sp.wait_ge(stored[q], 16 * CT + 16)

        @block.gpsimd
        def _(pool):
            pool.memset(padded[:, :, :, 0:CONV - 1], 0.0).then_inc(zeroed, 1)

        @block.scalar
        def _(act):
            act.preload_act_table(ACT.Silu)
            act.sem_inc(copied, BLOCKS)

            def high_weights(tile, q):
                act.wait_ge(arrived_w[q], 16 * tile + 16)
                act.wait_ge(product_done, 4 * (3 * tile + q) + 4)
                act.copy(w_hi[q][:], w32[q][:]).then_inc(w_hi_done, 1)

            def silu(tile, q):
                act.wait_ge(taps_done, 4 * (3 * tile + q) + 16)
                act.activation(rows[q][:], rows[q][:], ACT.Silu).then_inc(silu_done, 1)

            def body(tile, first, last):
                for q in range(3):
                    n = 3 * tile + q
                    if not (last and q == 2):
                        high_weights(tile + (q == 2), (q + 1) % 3)
                    act.wait_ge(taps_done, 4 * n + 4)
                    for blk in range(BLOCKS):
                        act.wait_ge(product_done, 4 * n + blk + 13)
                        b, half = divmod(blk, SEQ // TB)
                        at = CONV - 1 + half * TB
                        act.copy(padded[:, q, b, at:at + TB], banks[blk][:]).then_inc(copied, 1)
                    if not (first and q == 0):
                        silu(tile - (q == 0), (q - 1) % 3)

            high_weights(0, 0)
            body(0, True, False)
            with act.Fori(1, CT - 1) as tile:
                body(tile, False, False)
            body(CT - 1, False, True)
            silu(CT - 1, 2)

        @block.vector
        def _(dve):
            dve.sem_inc(taps_done, 12)
            dve.wait_ge(arrived, 16)
            dve.wait_ge(zeroed, 1)

            def low_weights(tile, q):
                dve.wait_ge(w_hi_done, 3 * tile + q + 1)
                dve.tensor_tensor(w_lo[q][:], w32[q][:], w_hi[q][:].bitcast(F32),
                                  ALU.subtract).then_inc(w_lo_done, 1)

            def body(tile, last):
                for q in range(3):
                    n = 3 * tile + q
                    if not (last and q == 2):
                        low_weights(tile + (q == 2), (q + 1) % 3)
                    dve.wait_ge(copied, 4 * n + 8)
                    dve.wait_ge(stored[q], 16 * tile + 16)
                    row = rows[q][:]
                    for i in range(CONV):
                        at = 3 * CONV * tile + CONV * q + i
                        tap = taps[:, bass.ds(at, 1)]
                        src = padded[:, q, :, i:i + SEQ]
                        if i == 0:
                            dve.tensor_scalar(row, src, tap, None, ALU.mult).then_inc(taps_done, 1)
                        else:
                            dve.wait_ge(taps_done, 4 * n + 12 + i)
                            dve.scalar_tensor_tensor(out=row, in0=src, scalar=tap, in1=row,
                                                     op0=ALU.mult, op1=ALU.add).then_inc(taps_done, 1)

            low_weights(0, 0)
            with dve.Fori(0, CT - 1) as tile:
                body(tile, False)
            body(CT - 1, True)

        @block.tensor
        def _(pe):
            pe.sem_inc(product_done, 12)
            with pe.Fori(0, CT) as tile:
                for q in range(3):
                    n = 3 * tile + q
                    pe.wait_ge(w_lo_done, n + 1)
                    for blk in range(BLOCKS):
                        pe.wait_ge(copied, 4 * n + blk + 1)
                        cols = slice(blk * TB, (blk + 1) * TB)
                        for kt in range(KT):
                            at = slice(kt * P, (kt + 1) * P)
                            last = matmul3(pe, banks[blk][:], w_hi[q][:, at], w_lo[q][:, at],
                                           feat_hi[:, kt, cols], feat_lo[:, kt, cols], kt == 0, kt == KT - 1)
                        last.then_inc(product_done, 1)


def gates_and_decays(nc, feat_hi, feat_lo, w32, rows, arrived, gate, beta, decay):
    with Scope(nc, "gd") as s:
        w_hi, w_lo = s.sb("w_hi", [P, KT, GATE_COLS], F32R), s.sb("w_lo", [P, KT, GATE_COLS], F32R)
        tile_hi, tile_lo = s.sb("tile_hi", [P, 2, KT, P], F32R), s.sb("tile_lo", [P, 2, KT, P], F32R)
        logits = s.sb("logits", [P, TILES, LOGITS])
        soft = s.sb("soft", [P, TILES, HEADS0])
        rate = s.sb("rate", [P, HEADS0])
        banks = [s.ps(f"bank{b}", [P, GATE_COLS]) for b in range(2)]
        w_hi_done, w_lo_done = s.sem("w_hi_done"), s.sem("w_lo_done")
        tiled, product_done, silu_done, logits_done, weighted = (
            s.sem(x) for x in ("tiled", "product_done", "silu_done", "logits_done", "weighted"))
        act_step, dve_step = s.sem("act_step"), s.sem("dve_step")
        block = s.block()

        @block.tensor
        def _(pe):
            pe.sem_inc(product_done, 2)
            pe.wait_ge(w_lo_done, 1)
            with pe.Fori(0, TILES // 2) as i:
                for b in range(2):
                    pe.wait_ge(tiled, 4 * i + 2 * b + 2)
                    pe.wait_ge(logits_done, 2 * i + b + 1)
                    for kt in range(KT):
                        last = matmul3(pe, banks[b][:], tile_hi[:, b, kt, :], tile_lo[:, b, kt, :],
                                       w_hi[:, kt, :], w_lo[:, kt, :], kt == 0, kt == KT - 1)
                    last.then_inc(product_done, 1)

        @block.scalar
        def _(act):
            act.preload_act_table(ACT.Silu)
            act.sem_inc(logits_done, 2)
            act.wait_ge(arrived, 32)
            act.copy(w_hi[:], w32[:]).then_inc(w_hi_done, 1)
            with act.Fori(0, TILES // 2) as i:
                for b in range(2):
                    act.wait_ge(product_done, 2 * i + b + 3)
                    at = bass.ds(2 * i + b, 1)
                    act.activation(gate[:, at, 0:KEY], banks[b][:, 0:KEY], ACT.Silu).then_inc(silu_done, 1)
                    act.copy(logits[:, at, :], banks[b][:, KEY:]).then_inc(logits_done, 1)
            act.preload_act_table_set("natural_log_exp_and_others")
            act.activation(rate[:], rows[:, KEY + HEADS0:], ACT.Exp).then_inc(act_step, 1)
            act.wait_ge(logits_done, TILES + 2)
            act.activation(beta[:], logits[:, :, 0:HEADS0], ACT.Exp, scale=-1.0).then_inc(act_step, 1)
            act.wait_ge(dve_step, 2)
            act.activation(soft[:], soft[:], ACT.Exp, scale=-1.0).then_inc(act_step, 1)
            act.wait_ge(dve_step, 3)
            act.activation(soft[:], soft[:], ACT.Ln).then_inc(act_step, 1)

        @block.vector
        def _(dve):
            dve.wait_ge(w_hi_done, 1)
            dve.tensor_tensor(w_lo[:], w32[:], w_hi[:].bitcast(F32), ALU.subtract).then_inc(w_lo_done, 1)
            norm_weight = rows[:, 0:KEY].rearrange("p (o n) -> p o n", o=1)

            def stage(i, b):
                dve.wait_ge(product_done, i + 1)
                cols = bass.ts(i, P)
                dve.tensor_copy(tile_hi[:, b], feat_hi[:, :, cols]).then_inc(tiled, 1)
                dve.tensor_copy(tile_lo[:, b], feat_lo[:, :, cols]).then_inc(tiled, 1)

            def weight(i):
                dve.wait_ge(silu_done, i + 1)
                row = gate[:, bass.ds(i, 1), 0:KEY]
                dve.tensor_tensor(row, row, norm_weight, ALU.mult).then_inc(weighted, 1)

            for b in range(2):
                stage(b, b)
            with dve.Fori(0, TILES // 2 - 1) as i:
                for b in range(2):
                    stage(2 * i + 2 + b, b)
                for b in range(2):
                    weight(2 * i + b)
            for b in range(2):
                weight(TILES - 2 + b)
            dve.wait_ge(logits_done, TILES + 2)
            z = logits[:, :, HEADS0:]
            bias = rows[:, KEY:KEY + HEADS0].rearrange("p (o h) -> p o h", o=1).broadcast_to([P, TILES, HEADS0])
            dve.tensor_tensor(z, z, bias, ALU.add).then_inc(dve_step, 1)
            dve.wait_ge(dve_step, 1)
            dve.scalar_tensor_tensor(out=soft[:], in0=z, scalar=-1.0, in1=z, op0=ALU.mult,
                                     op1=ALU.max).then_inc(dve_step, 1)
            dve.wait_ge(act_step, 3)
            dve.tensor_scalar(soft[:], soft[:], 1.0, None, ALU.add).then_inc(dve_step, 1)
            dve.tensor_scalar(beta[:], beta[:], 1.0, None, ALU.add).then_inc(dve_step, 1)
            dve.wait_ge(dve_step, 4)
            dve.reciprocal(beta[:], beta[:]).then_inc(dve_step, 1)
            dve.wait_ge(act_step, 4)
            dve.scalar_tensor_tensor(out=soft[:], in0=z, scalar=0.0, in1=soft[:],
                                     op0=ALU.max, op1=ALU.add).then_inc(dve_step, 1)
            dve.wait_ge(dve_step, 6)
            spread = rate[:].rearrange("p (o h) -> p o h", o=1).broadcast_to([P, TILES, HEADS0])
            dve.tensor_tensor(decay[:], soft[:], spread, ALU.mult).then_inc(dve_step, 1)
            dve.wait_ge(dve_step, 7)
            dve.tensor_scalar(decay[:], decay[:], -1.0, None, ALU.mult).then_inc(dve_step, 1)


def delta_rule(nc, stream, ident, mask, hidden, qkv, beta, decay, w_out):
    with Scope(nc, "dr", give_back=True) as s:
        FOURS = BH // 4
        PAIRS = BH // 2
        FM_BANKS = (0, 1, 3, 4, 2, 5)
        w_hi, w_lo = s.sb("w_hi", [P, CT, DIM], F32R), s.sb("w_lo", [P, CT, DIM], F32R)
        raw = [s.sb(f"raw{u}", [P, BATCH, 3 * CT, P]) for u in range(2)]
        norm = s.sb("norm", [P, BATCH, 2, HEADS0])
        norm_x, o_norm_x = s.sb("norm_x", [P, BATCH, 2, HEADS0]), s.sb("o_norm_x", [P, BH])
        correction, o_correction = s.sb("correction", [P, BATCH, 2, HEADS0]), s.sb("o_correction", [P, BH])
        q_n, k_n, k_d, v_t = (s.sb(x, [P, BATCH, KEY]) for x in ("q_n", "k_n", "k_d", "v_t"))
        o_n = s.sb("o_n", [P, BATCH, KEY])
        o_hi, o_lo = s.sb("o_hi", [P, BATCH, CT, P], F32R), s.sb("o_lo", [P, BATCH, CT, P], F32R)
        q_g = s.sb("q_g", [P, BATCH, KEY])
        o_square = q_g
        k_w = s.sb("k_w", [P, BATCH, KEY])
        fm = s.sb("fm", [P, 3, BATCH, CT, P])
        g_now, beta_now = s.sb("g_now", [P, BATCH, HEADS0]), s.sb("beta_now", [P, BATCH, HEADS0])
        g_cols = s.sb("g_cols", [P, BH, P])
        w32 = g_cols[:].rearrange("p h t -> p (h t)").rearrange("p (k n) -> p k n", k=CT)
        e_g = s.sb("e_g", [P, 3, BH])
        minus_e_g = s.sb("minus_e_g", [P, BH])
        e_end = s.sb("e_end", [P, PAIRS])
        att = s.sb("att", [P, BH, P])
        a_t = s.sb("a_t", [P, BH, P])
        a_l = s.sb("a_l", [P, 2, BH, P])
        t_m, t_t, y_m = (s.sb(x, [P, BH, P]) for x in ("t_m", "t_t", "y_m"))
        below = s.sb("below", [P, BH, P])
        square = s.sb("square", [P, BATCH, 2, KEY])
        w_t = s.sb("w_t", [P, PAIRS, P])
        u_m = s.sb("u_m", [P, BH, HEAD_DIM0])
        state = s.sb("state", [P, PAIRS, HEAD_DIM0])
        o_norm = s.sb("o_norm", [P, BH])
        banks = [s.ps(f"bank{b}", [P, TB]) for b in range(8)]

        arrived, residual_in = s.sem("arrived"), s.sem("residual_in")
        raw_in = [s.sem(f"raw_in{u}") for u in range(2)]
        refined, o_refined = s.sem("refined"), s.sem("o_refined")
        a_l_done, below_done, factor_done, logs_done, o_logs_done = (
            s.sem(x) for x in ("a_l_done", "below_done", "factor_done", "logs_done", "o_logs_done"))
        w_hi_done, w_lo_done, const_done = s.sem("w_hi_done"), s.sem("w_lo_done"), s.sem("const_done")
        now_done, g_cols_done, norm_done, masked, o_norm_done = (
            s.sem(x) for x in ("now_done", "g_cols_done", "norm_done", "masked", "o_norm_done"))
        turned, sums_done, dlog_done, fm_turned, kk_done, qk_done, t0_turned = (
            s.sem(x) for x in ("turned", "sums_done", "dlog_done", "fm_turned", "kk_done", "qk_done", "t0_turned"))
        y_ps, z_ps, w_ps, u_ps, o_ps, state_ps, o_turned, out_ps = (
            s.sem(x) for x in ("y_ps", "z_ps", "w_ps", "u_ps", "o_ps", "state_ps", "o_turned", "out_ps"))
        e_g_done, squared, v_done, dec_done, fm_done, t0_done, w_done, o_squared, o_hi_done = (
            s.sem(x) for x in ("e_g_done", "squared", "v_done", "dec_done", "fm_done", "t0_done", "w_done",
                               "o_squared", "o_hi_done"))
        summed, normed, scaled, small, a_done, att_done, tt_done, y_done, t_done = (
            s.sem(x) for x in ("summed", "normed", "scaled", "small", "a_done", "att_done", "tt_done", "y_done", "t_done"))
        evens_done = s.sem("evens_done")
        t_turned, t_t_done = s.sem("t_turned"), s.sem("t_t_done")
        pairs_done = s.sem("pairs_done")
        u_done, state_done, o_summed, o_done, gated, o_lo_done, written = (
            s.sem(x) for x in ("u_done", "state_done", "o_summed", "o_done", "gated", "o_lo_done", "written"))
        block = s.block()

        def const(which, heads):
            return mask[:, which:which + 1, :].broadcast_to([P, heads, P])

        def fours(ap, f):
            return ap[:, 4 * f:4 * f + 4, :]

        def product_heads(ap, f):
            return ap[:, (slice(0, 8, 2), slice(1, 8, 2), slice(8, 12))[f], :]

        def bank_of_four(b):
            return banks[b][:].rearrange("p (h t) -> p h t", h=4)

        def bank_of_heads(b):
            return banks[b][:, 0:KEY].rearrange("p (h d) -> p h d", h=HEADS0)

        def heads(ap):
            if len(ap.shape) == 2:
                return ap.rearrange("p (h d) -> p h d", d=HEAD_DIM0)
            return ap.rearrange("p b (h d) -> p (b h) d", d=HEAD_DIM0)

        def along(ap, width):
            return ap.unsqueeze(2).broadcast_to([P, ap.shape[1], width])

        def tile_of(b, c):
            return bass.ds(b * CHUNKS + c, 1)

        def half_rows(h):
            return slice((h % 2) * HEAD_DIM0, (h % 2 + 1) * HEAD_DIM0)

        @block.sync
        def _(sp):
            sp.dma_start(w32, w_out.rearrange("(k p) n -> p k n", p=P)).then_inc(arrived, 16)

            def load(c):
                for b in range(BATCH):
                    cols = slice(b * SEQ + c * CHUNK, b * SEQ + (c + 1) * CHUNK)
                    sp.dma_start(raw[c % 2][:, b], qkv[:, :, cols].rearrange("i p t -> p i t")).then_inc(raw_in[c % 2], 16)

            load(0)
            for c in range(CHUNKS):
                if c + 1 < CHUNKS:
                    if c:
                        sp.wait_ge(turned, 6 * c)
                    load(c + 1)
                for b in range(BATCH):
                    sp.wait_ge(gated, 2 * c + b + 1)
                    rows = hidden[(b * CHUNKS + c) * P:(b * CHUNKS + c + 1) * P, :]
                    sp.dma_start(stream[:, b * CHUNKS + c, :], rows).then_inc(residual_in, 16)

        @block.gpsimd
        def _(pool):
            pool.memset(state[:], 0.0).then_inc(const_done, 1)
            pool.wait_ge(w_lo_done, 1)
            with pool.Fori(0, CHUNKS) as c:
                pool.wait_ge(state_done, 2 * c + 2)
                for b in range(BATCH):
                    pool.tensor_copy(g_now[:, b, :], decay[:, tile_of(b, c), :]).then_inc(now_done, 1)
                    pool.tensor_copy(beta_now[:, b, :], beta[:, tile_of(b, c), :]).then_inc(now_done, 1)
                pool.wait_ge(now_done, 4 * c + 4)
                g_flat = g_now[:].rearrange("p b h -> p (b h)")
                beta_flat = beta_now[:].rearrange("p b h -> p (b h)")
                pool.tensor_tensor(g_cols[:], const(UPTO, BH), along(g_flat, P), ALU.mult).then_inc(g_cols_done, 1)
                pool.tensor_tensor(below[:], const(BEFORE, BH), along(beta_flat, P), ALU.mult).then_inc(below_done, 1)
                pool.wait_ge(below_done, c + 1)
                pool.wait_ge(dec_done, 3 * c + 3)
                pool.tensor_tensor(a_t[:], att[:], below[:], ALU.mult).then_inc(factor_done, 1)
                for level in range(LEVELS):
                    if level == 0:
                        pool.wait_ge(a_done, 3 * c + 3)
                    if level == 2:
                        pool.wait_ge(att_done, 3 * c + 3)
                        pool.tensor_tensor(att[:], att[:], const(UPTO, BH), ALU.mult).then_inc(masked, 1)
                    if level >= 2:
                        pool.wait_ge(y_ps, FOURS * (LEVELS * c + level - 1))
                    pool.tensor_tensor(a_l[:, level % 2], a_t[:], const(LEVEL0 + level, BH), ALU.mult).then_inc(a_l_done, 1)

        @block.scalar
        def _(act):
            act.preload_act_table_set("natural_log_exp_and_others")
            act.wait_ge(arrived, 16)
            act.copy(w_hi[:], w32).then_inc(w_hi_done, 1)

            def split_output(c):
                for b in range(BATCH):
                    act.wait_ge(o_turned, 2 * c + b + 1)
                    act.copy(o_hi[:, b], banks[2 + 3 * b][:, 0:KEY].rearrange("p (k t) -> p k t", k=CT))\
                       .then_inc(o_hi_done, 1)

            def chunk(c, first):
                for b in range(BATCH):
                    for part in range(2):
                        act.wait_ge(turned, 6 * c + 3 * b + part + 1)
                        act.activation(square[:, b, part, :], banks[3 * b + part][:, 0:KEY],
                                       ACT.Square).then_inc(squared, 1)
                    act.wait_ge(turned, 6 * c + 3 * b + 3)
                    act.copy(v_t[:, b, :], banks[3 * b + 2][:, 0:KEY]).then_inc(v_done, 1)
                act.wait_ge(sums_done, c + 1)
                act.activation(e_g[:], banks[6][:, 0:3 * BH], ACT.Exp).then_inc(e_g_done, 1)
                act.wait_ge(summed, 2 * c + 2)
                act.activation(norm[:], norm_x[:], ACT.Ln).then_inc(logs_done, 1)
                act.wait_ge(logs_done, c + 1)
                act.activation(norm[:], norm[:], ACT.Exp, scale=-0.5).then_inc(norm_done, 1)
                for f in range(FOURS):
                    act.wait_ge(dlog_done, 3 * c + f + 1)
                    act.activation(fours(att, f), bank_of_four(7 - f % 2), ACT.Exp).then_inc(dec_done, 1)
                if not first:
                    split_output(c - 1)
                for x in range(6):
                    act.wait_ge(fm_turned, 6 * c + x + 1)
                    act.copy(fm[:, x // 2, x % 2], banks[FM_BANKS[x]][:, 0:KEY].rearrange("p (k t) -> p k t", k=CT))\
                       .then_inc(fm_done, 1)
                for f in range(FOURS):
                    act.wait_ge(t0_turned, 3 * c + f + 1)
                    act.copy(fours(t_m, f), bank_of_four(f)).then_inc(t0_done, 1)
                for level in range(LEVELS):
                    for f in range(FOURS):
                        at = FOURS * (LEVELS * c + level) + f
                        act.wait_ge(y_ps, at + 1)
                        act.copy(fours(y_m, f), bank_of_four(f)).then_inc(y_done, 1)
                    if level < LEVELS - 1:
                        for f in range(FOURS):
                            act.wait_ge(t_turned, FOURS * ((LEVELS - 1) * c + level) + f + 1)
                            act.copy(fours(t_t, f), bank_of_four(f)).then_inc(t_t_done, 1)
                for b in range(BATCH):
                    act.wait_ge(w_ps, 2 * c + b + 1)
                    act.copy(w_t[:, CT * b:CT * b + CT, :], banks[6 + b][:, 0:KEY].rearrange("p (k t) -> p k t", k=CT))\
                       .then_inc(w_done, 1)
                for odd in range(2):
                    act.wait_ge(o_ps, 2 * c + odd + 1)
                    act.activation(o_square[:, odd, :], banks[6 + odd][:, 0:KEY], ACT.Square).then_inc(o_squared, 1)
                act.wait_ge(o_summed, 2 * c + 2)
                act.activation(o_norm[:], o_norm_x[:], ACT.Ln).then_inc(o_logs_done, 1)
                act.wait_ge(o_logs_done, c + 1)
                act.activation(o_norm[:], o_norm[:], ACT.Exp, scale=-0.5).then_inc(o_norm_done, 1)

            chunk(0, True)
            with act.Fori(1, CHUNKS) as c:
                chunk(c, False)
            split_output(CHUNKS - 1)

        @block.vector
        def _(dve):
            dve.wait_ge(w_hi_done, 1)
            dve.tensor_tensor(w_lo[:], w32, w_hi[:].bitcast(F32), ALU.subtract).then_inc(w_lo_done, 1)
            dve.sem_inc(written, 2)
            dve.sem_inc(state_done, 2)
            dve.sem_inc(o_done, 2)

            def refine(y, x, t, done, count):
                dve.tensor_tensor(t, y, y, ALU.mult).then_inc(done, 1)
                dve.wait_ge(done, count + 1)
                dve.tensor_tensor(t, t, x, ALU.mult).then_inc(done, 1)
                dve.wait_ge(done, count + 2)
                dve.tensor_scalar(t, t, -0.5, 1.5, ALU.mult, ALU.add).then_inc(done, 1)
                dve.wait_ge(done, count + 3)
                dve.tensor_tensor(y, y, t, ALU.mult).then_inc(done, 1)
                dve.wait_ge(done, count + 4)

            def low_output(c):
                for b in range(BATCH):
                    dve.wait_ge(o_hi_done, 2 * c + b + 1)
                    dve.tensor_tensor(o_lo[:, b], banks[2 + 3 * b][:, 0:KEY].rearrange("p (k t) -> p k t", k=CT),
                                      o_hi[:, b].bitcast(F32), ALU.subtract).then_inc(o_lo_done, 1)

            def add_output(c):
                dve.wait_ge(residual_in, 32 * c + 32)
                for b in range(BATCH):
                    dve.wait_ge(out_ps, 2 * c + b + 1)
                    row = stream[:, tile_of(b, c), :]
                    bank = banks[6 + b][:].rearrange("p (o n) -> p o n", o=1)
                    dve.tensor_tensor(row, row, bank, ALU.add).then_inc(written, 1)

            def chunk(c, first):
                dve.wait_ge(squared, 4 * c + 4)
                dve.tensor_reduce(norm_x[:].rearrange("p b a h -> p (b a h)"),
                                  square.rearrange("p b a (h d) -> p (b a h) d", d=HEAD_DIM0),
                                  AX.X, ALU.add).then_inc(summed, 1)
                dve.wait_ge(summed, 2 * c + 1)
                dve.tensor_scalar(norm_x[:], norm_x[:], 1e-6, None, ALU.add).then_inc(summed, 1)
                dve.wait_ge(norm_done, c + 1)
                refine(norm[:], norm_x[:], correction[:], refined, 4 * c)
                dve.tensor_scalar(norm[:, :, 0, :], norm[:, :, 0, :], HEAD_DIM0 ** -0.5, None,
                                  ALU.mult).then_inc(small, 1)
                dve.wait_ge(e_g_done, c + 1)
                dve.tensor_scalar(minus_e_g[:], e_g[:, 0, :], -1.0, None, ALU.mult).then_inc(small, 1)
                dve.tensor_copy(e_end[0:HEAD_DIM0, :], e_g[0:HEAD_DIM0, 2, 0::2]).then_inc(small, 1)
                dve.tensor_copy(e_end[HEAD_DIM0:, :], e_g[HEAD_DIM0:, 2, 1::2]).then_inc(small, 1)
                dve.wait_ge(small, 4 * c + 4)
                for b in range(BATCH):
                    dve.tensor_tensor(heads(k_n[:, b, :]), bank_of_heads(3 * b + 1),
                                      along(norm[:, b, 1, :], HEAD_DIM0), ALU.mult).then_inc(normed, 1)
                    dve.tensor_tensor(heads(q_n[:, b, :]), bank_of_heads(3 * b),
                                      along(norm[:, b, 0, :], HEAD_DIM0), ALU.mult).then_inc(normed, 1)
                dve.wait_ge(normed, 4 * c + 4)
                dve.tensor_tensor(heads(q_g[:]), heads(q_n[:]), along(e_g[:, 0, :], HEAD_DIM0), ALU.mult).then_inc(scaled, 1)
                if not first:
                    low_output(c - 1)
                dve.tensor_tensor(heads(k_w[:]), heads(k_n[:]), along(minus_e_g[:], HEAD_DIM0), ALU.mult).then_inc(scaled, 1)
                dve.tensor_tensor(heads(k_d[:]), heads(k_n[:]), along(e_g[:, 1, :], HEAD_DIM0), ALU.mult).then_inc(scaled, 1)
                dve.wait_ge(factor_done, c + 1)
                for f in range(FOURS):
                    dve.wait_ge(kk_done, 3 * c + f + 1)
                    dve.tensor_tensor(product_heads(a_t, f), bank_of_four(f), product_heads(a_t, f), ALU.mult).then_inc(a_done, 1)
                for f in range(FOURS):
                    dve.wait_ge(a_done, 3 * c + (2, 2, 3)[f])
                    dve.tensor_tensor(fours(t_t, f), fours(a_t, f), const(PAIR_T, 4), ALU.mult).then_inc(pairs_done, 1)
                for f in range(FOURS):
                    dve.wait_ge(pairs_done, 3 * c + f + 1)
                    dve.tensor_tensor(fours(t_t, f), fours(t_t, f), ident[:].unsqueeze(1).broadcast_to([P, 4, P]),
                                      ALU.add).then_inc(tt_done, 1)
                for f in range(FOURS):
                    dve.wait_ge(qk_done, 3 * c + f + 1)
                    dve.tensor_tensor(product_heads(att, f), bank_of_four(3 + f), product_heads(att, f), ALU.mult).then_inc(att_done, 1)
                if not first:
                    add_output(c - 1)
                for level in range(LEVELS):
                    for f in range(FOURS):
                        at = FOURS * (LEVELS * c + level) + f
                        dve.wait_ge(z_ps, at + 1)
                        t, bank = (t_m, 3 + f) if level < LEVELS - 1 else (t_t, f)
                        dve.tensor_tensor(fours(t, f), fours(t, f), bank_of_four(bank), ALU.add).then_inc(t_done, 1)
                beta_flat = beta_now[:].rearrange("p b h -> p (b h)")
                for odd in range(2):
                    dve.wait_ge(u_ps, 2 * c + odd + 1)
                    dve.tensor_tensor(u_m[:, odd::2, :], bank_of_heads(odd),
                                      along(beta_flat[:, odd::2], HEAD_DIM0), ALU.mult).then_inc(u_done, 1)
                for odd in range(2):
                    dve.wait_ge(o_squared, 2 * c + odd + 1)
                dve.tensor_reduce(o_norm_x[:], heads(o_square[:]), AX.X, ALU.add).then_inc(o_summed, 1)
                dve.wait_ge(o_summed, 2 * c + 1)
                dve.tensor_scalar(o_norm_x[:], o_norm_x[:], 1.0 / HEAD_DIM0, EPS, ALU.mult, ALU.add).then_inc(o_summed, 1)
                dve.wait_ge(state_ps, c + 1)
                dve.tensor_tensor(state[:], state[:], along(e_end[:], HEAD_DIM0), ALU.mult).then_inc(state_done, 1)
                dve.wait_ge(state_done, 2 * c + 3)
                dve.tensor_tensor(state[:], state[:], banks[4][:, 0:KEY].rearrange("p (j d) -> p j d", j=PAIRS),
                                  ALU.add).then_inc(state_done, 1)
                dve.wait_ge(o_norm_done, c + 1)
                refine(o_norm[:], o_norm_x[:], o_correction[:], o_refined, 4 * c)
                for odd in range(2):
                    dve.tensor_tensor(heads(o_n[:])[:, odd::2, :], bank_of_heads(6 + odd),
                                      along(o_norm[:, HEADS0 * odd:HEADS0 * (odd + 1)], HEAD_DIM0),
                                      ALU.mult).then_inc(o_done, 1)
                dve.wait_ge(o_done, 2 * c + 4)
                for b in range(BATCH):
                    row = o_n[:, b:b + 1, :]
                    dve.tensor_tensor(row, row, stream[:, tile_of(b, c), 0:KEY], ALU.mult).then_inc(gated, 1)

            chunk(0, True)
            with dve.Fori(1, CHUNKS) as c:
                chunk(c, False)
            low_output(CHUNKS - 1)
            add_output(CHUNKS - 1)

        @block.tensor
        def _(pe):
            pe.wait_ge(w_lo_done, 1)
            pe.wait_ge(const_done, 1)

            def turn_output(c):
                for b in range(BATCH):
                    pe.wait_ge(gated, 2 * c + b + 1)
                    for k in range(CT):
                        last = pe.transpose(banks[2 + 3 * b][:, k * P:(k + 1) * P], o_n[:, b, k * P:(k + 1) * P], ident[:])
                    last.then_inc(o_turned, 1)

            def project_output(c):
                for b in range(BATCH):
                    pe.wait_ge(o_lo_done, 2 * c + b + 1)
                    for k in range(CT):
                        last = matmul3(pe, banks[6 + b][:], o_hi[:, b, k, :], o_lo[:, b, k, :],
                                       w_hi[:, k, :], w_lo[:, k, :], k == 0, k == CT - 1)
                    last.then_inc(out_ps, 1)

            def chunk(c, pair, u, first):
                for b in range(BATCH):
                    if b:
                        pe.wait_ge(state_done, 2 * c + 2)
                    pe.wait_ge(raw_in[u], 32 * (pair + 1))
                    for part in range(3):
                        for k in range(CT):
                            last = pe.transpose(banks[3 * b + part][:, k * P:(k + 1) * P], raw[u][:, b, CT * part + k, :], ident[:])
                        last.then_inc(turned, 1)
                pe.wait_ge(o_done, 2 * c + 2)
                pe.wait_ge(now_done, 4 * c + 4)
                g = g_now[:].rearrange("p b h -> p (b h)")
                for x, which in enumerate((UPTO, AFTER, ONES)):
                    last = pe.matmul(banks[6][:, BH * x:BH * (x + 1)], mask[:, which, :], g, start=True, stop=True)
                last.then_inc(sums_done, 1)
                pe.wait_ge(g_cols_done, c + 1)
                for f in range(FOURS):
                    if f == 1:
                        pe.wait_ge(e_g_done, c + 1)
                    if f == 2:
                        pe.wait_ge(dec_done, 3 * c + 1)
                    pe.matmul(banks[7 - f % 2][:], mask[:, AFTER, :], fours(g_cols, f).rearrange("p h t -> p (h t)"),
                              start=True, stop=True).then_inc(dlog_done, 1)
                pe.wait_ge(v_done, 2 * c + 2)
                if not first:
                    turn_output(c - 1)
                for x, (source, done, count) in enumerate((
                        (k_n, normed, 4 * c + 4), (k_n, normed, 4 * c + 4), (q_n, normed, 4 * c + 4),
                        (q_n, normed, 4 * c + 4), (q_g, scaled, 3 * c + 1), (q_g, scaled, 3 * c + 1))):
                    pe.wait_ge(done, count)
                    if x == 4 and not first:
                        pe.wait_ge(o_lo_done, 2 * c)
                    for k in range(CT):
                        last = pe.transpose(banks[FM_BANKS[x]][:, k * P:(k + 1) * P], source[:, x % 2, k * P:(k + 1) * P], ident[:])
                    last.then_inc(fm_turned, 1)
                for kind, done in ((0, kk_done), (1, qk_done)):
                    pe.wait_ge(fm_done, 6 * c + 6)
                    for i in (0, 1, 2, 3, 4, 5, 6, 7, 8, 10, 9, 11):
                        b, h = divmod(i, HEADS0)
                        bank, col = (i % 2, i // 2) if i < 8 else (2, i - 8)
                        if i == 9:
                            pe.wait_ge(evens_done, 2 * c + kind + 1)
                        last = pe.matmul(banks[3 * kind + bank][:, col * P:(col + 1) * P],
                                         fm[half_rows(h), 0, b, h // 2, :], fm[half_rows(h), kind, b, h // 2, :],
                                         start=True, stop=True)
                        if i in (6, 7, 11):
                            last.then_inc(done, 1)
                        if i == 10:
                            last.then_inc(evens_done, 1)
                if not first:
                    project_output(c - 1)
                for f in range(FOURS):
                    pe.wait_ge(tt_done, 3 * c + f + 1)
                    for j in range(4):
                        last = pe.transpose(banks[f][:, j * P:(j + 1) * P], t_t[:, 4 * f + j, :], ident[:])
                    last.then_inc(t0_turned, 1)
                updates = FOURS * LEVELS
                for level in range(LEVELS):
                    pe.wait_ge(a_l_done, LEVELS * c + level + 1)
                    for f in range(FOURS):
                        if level == 0:
                            pe.wait_ge(t0_done, 3 * c + f + 1)
                            pe.wait_ge(att_done, 3 * c + 3)
                        else:
                            pe.wait_ge(t_done, updates * c + FOURS * (level - 1) + f + 1)
                            pe.wait_ge(t_t_done, FOURS * ((LEVELS - 1) * c + level - 1) + f + 1)
                        for j in range(4):
                            x = 4 * f + j
                            last = pe.matmul(banks[f][:, j * P:(j + 1) * P], a_l[:, level % 2, x, :], t_m[:, x, :],
                                             start=True, stop=True)
                        last.then_inc(y_ps, 1)
                    for f in range(FOURS):
                        pe.wait_ge(y_done, FOURS * (LEVELS * c + level) + f + 1)
                        for j in range(4):
                            x = 4 * f + j
                            cols = slice(j * P, (j + 1) * P)
                            if level < LEVELS - 1:
                                last = pe.matmul(banks[3 + f][:, cols], t_t[:, x, :], y_m[:, x, :], start=True, stop=True)
                            else:
                                last = pe.matmul(banks[f][:, cols], y_m[:, x, :], t_t[:, x, :], start=True, stop=True)
                        last.then_inc(z_ps, 1)
                    if level < LEVELS - 1:
                        for f in range(FOURS):
                            pe.wait_ge(t_done, updates * c + FOURS * level + f + 1)
                            for j in range(4):
                                last = pe.transpose(banks[f][:, j * P:(j + 1) * P], t_m[:, 4 * f + j, :], ident[:])
                            last.then_inc(t_turned, 1)
                pe.wait_ge(t_done, updates * (c + 1))
                pe.wait_ge(scaled, 3 * c + 3)
                for i in range(BH):
                    b, h = divmod(i, HEADS0)
                    last = pe.matmul(banks[6 + b][half_rows(h), (h // 2) * P:(h // 2 + 1) * P],
                                     k_w[:, b, h * HEAD_DIM0:(h + 1) * HEAD_DIM0], t_t[:, i, :], start=True, stop=True)
                    if h == HEADS0 - 1:
                        last.then_inc(w_ps, 1)
                pe.wait_ge(w_done, 2 * c + 2)
                for i in range(BH):
                    b, h = divmod(i, HEADS0)
                    at = slice((i // 2) * HEAD_DIM0, (i // 2 + 1) * HEAD_DIM0)
                    pe.matmul(banks[i % 2][:, at], t_t[:, i, :], v_t[:, b, h * HEAD_DIM0:(h + 1) * HEAD_DIM0],
                              start=True, stop=False)
                    last = pe.matmul(banks[i % 2][:, at], w_t[half_rows(h), i // 2, :], state[half_rows(h), i // 2, :],
                                     start=False, stop=True)
                    if i >= BH - 2:
                        last.then_inc(u_ps, 1)
                for i in range(BH):
                    b, h = divmod(i, HEADS0)
                    at = slice((i // 2) * HEAD_DIM0, (i // 2 + 1) * HEAD_DIM0)
                    if i == 0:
                        pe.wait_ge(u_done, 2 * c + 2)
                        pe.wait_ge(masked, c + 1)
                    pe.matmul(banks[6 + i % 2][:, at], fm[half_rows(h), 2, b, h // 2, :], state[half_rows(h), i // 2, :],
                              start=True, stop=False)
                    last = pe.matmul(banks[6 + i % 2][:, at], att[:, i, :], u_m[:, i, :], start=False, stop=True)
                    if i >= BH - 2:
                        last.then_inc(o_ps, 1)
                for i in range(BH):
                    b, h = divmod(i, HEADS0)
                    last = pe.matmul(banks[4][half_rows(h), (i // 2) * HEAD_DIM0:(i // 2 + 1) * HEAD_DIM0],
                                     k_d[:, b, h * HEAD_DIM0:(h + 1) * HEAD_DIM0], u_m[:, i, :], start=True, stop=True)
                last.then_inc(state_ps, 1)

            chunk(0, 0, 0, True)
            chunk(1, 0, 1, False)
            with pe.Fori(1, CHUNKS // 2) as pair:
                for u in range(2):
                    chunk(2 * pair + u, pair, u, False)
            turn_output(CHUNKS - 1)
            project_output(CHUNKS - 1)



def delta_attention(nc, stream, ident, mask, arrivals, hidden, w_qkv, conv_w, w_gate, head_rows, w_out):
    with Scope(nc, "da") as keep:
        qkv = nc.dram_tensor("qkv", (3 * CT, P, TOKENS), F32).ap()
        beta, decay = keep.sb("beta", [P, TILES, HEADS0]), keep.sb("decay", [P, TILES, HEADS0])
        with Scope(nc, "daf") as f:
            feat_hi, feat_lo = f.sb("feat_hi", [P, KT, TOKENS], F32R), f.sb("feat_lo", [P, KT, TOKENS], F32R)
            normalise(nc, "n0a", stream, ident, feat_hi, feat_lo, feature_tiles_plain, arrivals)
            gate_w, gate_rows = f.sb("gate_w", [P, KT, GATE_COLS]), f.sb("gate_rows", [P, KEY + 2 * HEADS0])
            gate_in = f.sem("gate_in")

            def gate_loads(sp):
                sp.dma_start(gate_w[:], w_gate.rearrange("k p n -> p k n")).then_inc(gate_in, 16)
                sp.dma_start(gate_rows[:], head_rows.partition_broadcast(P)).then_inc(gate_in, 16)

            project_conv(nc, feat_hi, feat_lo, w_qkv, conv_w, qkv, gate_loads)
            gates_and_decays(nc, feat_hi, feat_lo, gate_w, gate_rows, gate_in, stream, beta, decay)
        delta_rule(nc, stream, ident, mask, hidden, qkv, beta, decay, w_out)


HEADS1, HALF, HEAD_DIM1, LATENT = 16, 16, 32, 64
QUAD = 4
QUADS = HEADS1 // QUAD
QTILES = SEQ // P
PARKED = 4 * SEQ // DIM
STACK = 4 * HALF


def latents(nc, feat_hi, feat_lo, w_down, w_value, lat_hi, lat_lo, values):
    with Scope(nc, "lat") as s:
        wd32 = s.sb("wd32", [P, KT, P])
        wv32 = s.sb("wv32", [P, DIM])
        wd_hi, wd_lo = s.sb("wd_hi", [P, KT, P], F32R), s.sb("wd_lo", [P, KT, P], F32R)
        wv_hi, wv_lo = s.sb("wv_hi", [P, DIM], F32R), s.sb("wv_lo", [P, DIM], F32R)
        lat_ps = [s.ps(f"lat{b}", [P, TB]) for b in range(2)]
        val_ps = [s.ps(f"val{b}", [P, DIM]) for b in range(2)]
        arrived = s.sem("arrived")
        w_hi_done, w_lo_done = s.sem("w_hi_done"), s.sem("w_lo_done")
        lat_done, val_done = s.sem("lat_done"), s.sem("val_done")
        hi_done, lo_done = s.sem("hi_done"), s.sem("lo_done")
        val_hi_done, val_lo_done = s.sem("val_hi_done"), s.sem("val_lo_done")
        block = s.block()
        KV = slice(LATENT, 2 * LATENT)

        def values_of(i, half):
            b, tile = divmod(i, QTILES)
            return values[:, QUADS * b:QUADS * (b + 1), tile, :, half * HEAD_DIM1:(half + 1) * HEAD_DIM1]

        @block.sync
        def _(sp):
            sp.dma_start(wd32[:], w_down.rearrange("(k p) n -> p k n", p=P)).then_inc(arrived, 16)
            sp.dma_start(wv32[KV, :], w_value).then_inc(arrived, 16)

        @block.scalar
        def _(act):
            act.wait_ge(arrived, 32)
            act.copy(wd_hi[:], wd32[:]).then_inc(w_hi_done, 1)
            act.copy(wv_hi[KV, :], wv32[KV, :]).then_inc(w_hi_done, 1)
            for b in range(BLOCKS):
                act.wait_ge(lat_done, b + 1)
                act.copy(lat_hi[:, b * TB:(b + 1) * TB], lat_ps[b % 2][:]).then_inc(hi_done, 1)
            for i in range(TILES):
                act.wait_ge(val_done, i + 1)
                act.copy(values_of(i, 0), val_ps[i % 2][:].rearrange("p (q h d) -> p q h d", q=QUADS, h=QUAD))\
                   .then_inc(val_hi_done, 1)

        @block.vector
        def _(dve):
            dve.wait_ge(w_hi_done, 2)
            dve.tensor_tensor(wd_lo[:], wd32[:], wd_hi[:].bitcast(F32), ALU.subtract).then_inc(w_lo_done, 1)
            dve.tensor_tensor(wv_lo[KV, :], wv32[KV, :], wv_hi[KV, :].bitcast(F32),
                              ALU.subtract).then_inc(w_lo_done, 1)
            for b in range(BLOCKS):
                dve.wait_ge(hi_done, b + 1)
                cols = slice(b * TB, (b + 1) * TB)
                dve.tensor_tensor(lat_lo[:, cols], lat_ps[b % 2][:], lat_hi[:, cols].bitcast(F32),
                                  ALU.subtract).then_inc(lo_done, 1)
            for i in range(TILES):
                dve.wait_ge(val_hi_done, i + 1)
                dve.tensor_tensor(values_of(i, 1), val_ps[i % 2][:].rearrange("p (q h d) -> p q h d", q=QUADS, h=QUAD),
                                  values_of(i, 0).bitcast(F32), ALU.subtract).then_inc(val_lo_done, 1)

        @block.tensor
        def _(pe):
            pe.wait_ge(w_hi_done, 2)
            pe.wait_ge(w_lo_done, 2)
            for b in range(BLOCKS):
                if b >= 2:
                    pe.wait_ge(lo_done, b - 1)
                cols = slice(b * TB, (b + 1) * TB)
                for kt in range(KT):
                    last = matmul3(pe, lat_ps[b % 2][:], wd_hi[:, kt, :], wd_lo[:, kt, :],
                                   feat_hi[:, kt, cols], feat_lo[:, kt, cols], kt == 0, kt == KT - 1)
                last.then_inc(lat_done, 1)
            for i in range(TILES):
                if i % SUB == 0:
                    pe.wait_ge(lo_done, i // SUB + 1)
                if i >= 2:
                    pe.wait_ge(val_lo_done, i - 1)
                cols = slice(i * P, (i + 1) * P)
                matmul3(pe, val_ps[i % 2][:], lat_hi[KV, cols], lat_lo[KV, cols], wv_hi[KV, :], wv_lo[KV, :],
                        True, True).then_inc(val_done, 1)


def rotated_heads(nc, lat_hi, lat_lo, w_up, cos_sin, rotated, parked_space, parked):
    with Scope(nc, "rot") as s:
        wu32 = s.sb("wu32", [P, QUADS, 2 * P])
        wu_hi, wu_lo = s.sb("wu_hi", [P, QUADS, 2 * P], F32R), s.sb("wu_lo", [P, QUADS, 2 * P], F32R)
        tables = s.sb("tables", [P, 2, SEQ])
        part = s.sb("part", [P, 4, SEQ])
        rot = s.sb("rot", [P, 2, SEQ])
        rot_hi, rot_lo = s.sb("rot_hi", [P, 2, SEQ], F32R), s.sb("rot_lo", [P, 2, SEQ], F32R)
        product = [s.ps(f"product{b}", [P, 2, TB]) for b in range(4)]
        arrived, wu_hi_done, wu_lo_done = s.sem("arrived"), s.sem("wu_hi_done"), s.sem("wu_lo_done")
        proj_done, part_done, rot_done = s.sem("proj_done"), s.sem("part_done"), s.sem("rot_done")
        rot_hi_done, rot_lo_done = s.sem("rot_hi_done"), s.sem("rot_lo_done")
        stored = [s.sem(f"stored{x}") for x in range(2)]
        parked_done = s.sem("parked_done")
        block = s.block()

        def passes(engine, body):
            for n in range(BATCH * QUADS):
                body(n, n // QUADS, n % QUADS)

        @block.sync
        def _(sp):
            sp.dma_start(wu32[:], w_up.rearrange("q p n -> p q n")).then_inc(arrived, 16)
            sp.dma_start(tables[:], cos_sin).then_inc(arrived, 16)
            sp.dma_start(parked, parked_space).then_inc(parked_done, 16)
            for x in range(2):
                sp.sem_inc(stored[x], 32)
            for n in range(BATCH * QUADS):
                for which, half, done in ((0, rot_hi, rot_hi_done), (1, rot_lo, rot_lo_done)):
                    sp.wait_ge(done, n + 1)
                    sp.dma_start(rotated[n, which], half[:, n % 2, :].bitcast(F32)).then_inc(stored[n % 2], 16)
            sp.wait_ge(parked_done, 16)
            for x in range(2):
                sp.wait_ge(stored[x], 32 * BATCH * QUADS // 2 + 32)

        @block.tensor
        def _(pe):
            pe.sem_inc(proj_done, 4)
            pe.wait_ge(wu_lo_done, 1)

            def body(n, b, quad):
                for x in range(2):
                    pe.wait_ge(part_done, 2 * n + x + 1)
                    bank = product[2 * (quad % 2) + x]
                    for half in range(2):
                        cols = bass.ds(b * SEQ + half * TB, TB)
                        last = matmul3(pe, bank[:, half, :], wu_hi[:, quad, x * P:(x + 1) * P],
                                       wu_lo[:, quad, x * P:(x + 1) * P], lat_hi[:, cols], lat_lo[:, cols], True, True)
                    last.then_inc(proj_done, 1)

            passes(pe, body)

        @block.vector
        def _(dve):
            dve.wait_ge(wu_hi_done, 1)
            dve.tensor_tensor(wu_lo[:], wu32[:], wu_hi[:].bitcast(F32), ALU.subtract).then_inc(wu_lo_done, 1)
            dve.sem_inc(part_done, 4)

            def low(n):
                dve.wait_ge(rot_hi_done, n + 1)
                dve.tensor_tensor(rot_lo[:, n % 2, :], rot[:, n % 2, :], rot_hi[:, n % 2, :].bitcast(F32),
                                  ALU.subtract).then_inc(rot_lo_done, 1)

            def body(n, b, quad):
                for x in range(2):
                    dve.wait_ge(proj_done, 2 * n + x + 5)
                    if n >= 2:
                        dve.wait_ge(rot_done, n - 1)
                    dve.tensor_tensor(part[:, 2 * (n % 2) + x, :], product[2 * (n % 2) + x][:].rearrange("p a t -> p (a t)"),
                                      tables[:, x, :], ALU.mult).then_inc(part_done, 1)
                if n:
                    low(n - 1)

            passes(dve, body)
            low(BATCH * QUADS - 1)

        @block.gpsimd
        def _(pool):
            def body(n, b, quad):
                pool.wait_ge(part_done, 2 * n + 6)
                pool.wait_ge(stored[quad % 2], 32 * (QUADS // 2 * b + quad // 2) + 32)
                pool.tensor_tensor(rot[:, quad % 2, :], part[:, 2 * (n % 2), :], part[:, 2 * (n % 2) + 1, :], ALU.add).then_inc(rot_done, 1)

            passes(pool, body)

        @block.scalar
        def _(act):
            act.wait_ge(arrived, 32)
            act.copy(wu_hi[:], wu32[:]).then_inc(wu_hi_done, 1)

            def body(n, b, quad):
                act.wait_ge(rot_done, n + 1)
                act.copy(rot_hi[:, quad % 2, :], rot[:, quad % 2, :]).then_inc(rot_hi_done, 1)

            passes(act, body)


OUT_ROWS = 2 * HEAD_DIM1 + 1
OUT_COLS = OUT_ROWS + 1
LOW_POOL = 768
AHEAD = QTILES + 4
BEHIND = 3


def softmax_heads(nc, ident, values, rotated, parked_space, mixed):
    with Scope(nc, "att") as s:
        q_stack = [s.sb(f"q_stack{j}", [P, SEQ], F32R) for j in range(QUAD)]
        k_stack = [s.sb(f"k_stack{j}", [P, SEQ], F32R) for j in range(QUAD)]
        top = [s.sb(f"top{b}", [P, STACK + QTILES]) for b in range(2)]
        top_rows = s.sb("top_rows", [P, P])
        head_values = s.sb("head_values", [P, 2, QTILES, OUT_COLS], F32R)
        probs = parked_space.rearrange("p i d -> p (i d)").rearrange("p (t n) -> p t n", t=4)
        p_hi, p_lo = s.sb("p_hi", [P, 4, SEQ], F32R), s.sb("p_lo", [P, 4, SEQ], F32R)
        out_t = s.sb("out_t", [P, 2, TB])
        inverse = s.sb("inverse", [P, QTILES])
        parts = s.sb("parts", [P, 2, QTILES, HEAD_DIM1])
        q_scores, k_scores = s.ps("q_scores", [P, 2, TB]), s.ps("k_scores", [P, 2, TB])
        out_ps = [s.ps(f"out{b}", [P, TB]) for b in range(2)]
        turned = s.ps("turned", [P, 2, TB])

        loaded = [s.sem(f"loaded{j}") for j in range(QUAD)]
        ones_done = s.sem("ones_done")
        a_done, max_done, top_turned, top_done = (s.sem(x) for x in ("a_done", "max_done", "top_turned", "top_done"))
        b_done, exp_done, hi_done, lo_dve, lo_pool = (s.sem(x) for x in ("b_done", "exp_done", "hi_done", "lo_dve", "lo_pool"))
        top_copied = s.sem("top_copied")
        values_ready, out_done, copied_act, copied_dve = (s.sem(x) for x in ("values_ready", "out_done", "copied_act", "copied_dve"))
        out_turned, inverse_done, parts_done, mixed_done = (s.sem(x) for x in ("out_turned", "inverse_done", "parts_done", "mixed_done"))
        block = s.block()
        PASSES = BATCH * QUADS
        TURN = 4
        SPREADS = ((0, 3), (3, 6), (6, 8))
        T = QTILES
        TOP = slice(STACK, STACK + T)

        def passes(engine, body):
            body(0, True, False)
            with engine.Fori(1, PASSES - 1) as n:
                body(n, False, False)
            body(PASSES - 1, False, True)

        @block.sync
        def _(sp):
            for n in range(PASSES):
                for j in range(QUAD):
                    if n:
                        sp.wait_ge(b_done, T * (QUAD * (n - 1) + j + 1))
                    for first, dst, which, copies in ((0, q_stack[j], 0, 0), (0, q_stack[j], 1, 0),
                                                      (LATENT, k_stack[j], 0, P * SEQ), (LATENT, k_stack[j], 1, P * SEQ)):
                        at = rotated[n, 0 if copies else which, first + HALF * j:first + HALF * (j + 1), :]
                        src = bass.AP(tensor=at.tensor, offset=at.offset, ap=[[copies, 2], [SEQ, HALF], [1, SEQ]])
                        rows = slice(which * STACK // 2, (which + 1) * STACK // 2)
                        sp.dma_start(dst[rows, :].bitcast(F32), src).then_inc(loaded[j], 16)

        @block.gpsimd
        def _(pool):
            def low(n, j, t):
                at = T * (QUAD * n + j) + t
                pool.wait_ge(hi_done, at + 1)
                pool.tensor_tensor(p_lo[:, t % 4, 0:LOW_POOL], probs[:, t % 4, 0:LOW_POOL],
                                   p_hi[:, t % 4, 0:LOW_POOL].bitcast(F32), ALU.subtract).then_inc(lo_pool, 1)

            def add_parts(n, j):
                g = QUAD * n + j
                pool.wait_ge(parts_done, 2 * g + 2)
                dst = mixed[:, bass.ds(n, 1), :, HEAD_DIM1 * j:HEAD_DIM1 * (j + 1)].rearrange("p o t d -> p (o t) d")
                pool.tensor_tensor(dst, parts[:, 0], parts[:, 1], ALU.add).then_inc(mixed_done, 1)

            def body(n, first, last):
                for j in range(QUAD):
                    for t in range(T):
                        low(n, j, t)
                        if t == 4 and not (first and j < 2):
                            add_parts(n + (j - 2) // QUAD, (j - 2) % QUAD)

            passes(pool, body)
            for j in (QUAD - 2, QUAD - 1):
                add_parts(PASSES - 1, j)

        @block.scalar
        def _(act):
            act.preload_act_table(ACT.Exp)

            def copy_out(g, first):
                act.wait_ge(out_done, T * (g + 1))
                if not first:
                    act.wait_ge(out_turned, g)
                act.copy(out_t[0:OUT_COLS, 0, :], out_ps[0][0:OUT_COLS, :]).then_inc(copied_act, 1)

            def high(at, t, first):
                act.wait_ge(exp_done, at + 1)
                if not first:
                    act.wait_ge(out_done, at - 3)
                act.copy(p_hi[:, t % 4, :], probs[:, t % 4, :]).then_inc(hi_done, 1)

            def body(n, first, last):
                for j in range(QUAD):
                    g = QUAD * n + j
                    for t in range(T):
                        at = T * g + t
                        early = first and j == 0
                        act.wait_ge(b_done, at + 1)
                        if not (early and t < 4):
                            act.wait_ge(lo_dve, at - 3)
                            act.wait_ge(lo_pool, at - 3)
                        act.activation(probs[:, t % 4, :], k_scores[:], ACT.Exp).then_inc(exp_done, 1)
                        if t == BEHIND and not early:
                            copy_out(g - 1, first and j == 1)
                        if not (early and t == 0):
                            high(at - 1, (t - 1) % T, early and t < 5)

            passes(act, body)
            high(T * QUAD * PASSES - 1, T - 1, False)
            copy_out(QUAD * PASSES - 1, False)

        @block.vector
        def _(dve):
            ones = probs[:, 0, :]
            dve.memset(ones, 1.0).then_inc(ones_done, 1)
            for b in range(2):
                dve.memset(top[b][:], 0.0).then_inc(ones_done, 1)
            by_query = turned[:, :, 0:T // 2 * OUT_COLS].rearrange("p a (t d) -> p a t d", d=OUT_COLS)
            by_tile = "p (a t) d -> p a t d"
            dve.wait_ge(ones_done, 3)
            for j in range(QUAD):
                dve.tensor_copy(k_stack[j][TOP, :], ones[TOP, :]).then_inc(ones_done, 1)
            extra = head_values[:, :, :, 2 * HEAD_DIM1:].rearrange("p b t x -> p (b t) x")
            dve.tensor_copy(extra, ones[:, 0:4 * T].rearrange("p (t x) -> p t x", x=2)).then_inc(ones_done, 1)

            def values_of(n, j, buffer):
                dve.tensor_copy(head_values[:, buffer, :, 0:2 * HEAD_DIM1],
                                 values[:, bass.ds(n, 1), :, j, :].rearrange("p o t d -> p (o t) d"))\
                    .then_inc(values_ready, 1)

            def maximum(g, buffer, t, first, scores=q_scores):
                if t == 0 and not first:
                    dve.wait_ge(top_turned, g - 1)
                dve.wait_ge(a_done, T * g + t + 1)
                dve.tensor_reduce(top[buffer][:, STACK + t:STACK + t + 1], scores[:], AX.XY, ALU.max,
                                  negate=True).then_inc(max_done, 1)

            def copy_top(g):
                dve.wait_ge(top_turned, g + 1)
                if not (isinstance(g, int) and g == 0):
                    dve.wait_ge(top_done, len(SPREADS) * g)
                dve.tensor_copy(top_rows[TOP, :], turned[TOP, 0, 0:P]).then_inc(top_copied, 1)

            def spread_top(g, j, piece):
                dve.wait_ge(top_copied, g + 1)
                tiles = slice(*SPREADS[piece])
                count = tiles.stop - tiles.start
                source = top_rows[TOP, :].unsqueeze(1).broadcast_to([T, count, P])
                own = ident[TOP, STACK + tiles.start:STACK + tiles.stop].unsqueeze(2).broadcast_to([T, count, P])
                dve.tensor_tensor(q_stack[j][TOP, :].rearrange("r (t q) -> r t q", t=T)[:, tiles, :], source, own,
                                  ALU.mult).then_inc(top_done, 1)

            def low(at, t):
                dve.wait_ge(hi_done, at + 1)
                dve.tensor_tensor(p_lo[:, t % 4, LOW_POOL:], probs[:, t % 4, LOW_POOL:],
                                  p_hi[:, t % 4, LOW_POOL:].bitcast(F32), ALU.subtract).then_inc(lo_dve, 1)

            def copy_out(g, first):
                dve.wait_ge(out_done, T * (g + 1))
                if not first:
                    dve.wait_ge(out_turned, g)
                dve.tensor_copy(out_t[0:OUT_COLS, 1, :], out_ps[1][0:OUT_COLS, :]).then_inc(copied_dve, 1)

            def invert_sums(g, first):
                dve.wait_ge(out_turned, g + 1)
                if not first:
                    dve.wait_ge(parts_done, 2 * g)
                dve.reciprocal(inverse[:].rearrange("p (a t) -> p a t", a=2), by_query[:, :, :, OUT_ROWS - 1])\
                   .then_inc(inverse_done, 1)

            def normalise_part(g, x, first):
                dve.wait_ge(inverse_done, g + 1)
                if not first:
                    dve.wait_ge(mixed_done, g)
                spread = inverse[:].unsqueeze(2).broadcast_to([P, T, HEAD_DIM1]).rearrange(by_tile, a=2)
                dve.tensor_tensor(parts[:, x].rearrange(by_tile, a=2),
                                  by_query[:, :, :, HEAD_DIM1 * x:HEAD_DIM1 * (x + 1)], spread,
                                  ALU.mult).then_inc(parts_done, 1)

            def body(n, first, last):
                for j in range(QUAD):
                    g = QUAD * n + j
                    early = first and j == 0
                    for t in range(T):
                        if not (early and t < 2):
                            low(T * g + t - 2, (t - 2) % T)
                        ahead, tile = divmod(t + AHEAD, T)
                        if t == 0:
                            values_of(n, j, j % 2)
                        if t == 1 and not (first and j < 2):
                            invert_sums(g - 2, first and j == 2)
                            normalise_part(g - 2, 0, first and j == 2)
                        if t == 2 and not (first and j < 2):
                            normalise_part(g - 2, 1, first and j == 2)
                        if t == BEHIND and not early:
                            copy_out(g - 1, first and j == 1)
                        if t > TURN and not (last and j == QUAD - 1):
                            spread_top(g + 1, (j + 1) % QUAD, t - TURN - 1)
                        if not (last and j + ahead >= QUAD):
                            maximum(g + ahead, (j + ahead) % 2, tile, first and j + ahead < 2)
                        if t == TURN and not (last and j == QUAD - 1):
                            copy_top(g + 1)

            for t in range(T):
                maximum(0, 0, t, True, (q_scores, k_scores)[t % 2])
            copy_top(0)
            for piece in range(len(SPREADS)):
                spread_top(0, 0, piece)
            for t in range(AHEAD - T):
                maximum(1, 1, t, True, (q_scores, k_scores)[t % 2])
            passes(dve, body)
            for t in (T - 2, T - 1):
                low(T * (QUAD * PASSES - 1) + t, t)
            copy_out(QUAD * PASSES - 1, False)
            for g in (QUAD * PASSES - 2, QUAD * PASSES - 1):
                invert_sums(g, False)
                for x in range(2):
                    normalise_part(g, x, False)

        @block.tensor
        def _(pe):
            pe.wait_ge(ones_done, 3 + QUAD + 1)

            def query_scores(g, n, j, t, prologue=False):
                if t == 0:
                    pe.wait_ge(loaded[j], 64 * (n + 1))
                scores = k_scores if prologue and t % 2 else q_scores
                if not prologue:
                    pe.wait_ge(max_done, T * g + t)
                elif T * g + t >= 2:
                    pe.wait_ge(max_done, T * g + t - 1)
                for half in range(2):
                    last = pe.matmul(scores[:, half, :], q_stack[j][0:STACK, t * P:(t + 1) * P],
                                     k_stack[j][0:STACK, half * TB:(half + 1) * TB], start=True, stop=True)
                last.then_inc(a_done, 1)

            def turn_top(g, buffer, first):
                pe.wait_ge(max_done, T * (g + 1))
                if not first:
                    pe.wait_ge(parts_done, 2 * (g - 2))
                pe.transpose(turned[0:STACK + T, 0, 0:P], top[buffer][:], ident[:]).then_inc(top_turned, 1)

            def key_scores(g, j, t, first):
                if t == 0:
                    pe.wait_ge(top_done, len(SPREADS) * (g + 1))
                if not (first and t == 0):
                    pe.wait_ge(exp_done, T * g + t)
                for half in range(2):
                    last = pe.matmul(k_scores[:, half, :], k_stack[j][0:STACK + T, t * P:(t + 1) * P],
                                     q_stack[j][0:STACK + T, half * TB:(half + 1) * TB], start=True, stop=True)
                last.then_inc(b_done, 1)

            def output(g, buffer, t, first):
                at = T * g + t
                if t == 0:
                    pe.wait_ge(values_ready, g + 1)
                    if not first:
                        pe.wait_ge(copied_act, g)
                        pe.wait_ge(copied_dve, g)
                pe.wait_ge(hi_done, at + 1)
                pe.wait_ge(lo_dve, at + 1)
                pe.wait_ge(lo_pool, at + 1)
                for which, part in enumerate((p_hi, p_lo)):
                    for half in range(2):
                        last = pe.matmul(out_ps[half][0:OUT_COLS, :], head_values[:, buffer, t, :],
                                         part[:, t % 4, half * TB:(half + 1) * TB],
                                         start=(t == 0 and which == 0), stop=(t == T - 1 and which == 1))
                last.then_inc(out_done, 1)

            def turn_out(g, first):
                if not first:
                    pe.wait_ge(parts_done, 2 * g)
                pe.wait_ge(copied_act, g + 1)
                pe.wait_ge(copied_dve, g + 1)
                for t in range(T):
                    half, at = divmod(t, T // 2)
                    last = pe.transpose(turned[:, half, at * OUT_COLS:(at + 1) * OUT_COLS],
                                        out_t[0:OUT_COLS, half, at * P:(at + 1) * P], ident[0:OUT_COLS, 0:OUT_COLS])
                last.then_inc(out_turned, 1)

            def body(n, first, last):
                for j in range(QUAD):
                    g = QUAD * n + j
                    early = first and j == 0
                    for t in range(T):
                        ahead, tile = divmod(t + AHEAD, T)
                        if t == 5 and not early:
                            if not (last and j == QUAD - 1):
                                pe.wait_ge(top_copied, g + 2)
                            turn_out(g - 1, first and j == 1)
                        if not (last and j + ahead >= QUAD):
                            query_scores(g + ahead, n + (j + ahead) // QUAD, (j + ahead) % QUAD, tile)
                        if t == TURN and not (last and j == QUAD - 1):
                            turn_top(g + 1, (j + 1) % 2, first and j < 2)
                        if not (last and j == QUAD - 1 and t == T - 1):
                            key_scores(g + (t + 1) // T, (j + (t + 1) // T) % QUAD, (t + 1) % T, False)
                        if not (early and t < BEHIND):
                            output(g + (t - BEHIND) // T, (j + (t - BEHIND) // T) % 2, (t - BEHIND) % T, early)

            for t in range(T):
                query_scores(0, 0, 0, t, True)
            turn_top(0, 0, True)
            for t in range(AHEAD - T):
                query_scores(1, 0, 1, t, True)
            pe.wait_ge(max_done, AHEAD)
            key_scores(0, 0, 0, True)
            passes(pe, body)
            for t in range(T - BEHIND, T):
                output(QUAD * PASSES - 1, 1, t, False)
            turn_out(QUAD * PASSES - 1, False)


def project_out(nc, prefix, stream, ident, mixed, w_out, width, parked_space, parked):
    kts = width // P
    with Scope(nc, prefix) as s:
        w32 = s.sb("w32", [P, kts, DIM])
        w_hi, w_lo = s.sb("w_hi", [P, kts, DIM], F32R), s.sb("w_lo", [P, kts, DIM], F32R)
        source = s.sb("source", [P, 2, width])
        x_hi, x_lo = s.sb("x_hi", [P, 4, kts, P], F32R), s.sb("x_lo", [P, 4, kts, P], F32R)
        turned = [s.ps(f"turned{b}", [P, kts, P]) for b in range(4)]
        out_ps = [s.ps(f"out{b}", [P, DIM]) for b in range(2)]
        restored = s.sem("restored")
        arrived, w_hi_done, w_lo_done = s.sem("arrived"), s.sem("w_hi_done"), s.sem("w_lo_done")
        source_done, turned_done = s.sem("source_done"), s.sem("turned_done")
        hi_done, lo_done, out_done, added = (s.sem(x) for x in ("hi_done", "lo_done", "out_done", "added"))
        block = s.block()

        @block.sync
        def _(sp):
            sp.dma_start(w32[:], w_out.rearrange("(k p) n -> p k n", p=P)).then_inc(arrived, 16)
            sp.dma_start(parked_space, parked).then_inc(restored, 16)

        @block.gpsimd
        def _(pool):
            with pool.Fori(0, BATCH) as sequence:
                with pool.Fori(0, QTILES // 2) as pair:
                    for b in range(2):
                        tile = 2 * pair + b
                        pool.wait_ge(turned_done, QTILES * sequence + tile + 1)
                        src = mixed[:, bass.ts(sequence, QUADS), bass.ds(tile, 1), :].rearrange("p q o d -> p (q o) d")
                        pool.tensor_copy(source[:, b, :].rearrange("p (q d) -> p q d", q=QUADS), src)\
                            .then_inc(source_done, 1)

        @block.scalar
        def _(act):
            act.wait_ge(arrived, 16)
            act.copy(w_hi[:], w32[:]).then_inc(w_hi_done, 1)
            with act.Fori(0, TILES // 4) as i:
                for b in range(4):
                    act.wait_ge(turned_done, 4 * i + b + 3)
                    act.wait_ge(out_done, 4 * i + b + 1)
                    act.copy(x_hi[:, b], turned[b][:]).then_inc(hi_done, 1)

        @block.vector
        def _(dve):
            dve.wait_ge(w_hi_done, 1)
            dve.tensor_tensor(w_lo[:], w32[:], w_hi[:].bitcast(F32), ALU.subtract).then_inc(w_lo_done, 1)
            dve.sem_inc(lo_done, 4)
            dve.sem_inc(added, 2)

            def low(i, b):
                dve.wait_ge(hi_done, i + 1)
                dve.tensor_tensor(x_lo[:, b], turned[b][:], x_hi[:, b].bitcast(F32),
                                  ALU.subtract).then_inc(lo_done, 1)

            def add(i, b):
                dve.wait_ge(out_done, i + 5)
                tile = stream[:, bass.ds(i, 1), :]
                dve.tensor_tensor(tile, tile, out_ps[b % 2][:], ALU.add).then_inc(added, 1)

            def body(i, last):
                for pair in range(2):
                    for b in (2 * pair, 2 * pair + 1):
                        if not (last and pair):
                            low(4 * i + b + 2, (b + 2) % 4)
                    for b in (2 * pair, 2 * pair + 1):
                        add(4 * i + b, b)

            for b in range(2):
                low(b, b)
            dve.wait_ge(restored, 16)
            with dve.Fori(0, TILES // 4 - 1) as i:
                body(i, False)
            body(TILES // 4 - 1, True)

        @block.tensor
        def _(pe):
            pe.sem_inc(turned_done, 2)
            pe.sem_inc(out_done, 4)
            pe.wait_ge(w_lo_done, 1)

            def turn(i, b):
                pe.wait_ge(source_done, i + 1)
                pe.wait_ge(lo_done, i + 1)
                for k in range(kts):
                    last = pe.transpose(turned[b][:, k, :], source[:, b % 2, k * P:(k + 1) * P], ident[:])
                last.then_inc(turned_done, 1)

            def product(i, b):
                pe.wait_ge(lo_done, i + 5)
                pe.wait_ge(added, i + 1)
                for k in range(kts):
                    last = matmul3(pe, out_ps[b % 2][:], x_hi[:, b, k, :], x_lo[:, b, k, :],
                                   w_hi[:, k, :], w_lo[:, k, :], k == 0, k == kts - 1)
                last.then_inc(out_done, 1)

            def body(i, last):
                for pair in range(2):
                    for b in (2 * pair, 2 * pair + 1):
                        if not (last and pair):
                            turn(4 * i + b + 2, (b + 2) % 4)
                    for b in (2 * pair, 2 * pair + 1):
                        product(4 * i + b, b)

            for b in range(2):
                turn(b, b)
            with pe.Fori(0, TILES // 4 - 1) as i:
                body(i, False)
            body(TILES // 4 - 1, True)



def latent_attention(nc, stream, ident, w_down, w_value, w_up, cos_sin, w_out):
    parked = nc.dram_tensor("parked", (P, PARKED, DIM), F32).ap()
    parked_space = stream[:, 0:PARKED, :]
    rotated = nc.dram_tensor("rotated", (BATCH * QUADS, 2, P, SEQ), F32).ap()
    with Scope(nc, "la") as keep:
        values = keep.sb("values", [P, BATCH * QUADS, QTILES, QUAD, 2 * HEAD_DIM1], F32R)
        with Scope(nc, "lal") as l:
            lat_hi, lat_lo = l.sb("lat_hi", [P, TOKENS], F32R), l.sb("lat_lo", [P, TOKENS], F32R)
            with Scope(nc, "laf") as f:
                feat_hi, feat_lo = f.sb("feat_hi", [P, KT, TOKENS], F32R), f.sb("feat_lo", [P, KT, TOKENS], F32R)
                normalise(nc, "n1a", stream, ident, feat_hi, feat_lo, feature_tiles_plain)
                latents(nc, feat_hi, feat_lo, w_down, w_value, lat_hi, lat_lo, values)
            rotated_heads(nc, lat_hi, lat_lo, w_up, cos_sin, rotated, parked_space, parked)
        mixed = keep.sb("mixed", [P, BATCH * QUADS, QTILES, QUAD * HEAD_DIM1])
        softmax_heads(nc, ident, values, rotated, parked_space, mixed)
        project_out(nc, "po1", stream, ident, mixed, w_out, DIM, parked_space, parked)


SPARSE_HIDDEN = 2048
SPARSE_GROUP = 4 * P
SPARSE_GROUPS = SPARSE_HIDDEN // SPARSE_GROUP


def load_sparse(sp, staged, arrived, weights, group, part):
    sp.dma_start(staged[part % 2][:], weights[group, part]).then_inc(arrived[part], 16)


def sparse_feed_forward(nc, stream, feat_hi, feat_lo, weights, staged, arrived, out):
    with Scope(nc, "sp") as s:
        WIDE = 4 * DIM
        w_hi = [s.sb(f"w_hi{q}", [P, WIDE], F32R) for q in range(3)]
        w_lo = [s.sb(f"w_lo{q}", [P, WIDE], F32R) for q in range(3)]
        silu = s.sb("silu", [P, 2, TB])
        hidden = s.sb("hidden", [P, 4, TB])
        size = s.sb("size", [P, 4, TB])
        beats = s.sb("beats", [P, 6, TB], BF16)
        wins = s.sb("wins", [P, 4, TB], BF16)
        h_hi = s.sb("h_hi", [P, 4, TB], F32R)
        h_lo = s.sb("h_lo", [P, 4, TB], F32R)
        gate_ps = [s.ps(f"gate{b}", [P, TB]) for b in range(2)]
        up_ps = [s.ps(f"up{b}", [P, TB]) for b in range(2)]
        down_ps = [s.ps(f"down{b}", [P, DIM]) for b in range(SUB)]

        w_hi_done, w_lo_done = s.sem("w_hi_done"), s.sem("w_lo_done")
        gate_done, up_done = s.sem("gate_done"), s.sem("up_done")
        silu_done, product_done, size_done = s.sem("silu_done"), s.sem("product_done"), s.sem("size_done")
        beats_done, half_done, wins_done, kept = (s.sem(x) for x in ("beats_done", "half_done", "wins_done", "kept"))
        h_hi_done, h_lo_done = s.sem("h_hi_done"), s.sem("h_lo_done")
        down_done, added, stored = s.sem("down_done"), s.sem("added"), s.sem("stored")
        block = s.block()

        @block.sync
        def _(sp):
            def load(group, part):
                load_sparse(sp, staged, arrived, weights, group, part)

            for g in range(SPARSE_GROUPS - 1):
                sp.wait_ge(w_lo_done, 3 * g + 1)
                load(g, 2)
                sp.wait_ge(w_lo_done, 3 * g + 2)
                load(g + 1, 1)
                sp.wait_ge(w_lo_done, 3 * g + 3)
                load(g + 1, 0)
            sp.wait_ge(w_lo_done, 3 * (SPARSE_GROUPS - 1) + 1)
            load(SPARSE_GROUPS - 1, 2)
            for tb in range(BLOCKS):
                sp.wait_ge(added, SUB * (BLOCKS * (SPARSE_GROUPS - 1) + tb + 2))
                rows = out[tb * TB:(tb + 1) * TB, :].rearrange("(i p) d -> p i d", p=P)
                sp.dma_start(rows, stream[:, tb * SUB:(tb + 1) * SUB, :]).then_inc(stored, 16)
            sp.wait_ge(stored, 16 * BLOCKS)

        @block.vector
        def _(dve):
            dve.sem_inc(added, SUB)
            dve.sem_inc(product_done, 2)
            dve.sem_inc(h_lo_done, 1)

            def low_weights(g, part):
                dve.wait_ge(w_hi_done, 3 * g + part + 1)
                dve.tensor_tensor(w_lo[part][:], staged[part % 2][:], w_hi[part][:].bitcast(F32),
                                  ALU.subtract).then_inc(w_lo_done, 1)

            def add(n, tb):
                for j in range(SUB):
                    dve.wait_ge(down_done, SUB * (n + 1) + j + 1)
                    tile = stream[:, tb * SUB + j, :]
                    dve.tensor_tensor(tile, tile, down_ps[j][:], ALU.add).then_inc(added, 1)

            def body(g, first, last):
                for tb in range(BLOCKS):
                    n = BLOCKS * g + tb
                    dve.wait_ge(h_lo_done, n + 1)
                    for r in range(4):
                        dve.wait_ge(up_done, 4 * n + r + 1)
                        dve.wait_ge(silu_done, 4 * n + r + 1)
                        dve.tensor_tensor(hidden[:, r, :], silu[:, r % 2, :], up_ps[r % 2][:],
                                          ALU.mult).then_inc(product_done, 1)
                    if tb == BLOCKS - 1 and not last:
                        low_weights(g + 1, 0)
                        low_weights(g + 1, 1)
                    dve.wait_ge(size_done, 4 * n + 4)
                    for a, at in ((0, 0), (1, 3), (2, 5)):
                        count = 3 - a
                        dve.tensor_tensor(beats[:, at:at + count, :],
                                          size[:, a:a + 1, :].broadcast_to([P, count, TB]),
                                          size[:, a + 1:4, :], ALU.is_ge).then_inc(beats_done, 1)
                    dve.wait_ge(beats_done, 3 * n + 3)
                    for r, (x, y, op) in enumerate(((0, 1, ALU.add), (3, 4, ALU.add), (5, 1, ALU.subtract),
                                                    (2, 4, ALU.add))):
                        dve.tensor_tensor(wins[:, r, :], beats[:, x, :], beats[:, y, :], op).then_inc(half_done, 1)
                    for r, (x, op) in enumerate(((2, ALU.add), (0, ALU.subtract), (3, ALU.subtract), (5, ALU.add))):
                        dve.wait_ge(half_done, 4 * n + r + 1)
                        dve.tensor_tensor(wins[:, r, :], wins[:, r, :], beats[:, x, :], op).then_inc(wins_done, 1)
                    for r, (limit, op) in enumerate(((2.0, ALU.is_ge), (1.0, ALU.is_ge), (0.0, ALU.is_ge),
                                                     (1.0, ALU.is_le))):
                        dve.wait_ge(wins_done, 4 * n + r + 1)
                        dve.scalar_tensor_tensor(out=hidden[:, r, :], in0=wins[:, r, :], scalar=limit,
                                                 in1=hidden[:, r, :], op0=op, op1=ALU.mult).then_inc(kept, 1)
                    if not (first and tb == 0):
                        add(n - 1, (tb - 1) % BLOCKS)
                    if tb == 0:
                        low_weights(g, 2)
                    dve.wait_ge(h_hi_done, n + 1)
                    dve.tensor_tensor(h_lo[:], hidden[:], h_hi[:].bitcast(F32), ALU.subtract).then_inc(h_lo_done, 1)

            low_weights(0, 0)
            low_weights(0, 1)
            body(0, True, False)
            with dve.Fori(1, SPARSE_GROUPS - 1) as g:
                body(g, False, False)
            body(SPARSE_GROUPS - 1, False, True)
            add(SPARSE_GROUPS * BLOCKS - 1, BLOCKS - 1)

        @block.scalar
        def _(act):
            act.preload_act_table(ACT.Silu)

            def high_weights(g, part):
                act.wait_ge(arrived[part], 16 * g + 16)
                act.copy(w_hi[part][:], staged[part % 2][:]).then_inc(w_hi_done, 1)

            def body(g, last):
                for tb in range(BLOCKS):
                    n = BLOCKS * g + tb

                    def magnitude(r):
                        act.wait_ge(product_done, 4 * n + r + 3)
                        act.activation(size[:, r, :], hidden[:, r, :], ACT.Abs).then_inc(size_done, 1)

                    for r in range(4):
                        act.wait_ge(gate_done, 4 * n + r + 1)
                        act.wait_ge(product_done, 4 * n + r + 1)
                        act.activation(silu[:, r % 2, :], gate_ps[r % 2][:], ACT.Silu).then_inc(silu_done, 1)
                        if r:
                            magnitude(r - 1)
                    magnitude(3)
                    if tb == BLOCKS - 1 and not last:
                        act.wait_ge(up_done, 4 * n + 4)
                        high_weights(g + 1, 0)
                        high_weights(g + 1, 1)
                    act.wait_ge(down_done, SUB * (n + 1))
                    if tb == 0:
                        high_weights(g, 2)
                    act.wait_ge(kept, 4 * n + 4)
                    act.copy(h_hi[:], hidden[:]).then_inc(h_hi_done, 1)

            high_weights(0, 0)
            high_weights(0, 1)
            with act.Fori(0, SPARSE_GROUPS - 1) as g:
                body(g, False)
            body(SPARSE_GROUPS - 1, True)

        @block.tensor
        def _(pe):
            pe.sem_inc(down_done, SUB)

            def gate_up(n, g, tb):
                pe.wait_ge(w_hi_done, 3 * g + 2)
                pe.wait_ge(w_lo_done, 3 * g + 2)
                cols = slice(tb * TB, (tb + 1) * TB)
                for r in range(4):
                    for part, ps in ((0, gate_ps[r % 2]), (1, up_ps[r % 2])):
                        if part == 0 and not (isinstance(n, int) and 4 * n + r < 2):
                            pe.wait_ge(silu_done, 4 * n + r - 1)
                        if part == 1:
                            pe.wait_ge(product_done, 4 * n + r + 1)
                        for kt in range(KT):
                            at = kt * DIM + r * P
                            last = matmul3(pe, ps[:], w_hi[part][:, at:at + P], w_lo[part][:, at:at + P],
                                           feat_hi[:, kt, cols], feat_lo[:, kt, cols], kt == 0, kt == KT - 1)
                        last.then_inc((gate_done, up_done)[part], 1)

            def down(n, g, tb):
                if tb == 0:
                    pe.wait_ge(w_lo_done, 3 * g + 3)
                pe.wait_ge(h_lo_done, n + 2)
                for j in range(SUB):
                    pe.wait_ge(added, SUB * n + j + 1)
                    rows = slice(j * P, (j + 1) * P)
                    for r in range(4):
                        at = slice(r * DIM, (r + 1) * DIM)
                        last = matmul3(pe, down_ps[j][:], h_hi[:, r, rows], h_lo[:, r, rows],
                                       w_hi[2][:, at], w_lo[2][:, at], r == 0, r == 3)
                    last.then_inc(down_done, 1)

            def body(g, last):
                for tb in range(BLOCKS):
                    n = BLOCKS * g + tb
                    nxt = tb + 1
                    if not (last and nxt == BLOCKS):
                        gate_up(n + 1, g + nxt // BLOCKS, nxt % BLOCKS)
                    down(n, g, tb)

            gate_up(0, 0, 0)
            with pe.Fori(0, SPARSE_GROUPS - 1) as g:
                body(g, False)
            body(SPARSE_GROUPS - 1, True)


def four_sublayers(nc, hidden, ident_in, masks_in, w_qkv, conv_w, w_gate, head_rows, w_out0, codes, scales,
                   w_down1, w_value1, w_up1, cos_sin, w_out1, w_sparse, out):
    with Scope(nc, "k") as s:
        stream = s.sb("stream", [P, TILES, DIM])
        ident = s.sb("ident", [P, P])
        arrived = [s.sem(f"arrived{q}") for q in range(BLOCKS)]
        constants_in = s.sem("constants_in")
        with Scope(nc, "l0") as l0:
            mask = l0.sb("mask", [P, N_MASKS, P])
            with nc.Block() as block:
                @block.sync
                def _(sp):
                    for q in range(BLOCKS):
                        rows = hidden[q * TB:(q + 1) * TB, :].rearrange("(i p) d -> p i d", p=P)
                        sp.dma_start(stream[:, q * SUB:(q + 1) * SUB, :], rows).then_inc(arrived[q], 16)
                        if q == 0:
                            sp.dma_start(ident[:], ident_in).then_inc(constants_in, 16)
                    sp.dma_start(mask[:], masks_in).then_inc(constants_in, 16)
            delta_attention(nc, stream, ident, mask, (arrived, constants_in, 32), hidden, w_qkv, conv_w, w_gate, head_rows, w_out0)
        with Scope(nc, "f0") as f:
            feat_hi, feat_lo = f.sb("feat_hi", [P, KT, TOKENS], F32R), f.sb("feat_lo", [P, KT, TOKENS], F32R)
            staging = f.sb("words", [P, FP4_COLS], I32), f.sb("scale", [P, FP4_COLS]), f.sem("loaded")
            normalise(nc, "n0f", stream, ident, feat_hi, feat_lo, feature_tiles_nibbles,
                      prefetch=lambda sp: load_codes(sp, staging, codes, scales, 0))
            nvfp4_feed_forward(nc, stream, feat_hi, feat_lo, codes, scales, staging)
        latent_attention(nc, stream, ident, w_down1, w_value1, w_up1, cos_sin, w_out1)
        with Scope(nc, "f1") as f:
            feat_hi, feat_lo = f.sb("feat_hi", [P, KT, TOKENS], F32R), f.sb("feat_lo", [P, KT, TOKENS], F32R)
            staged = [f.sb(f"staged{b}", [P, 4 * DIM]) for b in range(2)]
            parts_in = [f.sem(f"parts_in{q}") for q in range(3)]

            def first_parts(sp):
                for part in range(2):
                    load_sparse(sp, staged, parts_in, w_sparse, 0, part)

            normalise(nc, "n1f", stream, ident, feat_hi, feat_lo, feature_tiles_plain, prefetch=first_parts)
            sparse_feed_forward(nc, stream, feat_hi, feat_lo, w_sparse, staged, parts_in, out)


def rotary_tables():
    inverse = (1.0 / 10000.0 ** (np.arange(0, HALF, 2, dtype=np.float32) / HALF)).astype(np.float32)
    angle = (np.arange(SEQ, dtype=np.float32)[:, None] * inverse[None]).astype(np.float32)
    angle = np.concatenate([angle, angle], -1).T
    sign = np.where(np.arange(HALF) < HALF // 2, -1, 1)[:, None]
    table = np.stack([np.tile(np.cos(angle), (P // HALF, 1)), np.tile(np.sin(angle) * sign, (P // HALF, 1))], 1)
    table = table.astype(np.float32)
    table[:P // 2] *= HALF ** -0.5
    return np.ascontiguousarray(table)


def delta_layout(x):
    names = "qkv"
    w = np.stack([x[f"L0_attn_W{n}"] for n in names]).reshape(3, CT, P, KT, P)
    conv = np.stack([x[f"L0_attn_conv_{n}"] for n in names]).reshape(3, CT, P, CONV)
    gate = np.concatenate([x["L0_attn_Wg"].T, x["L0_attn_Wb"].T, x["L0_attn_Wa"].T], 1)
    return (w.transpose(1, 0, 4, 3, 2).reshape(CT, 3, P, KT * P), conv.transpose(2, 1, 0, 3).reshape(P, CT, 3 * CONV),
            gate.reshape(KT, P, GATE_COLS),
            np.concatenate([np.tile(x["L0_attn_o_norm_w"], HEADS0), x["L0_attn_dt_bias"], x["L0_attn_A_log"]]),
            x["L0_attn_Wo"].T)


def nvfp4_layout(x):
    def rows(a):
        inner = a.shape[1] // 2
        a = a.reshape(FP4_GROUPS, P, 2, 2, inner)
        return a.transpose(0, 4, 3, 2, 1).reshape(FP4_GROUPS, inner, 2 * FP4_GROUP)

    def down(a):
        return a.T.reshape(FP4_GROUPS, a.shape[1] // FP4_GROUPS, DIM)

    return tuple(np.concatenate([rows(x[f"L0_ffn_gate_{n}"]), rows(x[f"L0_ffn_up_{n}"]), down(x[f"L0_ffn_down_{n}"])], 2)
                 for n in ("W_packed", "scales"))


def latent_up_layout(x):
    swapped = [(d + HALF // 2) % HALF for d in range(HALF)]
    up = np.zeros((P, QUADS, 2, P), np.float32)
    for side, name in enumerate(("L1_attn_wq_u", "L1_attn_wk_u")):
        w = x[name].reshape(LATENT, QUADS, QUAD, HALF)
        at = slice(side * LATENT, (side + 1) * LATENT)
        for which, cols in enumerate((w, w[..., swapped])):
            up[at, :, which, at] = cols.reshape(LATENT, QUADS, QUAD * HALF)
    return up.reshape(P, QUADS, 2 * P).transpose(1, 0, 2)


def sparse_layout(x):
    def into(w):
        w = w.reshape(KT, P, SPARSE_GROUPS, P, 4)
        return w.transpose(2, 1, 0, 4, 3).reshape(SPARSE_GROUPS, 1, P, 4 * DIM)
    down = x["L1_ffn_w_down"].reshape(SPARSE_GROUPS, 1, P, 4 * DIM)
    return np.concatenate([into(x["L1_ffn_w_gate"]), into(x["L1_ffn_w_up"]), down], 1)


def kernel(**inputs):
    import concourse.bacc as bacc
    from concourse.bass_utils import run_bass_kernel_spmd

    x = {name: np.asarray(a) for name, a in inputs.items()}
    w_qkv, conv_w, w_gate, head_rows, w_out0 = delta_layout(x)
    codes, scales = nvfp4_layout(x)
    arrays = {
        "hidden": x["L0_attn_hidden_states"].reshape(TOKENS, DIM),
        "ident_in": np.eye(P, dtype=np.float32), "masks_in": masks(),
        "w_qkv": w_qkv, "conv_w": conv_w, "w_gate": w_gate, "head_rows": head_rows, "w_out0": w_out0,
        "codes": codes, "scales": scales,
        "w_down1": np.concatenate([x["L1_attn_wq_d"], x["L1_attn_wkv_d"]], 1), "w_value1": x["L1_attn_wv_u"],
        "w_up1": latent_up_layout(x), "cos_sin": rotary_tables(), "w_out1": x["L1_attn_wo"],
        "w_sparse": sparse_layout(x),
    }
    arrays = {name: np.ascontiguousarray(a) for name, a in arrays.items()}
    nc = bacc.Bacc("TRN2", target_bir_lowering=False, num_devices=1)
    args = {name: nc.dram_tensor(name, a.shape, mybir.dt.from_np(a.dtype), kind="ExternalInput").ap()
            for name, a in arrays.items()}
    out = nc.dram_tensor("out", (TOKENS, DIM), F32, kind="ExternalOutput").ap()
    four_sublayers(nc, out=out, **args)
    result = run_bass_kernel_spmd(nc, [arrays], core_ids=[0])
    return result.results[0]["out"].reshape(BATCH, SEQ, DIM)
```
